# Optimizing a Trainium2 kernel written in Bass

```python
import numpy as np
import jax
import jax.numpy as jnp

def _softmax(x, axis=-1):
    return jax.nn.softmax(x, axis=axis)

def _gelu(x):
    return jax.nn.gelu(x, approximate=True)

def _silu(x):
    return jax.nn.silu(x)

def _sigmoid(x):
    return jax.nn.sigmoid(x)

def _layernorm(x, axis=-1, eps=1e-05):
    m = jnp.mean(x, axis=axis, keepdims=True)
    v = jnp.var(x, axis=axis, keepdims=True)
    return (x - m) / jnp.sqrt(v + eps)

def _scatter_add(tgt, idx, src, axis=0):
    return tgt.at[idx].add(src)

def _segment_sum(src, seg, n):
    return jax.ops.segment_sum(src, seg, n)
kernel_name = 'mk_adaln_d1_jaxref_r4_3e44fa'

def setup_inputs(seed: int=0):
    np.random.seed(seed)
    _w = jnp.asarray

    def _L0_attn_setup():
        import jax, jax.numpy as jnp
        import numpy as np
        DIM = 256
        HEADS = 16
        HEAD_DIM = DIM // HEADS
        ROPE_BASE = 500000.0
        SCALE = HEAD_DIM ** (-0.5)

        def _rope_cos_sin(T, dtype=jnp.float32):
            inv_freq = 1.0 / ROPE_BASE ** (jnp.arange(0, HEAD_DIM, 2, dtype=jnp.float32) / HEAD_DIM)
            t = jnp.arange(T, dtype=jnp.float32)
            freqs = t[:, None] * inv_freq[None, :]
            emb = jnp.concatenate([freqs, freqs], axis=-1)
            return (jnp.cos(emb).astype(dtype), jnp.sin(emb).astype(dtype))

        def _rotate_half(x):
            x1, x2 = jnp.split(x, 2, axis=-1)
            return jnp.concatenate([-x2, x1], axis=-1)

        def _apply_rope(x, cos, sin):
            return x * cos + _rotate_half(x) * sin
        key = jax.random.key(seed)
        k1, k2, k3 = jax.random.split(key, 3)
        B, T = (4, 1024)
        x = jax.random.normal(k1, (B, T, DIM), dtype=jnp.float32)
        W_qkv = jax.random.normal(k2, (DIM, 3 * DIM), dtype=jnp.float32) * DIM ** (-0.5)
        W_out = jax.random.normal(k3, (DIM, DIM), dtype=jnp.float32) * DIM ** (-0.5)
        return {'x': x, 'W_qkv': W_qkv, 'W_out': W_out}
    _L0_attn_in = _L0_attn_setup()

    def _L0_ffn_setup():
        import jax, jax.numpy as jnp
        import numpy as np
        E = 8
        K = 2
        CF = 1.25
        key = jax.random.key(seed)
        kx, kr, kg, ku, kd = jax.random.split(key, 5)
        D, F = (256, 1024)
        x = jax.random.normal(kx, (4, 512, D), dtype=jnp.float32)
        router_w = 0.02 * jax.random.normal(kr, (E, D), dtype=jnp.float32)
        wg = jax.random.normal(kg, (E, D, F), dtype=jnp.float32) / np.sqrt(D)
        wu = jax.random.normal(ku, (E, D, F), dtype=jnp.float32) / np.sqrt(D)
        wd = jax.random.normal(kd, (E, F, D), dtype=jnp.float32) / np.sqrt(F)
        return {'x': x, 'router_w': router_w, 'wg': wg, 'wu': wu, 'wd': wd}
    _L0_ffn_in = _L0_ffn_setup()
    _L0_c = _w((lambda *s: np.random.randn(*s).astype(np.float32) * 0.05)(2, 256))
    _L0_wmod = _w((lambda *s: np.random.randn(*s).astype(np.float32) * 0.05)(256, 6 * 256) * 256 ** (-0.5))
    _d = {'L0_attn_x': _L0_attn_in['x'], 'L0_attn_W_qkv': _L0_attn_in['W_qkv'], 'L0_attn_W_out': _L0_attn_in['W_out'], 'L0_ffn_router_w': _L0_ffn_in['router_w'], 'L0_ffn_wg': _L0_ffn_in['wg'], 'L0_ffn_wu': _L0_ffn_in['wu'], 'L0_ffn_wd': _L0_ffn_in['wd'], 'L0_c': _L0_c, 'L0_wmod': _L0_wmod}
    _x0 = _d['L0_attn_x']
    _d['L0_attn_x'] = jax.random.normal(jax.random.fold_in(jax.random.key(seed), 1), (2, 2048, 256), dtype=_x0.dtype)
    del _x0
    return _d

def reference(L0_attn_x, L0_attn_W_qkv, L0_attn_W_out, L0_ffn_router_w, L0_ffn_wg, L0_ffn_wu, L0_ffn_wd, L0_c, L0_wmod):

    def _L0_attn_ref(x, W_qkv, W_out):
        import jax, jax.numpy as jnp
        import numpy as np
        DIM = 256
        HEADS = 16
        HEAD_DIM = DIM // HEADS
        ROPE_BASE = 500000.0
        SCALE = HEAD_DIM ** (-0.5)

        def _rope_cos_sin(T, dtype=jnp.float32):
            inv_freq = 1.0 / ROPE_BASE ** (jnp.arange(0, HEAD_DIM, 2, dtype=jnp.float32) / HEAD_DIM)
            t = jnp.arange(T, dtype=jnp.float32)
            freqs = t[:, None] * inv_freq[None, :]
            emb = jnp.concatenate([freqs, freqs], axis=-1)
            return (jnp.cos(emb).astype(dtype), jnp.sin(emb).astype(dtype))

        def _rotate_half(x):
            x1, x2 = jnp.split(x, 2, axis=-1)
            return jnp.concatenate([-x2, x1], axis=-1)

        def _apply_rope(x, cos, sin):
            return x * cos + _rotate_half(x) * sin
        B, T, D = x.shape
        H, hd = (HEADS, HEAD_DIM)
        qkv = (x @ W_qkv).reshape(B, T, 3, H, hd).transpose(2, 0, 3, 1, 4)
        q, k, v = (qkv[0], qkv[1], qkv[2])
        cos, sin = _rope_cos_sin(T, q.dtype)
        q = _apply_rope(q, cos, sin)
        k = _apply_rope(k, cos, sin)
        q_feat = jax.nn.elu(q * SCALE) + 1.0
        k_feat = jax.nn.elu(k) + 1.0
        kv = jnp.einsum('bhtd,bhtv->bhdv', k_feat, v)
        k_sum = k_feat.sum(axis=2)
        denom = jnp.maximum(jnp.einsum('bhtd,bhd->bht', q_feat, k_sum), 1e-06)
        out = jnp.einsum('bhtd,bhdv->bhtv', q_feat, kv) / denom[..., None]
        out = out.transpose(0, 2, 1, 3).reshape(B, T, D)
        return out @ W_out

    def _L0_ffn_ref(x, router_w, wg, wu, wd):
        import jax, jax.numpy as jnp
        import numpy as np
        E = 8
        K = 2
        CF = 1.25
        B, L, D = x.shape
        xf = x.reshape(-1, D)
        N = xf.shape[0]
        capacity = max(1, int(CF * N / E))
        logits = xf @ router_w.T
        probs = jax.nn.softmax(logits, axis=-1)
        topw, topi = jax.lax.top_k(probs, K)
        topw = topw / (topw.sum(-1, keepdims=True) + 1e-06)
        fe = topi.reshape(-1)
        fw = topw.reshape(-1)
        ft = jnp.repeat(jnp.arange(N), K)
        order = jnp.lexsort((-fw, fe))
        se, sw, st = (fe[order], fw[order], ft[order])
        counts = jax.ops.segment_sum(jnp.ones_like(se), se, num_segments=E)
        starts = jnp.cumsum(counts) - counts
        rank = jnp.arange(N * K) - starts[se]
        keep = rank < capacity
        pos = jnp.where(keep, rank, capacity)
        disp = jnp.zeros((E, capacity + 1, D), x.dtype).at[se, pos].set(xf[st])
        disp = disp[:, :capacity]
        g = jnp.einsum('ecd,edf->ecf', disp, wg)
        u = jnp.einsum('ecd,edf->ecf', disp, wu)
        eo = jnp.einsum('ecf,efd->ecd', jax.nn.silu(g) * u, wd)
        gathered = eo[se, jnp.minimum(pos, capacity - 1)]
        contrib = gathered * (sw * keep.astype(x.dtype))[:, None]
        out = jnp.zeros_like(xf).at[st].add(contrib)
        return out.reshape(B, L, D)
    x = L0_attn_x
    mod = (_silu(L0_c) @ L0_wmod).reshape(L0_c.shape[0], 6, 1, -1)
    sa, ca, ga, sb, cb, gb = (mod[:, 0], mod[:, 1], mod[:, 2], mod[:, 3], mod[:, 4], mod[:, 5])
    ga = (2 * (ga >= 0) - 1) * jnp.maximum(jnp.abs(ga), 0.25)
    gb = (2 * (gb >= 0) - 1) * jnp.maximum(jnp.abs(gb), 0.25)
    h = _layernorm(x, axis=-1) * (1 + ca) + sa
    x = x + ga * _L0_attn_ref(h, L0_attn_W_qkv, L0_attn_W_out)
    h = _layernorm(x, axis=-1) * (1 + cb) + sb
    x = x + gb * _L0_ffn_ref(h, L0_ffn_router_w, L0_ffn_wg, L0_ffn_wu, L0_ffn_wd)
    return x

_drawn_inputs = setup_inputs


def setup_inputs(seed=0):
    import zlib

    import numpy as np

    out = dict(_drawn_inputs(seed))
    spreads = {}
    factors = {'L0_attn_W_qkv': 7.195, 'L0_attn_W_out': 6.558}
    for name, (base, spread) in spreads.items():
        noise = np.random.default_rng([zlib.crc32(name.encode()), seed]).standard_normal(out[name].shape)
        drawn = base * np.exp(spread * noise) if base else spread * noise
        out[name] = jnp.asarray(drawn.astype(out[name].dtype))
    for name, factor in factors.items():
        out[name] = (out[name] * factor).astype(out[name].dtype)
    return out
```

```python
from contextlib import ExitStack

import concourse.bass as bass
from concourse import mybir

P = 128
F32, F32R = mybir.dt.float32, mybir.dt.float32r
BF16, I32 = mybir.dt.bfloat16, mybir.dt.int32
ALU = mybir.AluOpType
ACT = mybir.ActivationFunctionType
AX = mybir.AxisListType.X

B, T, D = 2, 2048, 256
H, HD = 16, 16
HALF = HD // 2
N = B * T
NT = N // P
TB = NT // B
KC = D // P
HC = H // KC
E, TOPK, F = 8, 2, 1024
CAP = int(1.25 * N / E)
CT = CAP // P
FC = F // P
HCAP = CAP // 2
WU = 5 * P + P
LAG = TB + 1
LN_EPS, DEN_EPS, TOPW_EPS, GATE_MIN = 1e-5, 1e-6, 1e-6, 0.25
TOP_BIT = 29
NV = 5
XF = 4
FAR = 1 << 20


class Step:

    def __init__(self, k, j, rep):
        self.k, self.j, self.rep = k, j, rep

    def t(self, off):
        return self.k * 2 + (self.j + off)

    def par(self, off):
        return (self.j + off) % 2

    def half(self, off):
        return self.k + (self.j + off) // 2


def wait(eng, sem, value):
    if isinstance(value, int) and value <= 0:
        return
    assert isinstance(value, int) or bass.sinput_min_value(value) > 0
    eng.wait_ge(sem, value)


def wait_apart(eng, sem, value, apart):
    wait(eng, sem, value)
    eng.sem_inc(apart, 1)


def steps(eng, emit, segments):
    for lo, hi, looped in segments:
        if looped:
            with eng.Fori(lo // 2, hi // 2) as k:
                emit(Step(k, 0, lo))
                emit(Step(k, 1, lo + 1))
        else:
            for s in range(lo, hi):
                emit(Step(s // 2, s % 2, s))


ATT = [(-2, 4, False), (4, TB - 2, True), (TB - 2, TB + 6, False), (TB + 6, NT - 4, True),
       (NT - 4, NT + 4, False), (NT + 4, NT + TB, True), (NT + TB, NT + TB + 4, False)]


def stages(s):
    r = s.rep
    u = r - LAG
    on = lambda t: 0 <= t < NT
    return dict(stats=on(r + 2), norm=on(r + 1), qkv=on(r), feat=on(r - 1), qload=on(u + 1), xrload=on(u),
                xload=on(r + 3), att=on(u), proj=on(u - 1), second=on(u - 2), logit=on(u - 3))


def build_program(nc, x, w_qkv, w_out, router, wg, wu, wd, c, wmod, rope, consts, out):
    xt = x.rearrange("b (n p) d -> (b n) p d", p=P)
    out_rows = out.rearrange("b t d -> (b t) d")
    out_t = out_rows.rearrange("(n p) d -> n p d", p=P)
    h2_rows = nc.dram_tensor("h2_rows", (N, D), F32, kind="Internal").ap()
    h2_t = h2_rows.rearrange("(n p) d -> n p d", p=P)
    q_store = nc.dram_tensor("q_store", (NT, P, D), F32, kind="Internal").ap()

    with ExitStack() as ctx:
        def sb(name, shape, dt=F32):
            return ctx.enter_context(nc.sbuf_tensor(name, shape, dt))

        def sem(name):
            return ctx.enter_context(nc.semaphore(name))

        bank = [ctx.enter_context(nc.psum_tensor(f"bank{i}", [P, 512], F32)) for i in range(8)]

        const_sb = sb("const_sb", [P, 3 * P + HC + E])
        ident = const_sb[:, 0:P]
        blk = const_sb[:, P:2 * P + HC]
        sel_e = const_sb[:, 2 * P + HC:2 * P + HC + E]
        same_f = const_sb[:, 2 * P + HC + E:]
        same_e = sb("same_e", [P, P], BF16)
        before = sb("before", [P, P], BF16)
        ones_b = sb("ones_b", [P, P], BF16)
        ones_f = sb("ones_f", [P, P])
        zeros = sb("zeros", [1, 512], BF16)
        rope_sb = sb("rope_sb", [P, TB, 3 * HALF])
        router_sb = sb("router_sb", [E, D])
        routerT = sb("routerT", [P, KC, E])
        c_sb = sb("c_sb", [B, D])
        c_act = sb("c_act", [B, D])
        cT = sb("cT", [P, KC, B])
        c_bc = sb("c_bc", [P, KC, B, P])
        mod_col = sb("mod_col", [P, 2, KC, B])
        row_sb = [sb(f"row_sb{b}", [P, 2, D]) for b in range(B)]
        gate_mag = sb("gate_mag", [P, 2, D])
        gate_sgn = sb("gate_sgn", [P, 2, D])
        gates = [sb(f"gates{b}", [P, 2, D]) for b in range(B)]
        pad = sb("pad", [1, HALF])
        half_neg = sb("half_neg", [P, 1])

        logits = sb("logits", [P, NT, E])

        big = [sb(f"big{i}", [P, NT, E]) for i in range(8)]
        small = [sb(f"small{i}", [P, NT]) for i in range(8)]
        rev = sb("rev", [P, E])
        wgt = sb("wgt", [P, NT, E])
        val = sb("val", [P, NT, E])
        valT = sb("valT", [P, 2 * P])
        thr, cand, bit = sb("thr", [P, 1], I32), sb("cand", [P, 1], I32), sb("bit", [P, 1], I32)
        flag = sb("flag", [P, 1], I32)
        cnt = sb("cnt", [P, 1], BF16)
        hit = sb("hit", [P, 2 * P], BF16)
        thr_sel, thr_b = sb("thr_sel", [P, E]), sb("thr_b", [P, E])
        mask2 = sb("mask2", [P, 2, E, NT], BF16)
        reset = sb("reset", [P, 2 * E, NT])
        run = sb("run", [P, 2, E, NT])
        pre = sb("pre", [P, 2, E, NT])
        need = sb("need", [P, E])
        slot, keep = sb("slot", [P, E, NT]), sb("keep", [P, E, NT])
        tmp_s = sb("tmp_s", [P, E, NT])
        vals = sb("vals", [P, E, NT, NV], BF16)
        w_hi, w_mid = sb("w_hi", [P, NT, E], BF16), sb("w_mid", [P, NT, E], BF16)
        w_r1, w_r2 = sb("w_r1", [P, NT, E]), sb("w_r2", [P, NT, E])

        iota_b = sb("iota_b", [P, P, NT], BF16)
        tile_ge = sb("tile_ge", [P, NT, CT + 1])
        tile_thr = sb("tile_thr", [P, CT + 1])
        in_tile = sb("in_tile", [P, NT, CT])
        tile_no = sb("tile_no", [P, NT])
        row_in = sb("row_in", [P, NT], BF16)
        onehot = sb("onehot", [P, P, NT], BF16)
        facts = sb("facts", [P, NT, NV, CT], BF16)
        got = sb("got", [P, NV, CT])
        tok = sb("tok", [P, CT])
        far = sb("far", [P, CT])
        g_idx = [sb(f"g_idx{i}", [P, CT], I32) for i in range(2)]
        s_idx = [sb(f"s_idx{i}", [P, CT], I32) for i in range(2)]
        w_slot = sb("w_slot", [P, 3, CT])
        w_b = [sb(f"w_b{i}", [P, B, CT]) for i in range(2)]

        w_raw = sb("w_raw", [P, FC, WU])
        w_h, w_l = sb("w_h", [P, FC, WU], F32R), sb("w_l", [P, FC, WU], F32R)
        own = ExitStack()

        def sa(name, shape, dt=F32):
            return own.enter_context(nc.sbuf_tensor(name, shape, dt))

        wmod_sb = sa("wmod_sb", [P, KC, 6 * D])
        wqkv_sb = sa("wqkv_sb", [P, KC, 3 * D])
        wout_sb = sa("wout_sb", [P, KC, D])
        wout_g = [sa(f"wout_g{b}", [P, KC, D]) for b in range(B)]
        x_in = [sa(f"x_in{i}", [P, D]) for i in range(2)]
        st1, mv1 = sa("st1", [P, 6]), sa("mv1", [P, 2])
        nm1, ve1, rs1 = sa("nm1", [P, 1]), sa("ve1", [P, 1]), sa("rs1", [P, 1])
        hn = sa("hn", [P, D])
        hT = sa("hT", [P, KC, P])
        rot_a, rot_b, rot = sa("rot_a", [P, 2 * D]), sa("rot_b", [P, 2 * D]), sa("rot", [P, 2 * D])
        ex, rl, feat = sa("ex", [P, 2 * D]), sa("rl", [P, 2 * D]), sa("feat", [P, 2 * D])
        vx = [sa(f"vx{i}", [P, KC, P + 1]) for i in range(2)]
        qT = [sa(f"qT{i}", [P, D]) for i in range(2)]
        kvb = [sa(f"kvb{b}", [P, KC, P + HC]) for b in range(B)]

        q_in = [sa(f"q_in{i}", [P, D]) for i in range(2)]
        den_m, den_r = sa("den_m", [P, KC, HC]), sa("den_r", [P, KC, HC])
        att, attT = sa("att", [P, D]), sa("attT", [P, D])
        x_re = [sa(f"x_re{i}", [P, D]) for i in range(2)]
        x2 = [sa(f"x2_{i}", [P, D]) for i in range(2)]
        st2, mv2 = sa("st2", [P, 6]), sa("mv2", [P, 2])
        nm2, ve2, rs2 = sa("nm2", [P, 1]), sa("ve2", [P, 1]), sa("rs2", [P, 1])
        xn2, xm2 = sa("xn2", [P, D]), sa("xm2", [P, D])
        h2 = [sa(f"h2_{i}", [P, D]) for i in range(2)]
        h2T = sa("h2T", [P, D])
        own.close()

        xg = sb("xg", [P, CT, D])
        xT_h = [sb(f"xT_h{i}", [P, KC, CAP], F32R) for i in range(2)]
        xT_l = [sb(f"xT_l{i}", [P, KC, CAP], F32R) for i in range(2)]
        act_g = [sb(f"act_g{i}", [P, HCAP]) for i in range(2)]
        hid = [sb(f"hid{i}", [P, HCAP]) for i in range(2)]
        hid_h = [sb(f"hid_h{i}", [P, CAP], F32R) for i in range(2)]
        hid_l = [sb(f"hid_l{i}", [P, CAP], F32R) for i in range(2)]
        gw0 = sb("gw0", [P, D])
        gw = sb("gw", [P, CT, D])
        xo, yo = sb("xo", [P, CT, D]), sb("yo", [P, CT, D])

        qk_ps = bank[0][:, :]
        v_ps = bank[1][:, 0:D]
        h2T_ps = bank[1][:, D:2 * D]
        o_ps = bank[2][:, 0:KC * (P + HC)].rearrange("p (c n) -> p c n", c=KC)
        lg_ps = bank[2][:, 480:480 + E]
        kv_ps = bank[3][:, 0:KC * (P + 1)].rearrange("p (c n) -> p c n", c=KC)
        hT_ps = [bank[4][:, 0:P], bank[6][:, 0:P]]
        qT_ps = bank[5][:, 0:D]
        oT_ps = bank[7][:, 0:D]
        y_ps = bank[7][:, D:2 * D]
        row_ps = [(bank[2], bank[7]), (bank[5], bank[3])]

        ld_c, ld_mod, ld_const, ld_w = sem("ld_c"), sem("ld_mod"), sem("ld_const"), sem("ld_w")
        ld_x, ld_q, ld_xr = ([sem(f"{n}{i}") for i in range(2)] for n in ("ld_x", "ld_q", "ld_xr"))
        st_q, st_x2, st_h2 = ([sem(f"{n}{i}") for i in range(2)] for n in ("st_q", "st_x2", "st_h2"))
        pe_pre, act_pre, dve_pre, pool_pre = sem("pe_pre"), sem("act_pre"), sem("dve_pre"), sem("pool_pre")
        link_s, plink_s = sem("link_s"), sem("plink_s")
        bn1, ag1, stat1, pow1, norm1 = sem("bn1"), sem("ag1"), sem("stat1"), sem("pow1"), sem("norm1")
        tr_h, hT_a, hT_d, qkv_done = sem("tr_h"), sem("hT_a"), sem("hT_d"), sem("qkv_done")
        rope_m, rope_d, v_done, exp_d, feat_d = (sem(n) for n in ("rope_m", "rope_d", "v_done", "exp_d", "feat_d"))
        tr_q, qT_d, kv_d, kvb_d, kvb_link = (sem(n) for n in ("tr_q", "qT_d", "kv_d", "kvb_d", "kvb_link"))
        o_d, dmax, drec, att_d = sem("o_d"), sem("dmax"), sem("drec"), sem("att_d")
        tr_o, oT_d, y_d, x2_d = sem("tr_o"), sem("oT_d"), sem("y_d"), sem("x2_d")
        bn2, ag2, stat2, pow2, pn2, pm2, h2_d = (sem(n) for n in ("bn2", "ag2", "stat2", "pow2", "pn2", "pm2", "h2_d"))
        tr_h2, h2T_d, lg_d, lgc = sem("tr_h2"), sem("h2T_d"), sem("lg_d"), sem("lgc")
        r_dve, r_act, r_pe, r_pool = sem("r_dve"), sem("r_act"), sem("r_pe"), sem("r_pool")
        cnt_d, tot_d, flag_d, thr_d, cand_d, bit_d = (sem(n) for n in ("cnt_d", "tot_d", "flag_d", "thr_d", "cand_d", "bit_d"))
        slots_d = sem("slots_d")
        ge_d, in_d, tn_d, ri_d = sem("ge_d"), sem("in_d"), sem("tn_d"), sem("ri_d")
        facts_d, look_d, got_d, fin_l, idx_d = (sem(n) for n in ("facts_d", "look_d", "got_d", "fin_l", "idx_d"))
        raw_a, raw_b, sp_h, sp_l = sem("raw_a"), sem("raw_b"), sem("sp_h"), sem("sp_l")
        ga_d, trx_d, xh_d, xl_d = sem("ga_d"), sem("trx_d"), sem("xh_d"), sem("xl_d")
        gu_d, silu_d, hid_d, hh_d, hl_d, dn_d = (sem(n) for n in ("gu_d", "silu_d", "hid_d", "hh_d", "hl_d", "dn_d"))
        y_tile = sem("y_tile")
        gw0_d, gw_d, xo_d, ym_d, yo_d, sc_d = (sem(n) for n in ("gw0_d", "gw_d", "xo_d", "ym_d", "yo_d", "sc_d"))

        apart = sem("apart")

        block = ctx.enter_context(nc.Block())

        @block.sync
        def _(sp):
            sp.dma_start(c_sb[:, :], c).then_inc(ld_c, 16)
            sp.dma_start(const_sb[:, :], consts).then_inc(ld_c, 16)
            sp.dma_start(x_in[0][:, :], xt[0]).then_inc(ld_x[0], 16)
            sp.dma_start(x_in[1][:, :], xt[1]).then_inc(ld_x[1], 16)
            sp.dma_start(wmod_sb[:, :, :], wmod.rearrange("(c p) n -> p c n", p=P)).then_inc(ld_mod, 16)
            sp.dma_start(rope_sb[:, :, :], rope.rearrange("(n p) d -> p n d", p=P)).then_inc(ld_const, 16)
            sp.dma_start(wqkv_sb[:, :, :], w_qkv.rearrange("(c p) n -> p c n", p=P)).then_inc(ld_w, 16)
            sp.dma_start(wout_sb[:, :, :], w_out.rearrange("(c p) n -> p c n", p=P)).then_inc(ld_w, 16)
            sp.dma_start(router_sb[:, :], router).then_inc(ld_w, 16)

            def load_weights(e, lo, done):
                hi = lo + FC // 2
                for k in range(KC):
                    for w, at in ((wg, 0), (wu, 2 * P)):
                        src = w[e, k * P:(k + 1) * P, :].rearrange("p (f n) -> p f n", n=P)
                        sp.dma_start(w_raw[:, lo:hi, at + k * P:at + (k + 1) * P], src[:, lo:hi, :]).then_inc(done, 16)
                sp.dma_start(w_raw[:, lo:hi, 4 * P:], wd[e].rearrange("(f p) n -> p f n", p=P)[:, lo:hi, :])\
                    .then_inc(done, 16)

            def step(s):
                on = stages(s)
                if on["qload"]:
                    o = 1 - LAG
                    wait(sp, o_d, s.t(o - 1))
                    wait(sp, st_q[s.par(o)], (s.half(o) + 1) * 16)
                    sp.dma_start(q_in[s.par(o)][:, :], q_store[s.t(o)]).then_inc(ld_q[s.par(o)], 16)
                if on["xrload"]:
                    o = -LAG
                    wait(sp, x2_d, s.t(o - 1))
                    sp.dma_start(x_re[s.par(o)][:, :], xt[s.t(o)]).then_inc(ld_xr[s.par(o)], 16)
                if on["second"]:
                    o = -LAG - 2
                    wait(sp, h2_d, s.t(o + 1))
                    sp.dma_start(h2_t[s.t(o)], h2[s.par(o)][:, :]).then_inc(st_h2[s.par(o)], 16)
                if on["xload"] and s.rep >= -1:
                    wait(sp, norm1, s.t(2))
                    sp.dma_start(x_in[s.par(3)][:, :], xt[s.t(3)]).then_inc(ld_x[s.par(3)], 16)
                if on["feat"]:
                    wait(sp, qT_d, s.t(0))
                    sp.dma_start(q_store[s.t(-1)], qT[s.par(-1)][:, :]).then_inc(st_q[s.par(-1)], 16)
                if on["proj"]:
                    o = -LAG - 1
                    wait(sp, x2_d, s.t(o + 1))
                    sp.dma_start(out_t[s.t(o)], x2[s.par(o)][:, :]).then_inc(st_x2[s.par(o)], 16)
                if s.rep == TB + 2:
                    load_weights(0, 0, raw_a)
                if s.rep == TB + 3:
                    load_weights(0, FC // 2, raw_b)

            steps(sp, step, ATT)

            sp.wait_ge(sp_h, 4)
            sp.wait_ge(sp_l, 4)
            load_weights(1, 0, raw_a)

            def expert(e, last):
                if last >= 1:
                    return
                wait(sp, sp_h, e * FC + FC)
                wait(sp, sp_l, e * FC + FC)
                load_weights(e + 1, FC // 2, raw_b)
                if last == 0:
                    wait(sp, sp_h, e * FC + FC + FC // 2)
                    wait(sp, sp_l, e * FC + FC + FC // 2)
                    load_weights(e + 2, 0, raw_a)

            with sp.Fori(0, (E - 2) // 2) as k:
                expert(k * 2, 0)
                expert(k * 2 + 1, 0)
            expert(E - 2, 0.5)

        @block.gpsimd
        def _(pool):
            pool.dma_start(pad[:, :], rope[0:1, 0:HALF]).then_inc(sc_d, 16)
            nc.gpsimd.memset(half_neg[:, :], -0.5).then_inc(plink_s, 1)
            nc.gpsimd.memset(ones_b[:, :], 1.0).then_inc(plink_s, 1)
            nc.gpsimd.memset(ones_f[:, :], 1.0).then_inc(plink_s, 1)
            nc.gpsimd.memset(zeros[:, :], 0.0).then_inc(plink_s, 1)
            for i in range(2):
                nc.gpsimd.memset(vx[i][:, :, P:P + 1], 1.0).then_inc(plink_s, 1)
            nc.gpsimd.memset(reset[:, :, :], 1.0).then_inc(plink_s, 1)
            pool.wait_ge(plink_s, 7)
            nc.gpsimd.memset(reset[:, :, 0:1], 0.0).then_inc(plink_s, 1)
            nc.gpsimd.affine_select(out=before[:, :], in_=ones_b[:, :], compare_op=ALU.is_gt, fill=0.0, base=0,
                                    pattern=[[1, P]], channel_multiplier=-1).then_inc(plink_s, 1)
            nc.gpsimd.iota(iota_b[:, :, :], pattern=[[1, P], [0, NT]], base=0, channel_multiplier=0,
                           allow_small_or_imprecise_dtypes=True).then_inc(plink_s, 1)
            nc.gpsimd.iota(rev[:, :], pattern=[[-1, E]], base=E, channel_multiplier=0,
                           allow_small_or_imprecise_dtypes=True).then_inc(plink_s, 1)
            nc.gpsimd.iota(tile_thr[:, :], pattern=[[P, CT + 1]], base=0, channel_multiplier=0,
                           allow_small_or_imprecise_dtypes=True).then_inc(plink_s, 1)
            nc.gpsimd.iota(vals[:, :, :, 0], pattern=[[0, E], [0, NT]], base=0, channel_multiplier=1,
                           allow_small_or_imprecise_dtypes=True).then_inc(plink_s, 1)
            nc.gpsimd.iota(vals[:, :, :, 1], pattern=[[0, E], [1, NT]], base=1, channel_multiplier=0,
                           allow_small_or_imprecise_dtypes=True).then_inc(plink_s, 1)

            def step(s):
                on = stages(s)
                if on["second"]:
                    o = -LAG - 2
                    b = (s.rep + o) // TB
                    wait(pool, stat2, s.t(o + 1))
                    nc.gpsimd.tensor_tensor(rs2[:, :], ve2[:, :], half_neg[:, :], ALU.pow).then_inc(pow2, 1)
                    wait_apart(pool, pow2, s.t(o + 1), apart)
                    nc.gpsimd.tensor_scalar(xn2[:, :], x2[s.par(o)][:, :], nm2[:, :], rs2[:, :], ALU.add, ALU.mult)\
                        .then_inc(pn2, 1)
                    pool.wait_ge(pn2, s.t(o + 1))
                    nc.gpsimd.tensor_tensor(xm2[:, :], xn2[:, :], row_sb[b][:, 1, :], ALU.mult).then_inc(pm2, 1)
                    pool.wait_ge(pm2, s.t(o + 1))
                    wait(pool, st_h2[s.par(o)], s.half(o) * 16)
                    wait(pool, tr_h2, s.t(o - 1))
                    nc.gpsimd.tensor_tensor(h2[s.par(o)][:, :], xm2[:, :], row_sb[b][:, 0, :], ALU.add)\
                        .then_inc(h2_d, 1)
                if on["norm"]:
                    wait(pool, stat1, s.t(2))
                    nc.gpsimd.tensor_tensor(rs1[:, :], ve1[:, :], half_neg[:, :], ALU.pow).then_inc(pow1, 1)
                    wait(pool, tr_h, s.t(1))
                    wait_apart(pool, pow1, s.t(2), apart)
                    nc.gpsimd.tensor_scalar(hn[:, :], x_in[s.par(1)][:, :], nm1[:, :], rs1[:, :], ALU.add, ALU.mult)\
                        .then_inc(norm1, 1)
                if on["qkv"]:
                    wait(pool, rope_m, s.t(1))
                    wait(pool, exp_d, s.t(0))
                    nc.gpsimd.tensor_tensor(rot[:, :], rot_a[:, :], rot_b[:, :], ALU.add).then_inc(rope_d, 1)

            steps(pool, step, ATT)

            wT = lambda a: a.rearrange("p n e -> p e n")
            pool.wait_ge(r_dve, 1)
            nc.gpsimd.tensor_copy(w_hi[:, :, :], wgt[:, :, :]).then_inc(r_pool, 1)
            pool.wait_ge(r_pool, 1)
            nc.gpsimd.tensor_tensor(w_r1[:, :, :], wgt[:, :, :], w_hi[:, :, :], ALU.subtract).then_inc(r_pool, 1)
            pool.wait_ge(r_pool, 2)
            nc.gpsimd.tensor_copy(w_mid[:, :, :], w_r1[:, :, :]).then_inc(r_pool, 1)
            pool.wait_ge(r_pool, 3)
            nc.gpsimd.tensor_tensor(w_r2[:, :, :], w_r1[:, :, :], w_mid[:, :, :], ALU.subtract).then_inc(r_pool, 1)
            pool.wait_ge(r_pool, 4)
            nc.gpsimd.tensor_copy(vals[:, :, :, 2], wT(w_hi[:, :, :])).then_inc(r_pool, 1)
            nc.gpsimd.tensor_copy(vals[:, :, :, 3], wT(w_mid[:, :, :])).then_inc(r_pool, 1)
            nc.gpsimd.tensor_copy(vals[:, :, :, 4], wT(w_r2[:, :, :])).then_inc(r_pool, 1)

            def split_low(e, f, count):
                raw = raw_a if f < FC // 2 else raw_b
                wait(pool, raw, (e + 1) * 5 * 16)
                wait(pool, sp_h, count + 1)
                nc.gpsimd.tensor_tensor(w_l[:, f, :], w_raw[:, f, :], w_h[:, f, :].bitcast(F32), ALU.subtract)\
                    .then_inc(sp_l, 1)

            for f in range(FC - 2):
                split_low(0, f, f)

            def gather(rows, dst, idx, done):
                for a in range(CT):
                    nc.gpsimd.indirect_dma_start(
                        out=dst[:, a, :], out_offset=None, in_=rows,
                        in_offset=bass.IndirectOffsetOnAxis(ap=idx[:, a:a + 1], axis=0)).then_inc(done, 16)

            for i in range(2):
                pool.wait_ge(st_h2[i], NT // 2 * 16)
                pool.wait_ge(st_x2[i], NT // 2 * 16)
            pool.wait_ge(idx_d, 1)
            gather(h2_rows, xg, g_idx[0], ga_d)

            def expert(e, par, last):
                for f in (0, 1):
                    split_low(e, FC - 2 + f, e * FC + FC - 2 + f)
                if last < 1:
                    wait_apart(pool, idx_d, e + 2, apart)
                    wait_apart(pool, trx_d, e * 3 + 3, apart)
                    gather(h2_rows, xg, g_idx[1 - par], ga_d)
                wait_apart(pool, sc_d, e * CT * 16 + 16, apart)
                gather(out_rows, xo, g_idx[par], xo_d)
                if last < 1:
                    for f in range(FC - 2):
                        split_low(e + 1, f, e * FC + FC + f)
                for a in range(CT):
                    wait_apart(pool, yo_d, e * CT + a + 1, apart)
                    nc.gpsimd.indirect_dma_start(
                        out=out_rows, out_offset=bass.IndirectOffsetOnAxis(ap=s_idx[par][:, a:a + 1], axis=0),
                        in_=yo[:, a, :], in_offset=None, bounds_check=N - 1, oob_is_err=False).then_inc(sc_d, 16)

            with pool.Fori(0, (E - 2) // 2) as k:
                expert(k * 2, 0, 0)
                expert(k * 2 + 1, 1, 0)
            expert(E - 2, 0, 0.5)
            expert(E - 1, 1, 1)
            pool.wait_ge(sc_d, E * CT * 16 + 16)

        @block.scalar
        def _(act):
            act.wait_ge(ld_c, 32)
            nc.scalar.activation(c_act[:, :], c_sb[:, :], ACT.Silu).then_inc(act_pre, 1)

            def step(s):
                on = stages(s)
                if on["feat"]:
                    wait(act, rope_d, s.t(0))
                    wait(act, feat_d, s.t(-1))
                    nc.scalar.activation(ex[:, :], rot[:, :], ACT.Exp)
                    nc.scalar.activation(rl[:, :], rot[:, :], ACT.Relu).then_inc(exp_d, 1)
                if on["proj"]:
                    o = -LAG - 1
                    wait(act, tr_o, s.t(o + 1))
                    wait(act, y_d, s.t(o))
                    nc.scalar.copy(attT[:, :], oT_ps).then_inc(oT_d, 1)
                if on["logit"]:
                    o = -LAG - 3
                    wait(act, lg_d, s.t(o + 1))
                    nc.scalar.copy(logits[:, s.t(o), :], lg_ps).then_inc(lgc, 1)
                if on["qkv"]:
                    wait(act, qkv_done, s.t(1))
                    wait(act, kv_d, s.t(-1))
                    if s.rep < 2:
                        act.wait_ge(plink_s, 7)
                    nc.scalar.copy(vx[s.par(0)][:, :, 0:P], v_ps.rearrange("p (c n) -> p c n", c=KC)).then_inc(v_done, 1)
                if on["feat"]:
                    wait(act, tr_q, s.t(0))
                    wait(act, st_q[s.par(-1)], s.half(-1) * 16)
                    nc.scalar.copy(qT[s.par(-1)][:, :], qT_ps).then_inc(qT_d, 1)
                if on["second"]:
                    o = -LAG - 2
                    wait(act, tr_h2, s.t(o + 1))
                    wait(act, lg_d, s.t(o))
                    nc.scalar.copy(h2T[:, :], h2T_ps).then_inc(h2T_d, 1)
                if on["norm"]:
                    b = (s.rep + 1) // TB
                    if s.rep == -1:
                        act.wait_ge(dve_pre, 3)
                    wait(act, tr_h, s.t(2))
                    wait(act, qkv_done, s.t(1))
                    nc.scalar.activation(hT[:, 0, :], hT_ps[0], ACT.Identity, bias=mod_col[:, 0, 0, b:b + 1],
                                         scale=mod_col[:, 1, 0, b:b + 1]).then_inc(hT_a, 1)

            steps(act, step, ATT)

            act.wait_ge(r_act, 1)
            nc.scalar.activation(big[1][:, :, :], big[0][:, :, :], ACT.Exp).then_inc(act_pre, 1)

            def split_high(e, f, count, implied=False):
                raw = raw_a if f < FC // 2 else raw_b
                wait(act, raw, (e + 1) * 5 * 16)
                if not implied:
                    wait(act, dn_d, count - FC + 1)
                nc.scalar.copy(w_h[:, f, :], w_raw[:, f, :]).then_inc(sp_h, 1)

            for f in range(FC - 2):
                split_high(0, f, f)

            def x_high(e, par, g):
                n = min(2, CT - 2 * g) * P
                wait(act, trx_d, e * 3 + g + 1)
                nc.scalar.copy(xT_h[par][:, :, 2 * g * P:2 * g * P + n],
                               bank[7][:, 0:2 * n].rearrange("p (c n) -> p c n", c=KC)).then_inc(xh_d, 1)

            for g in range(3):
                x_high(0, 0, g)

            def expert(e, par, last):
                def weigh(a):
                    wait(act, idx_d, e + 1)
                    if a:
                        wait(act, gw_d, e * CT + a)
                    nc.scalar.activation(gw0[:, :], gates[0][:, 1, :], ACT.Copy, scale=w_b[par][:, 0, a:a + 1])\
                        .then_inc(gw0_d, 1)

                for f in range(FC):
                    for h in range(2):
                        i = e * 2 * FC + 2 * f + h
                        wait(act, gu_d, i + 1)
                        if f:
                            wait(act, hid_d, i - 1)
                        nc.scalar.activation(act_g[h][:, :], bank[2 * h][:, 0:HCAP], ACT.Silu).then_inc(silu_d, 1)
                        wait(act, hid_d, i + 1)
                        if f >= 2:
                            wait(act, dn_d, e * FC + f - 1)
                        nc.scalar.copy(hid_h[f % 2][:, h * HCAP:(h + 1) * HCAP], hid[h][:, :]).then_inc(hh_d, 1)
                    if f < 2:
                        split_high(e, FC - 2 + f, e * FC + FC - 2 + f, implied=True)
                    elif last < 1:
                        split_high(e + 1, f - 2, e * FC + FC + f - 2)
                    if f < CT:
                        weigh(f)
                    if last < 1 and XF <= f < XF + 3:
                        x_high(e + 1, 1 - par, f - XF)

            with act.Fori(0, (E - 2) // 2) as k:
                expert(k * 2, 0, 0)
                expert(k * 2 + 1, 1, 0)
            expert(E - 2, 0, 0.5)
            expert(E - 1, 1, 1)

        @block.vector
        def _(dve):
            chain = [0]

            def link(ins):
                chain[0] += 1
                ins.then_inc(link_s, 1)
                dve.wait_ge(link_s, chain[0])

            V = nc.vector
            dve.wait_ge(pe_pre, 1)
            link(V.tensor_copy(cT[:, :, :], bank[0][:, 0:KC * B].rearrange("p (c b) -> p c b", c=KC)))
            V.tensor_copy(c_bc[:, :, :, :], cT[:, :, :].unsqueeze(3).to_broadcast([P, KC, B, P])).then_inc(dve_pre, 1)
            dve.wait_ge(pe_pre, 2)
            V.tensor_copy(mod_col[:, 0, :, :], bank[1][:, 0:KC * B].rearrange("p (c b) -> p c b", c=KC))\
                .then_inc(dve_pre, 1)
            V.tensor_scalar(mod_col[:, 1, :, :], bank[1][:, KC * B:2 * KC * B].rearrange("p (c b) -> p c b", c=KC),
                            1.0, None, ALU.add).then_inc(dve_pre, 1)

            def prepare_weights():
                dve.wait_ge(ld_w, 48)
                V.tensor_scalar(wqkv_sb[:, :, 0:D], wqkv_sb[:, :, 0:D], float(HD) ** -0.5, None, ALU.mult)
                dve.wait_ge(pe_pre, 3 + B)
                V.tensor_copy(same_e[:, :], same_f)
                V.tensor_copy(routerT[:, :, :], bank[0][:, 2 * P:2 * P + KC * E].rearrange("p (c e) -> p c e", c=KC))\
                    .then_inc(dve_pre, 1)

            def gate_rows(b):
                dve.wait_ge(pe_pre, 4)
                rows = row_ps[b]
                g_ps = [rows[0][:, 0:D], rows[1][:, D:2 * D]]
                V.tensor_copy(row_sb[b][:, 0, :], rows[0][:, D:2 * D])
                V.tensor_scalar(row_sb[b][:, 1, :], rows[1][:, 0:D], 1.0, None, ALU.add)
                for i in range(2):
                    V.tensor_scalar(gate_sgn[:, i, :], g_ps[i], 0.0, 2.0, ALU.is_ge, ALU.mult)
                    link(V.tensor_scalar(gate_mag[:, i, :], g_ps[i], -1.0, None, ALU.mult))
                    link(V.tensor_tensor(gate_mag[:, i, :], g_ps[i], gate_mag[:, i, :], ALU.max))
                link(V.tensor_scalar(gate_mag[:, :, :], gate_mag[:, :, :], GATE_MIN, None, ALU.max))
                link(V.scalar_tensor_tensor(gates[b][:, :, :], gate_sgn[:, :, :], -1.0, gate_mag[:, :, :],
                                            ALU.add, ALU.mult))
                V.tensor_tensor(wout_g[b][:, :, :], wout_sb[:, :, :],
                                gates[b][:, 0, :].unsqueeze(1).to_broadcast([P, KC, D]), ALU.mult).then_inc(dve_pre, 1)

            def stats(src, st, mv, nm, ve, bn, ag, done, count):
                V.bn_stats(st[:, :], src).then_inc(bn, 1)
                wait_apart(dve, bn, count, apart)
                V.bn_aggr(mv[:, :], st[:, :]).then_inc(ag, 1)
                dve.wait_ge(ag, count)
                V.tensor_scalar(nm[:, :], mv[:, 0:1], -1.0, None, ALU.mult)
                V.tensor_scalar(ve[:, :], mv[:, 1:2], LN_EPS, None, ALU.add).then_inc(done, 1)

            def step(s):
                on = stages(s)
                if on["feat"]:
                    wait(dve, exp_d, s.t(0))
                    wait(dve, tr_q, s.t(-1))
                    wait(dve, kv_d, s.t(-1))
                    V.scalar_tensor_tensor(feat[:, :], ex[:, :], 1.0, rl[:, :], ALU.min, ALU.add).then_inc(feat_d, 1)
                if on["qkv"]:
                    if s.rep == 0:
                        dve.wait_ge(ld_const, 16)
                    cs = rope_sb[:, s.t(-(s.rep // TB) * TB), :]
                    wait(dve, qkv_done, s.t(1))
                    wait(dve, rope_d, s.t(0))
                    g = 2 * D // HALF
                    V.tensor_tensor(rot_a[:, :].rearrange("p (g d) -> p g d", d=HALF),
                                    qk_ps.rearrange("p (g d) -> p g d", d=HALF),
                                    cs[:, 0:HALF].unsqueeze(1).to_broadcast([P, g, HALF]), ALU.mult)
                    qv = qk_ps.rearrange("p (g a d) -> p g a d", a=2, d=HALF)
                    rv = rot_b[:, :].rearrange("p (g a d) -> p g a d", a=2, d=HALF)
                    V.tensor_tensor(rv[:, :, 0, :], qv[:, :, 1, :],
                                    cs[:, 2 * HALF:].unsqueeze(1).to_broadcast([P, g // 2, HALF]), ALU.mult)
                    V.tensor_tensor(rv[:, :, 1, :], qv[:, :, 0, :],
                                    cs[:, HALF:2 * HALF].unsqueeze(1).to_broadcast([P, g // 2, HALF]), ALU.mult)\
                        .then_inc(rope_m, 1)
                if on["proj"]:
                    o = -LAG - 1
                    wait(dve, y_d, s.t(o + 1))
                    wait(dve, ld_xr[s.par(o)], (s.half(o) + 1) * 16)
                    wait(dve, st_x2[s.par(o)], s.half(o) * 16)
                    wait(dve, pn2, s.t(o - 1))
                    V.tensor_tensor(x2[s.par(o)][:, :], y_ps, x_re[s.par(o)][:, :], ALU.add).then_inc(x2_d, 1)
                if on["att"]:
                    o = -LAG
                    wait(dve, o_d, s.t(o + 1))
                    V.tensor_scalar(den_m[:, :, :], o_ps[:, :, P:], DEN_EPS, None, ALU.max).then_inc(dmax, 1)
                    dve.wait_ge(dmax, s.t(o + 1))
                    V.reciprocal(den_r[:, :, :], den_m[:, :, :]).then_inc(drec, 1)
                if on["proj"]:
                    o = -LAG - 1
                    dve.wait_ge(x2_d, s.t(o + 1))
                    wait(dve, pn2, s.t(o))
                    stats(x2[s.par(o)][:, :], st2, mv2, nm2, ve2, bn2, ag2, stat2, s.t(o + 1))
                if on["att"]:
                    o = -LAG
                    dve.wait_ge(drec, s.t(o + 1))
                    wait(dve, tr_o, s.t(o))
                    V.tensor_tensor(att[:, :].rearrange("p (c h d) -> p c h d", c=KC, d=HD),
                                    o_ps[:, :, 0:P].rearrange("p c (h d) -> p c h d", d=HD),
                                    den_r[:, :, :].unsqueeze(3).to_broadcast([P, KC, HC, HD]), ALU.mult)\
                        .then_inc(att_d, 1)
                if s.rep in (TB, NT):
                    b = s.rep // TB - 1
                    dve.wait_ge(kv_d, s.rep)
                    V.tensor_tensor(kvb[b][:, :, 0:P], kv_ps[:, :, 0:P],
                                    blk[:, 0:P].unsqueeze(1).to_broadcast([P, KC, P]), ALU.mult)
                    V.tensor_tensor(kvb[b][:, :, P:], kv_ps[:, :, P:P + 1].to_broadcast([P, KC, HC]),
                                    blk[:, P:].unsqueeze(1).to_broadcast([P, KC, HC]), ALU.mult).then_inc(kvb_d, 1)
                if on["norm"]:
                    b = (s.rep + 1) // TB
                    wait(dve, tr_h, s.t(2))
                    wait(dve, qkv_done, s.t(1))
                    if s.rep == -1:
                        dve.wait_ge(dve_pre, 3)
                    V.tensor_scalar(hT[:, 1, :], hT_ps[1], mod_col[:, 1, 1, b:b + 1], mod_col[:, 0, 1, b:b + 1],
                                    ALU.mult, ALU.add).then_inc(hT_d, 1)
                if on["stats"]:
                    wait(dve, ld_x[s.par(2)], (s.half(2) + 1) * 16)
                    wait(dve, norm1, s.t(2))
                    stats(x_in[s.par(2)][:, :], st1, mv1, nm1, ve1, bn1, ag1, stat1, s.t(3))
                if s.rep == -2:
                    prepare_weights()
                if s.rep in (0, 1):
                    gate_rows(1 - s.rep)

            steps(dve, step, ATT)

            b8 = lambda a: a.unsqueeze(2).to_broadcast([P, NT, E])
            rev_b = rev[:, :].unsqueeze(1).to_broadcast([P, NT, E])
            X = [t[:, :, :] for t in big]
            Y = [t[:, :] for t in small]
            TT, RED = V.tensor_tensor, V.tensor_reduce
            dve.wait_ge(lgc, NT)
            dve.wait_ge(plink_s, 13)
            link(RED(Y[0], logits[:, :, :], AX, ALU.max))
            TT(X[0], logits[:, :, :], b8(Y[0]), ALU.subtract).then_inc(r_act, 1)
            dve.wait_ge(act_pre, 2)
            link(RED(Y[1], X[1], AX, ALU.add))
            link(V.reciprocal(Y[2], Y[1]))
            link(TT(X[2], X[1], b8(Y[2]), ALU.mult))
            tops = []
            prob = X[2]
            for i in range(TOPK):
                m, first, hot, q = Y[3 + i], Y[5 + i], X[3 + i], X[5]
                link(RED(m, prob, AX, ALU.max))
                link(TT(q, prob, b8(m), ALU.is_equal))
                link(TT(q, q, rev_b, ALU.mult))
                link(RED(first, q, AX, ALU.max))
                link(TT(hot, q, b8(first), ALU.is_equal))
                tops.append((m, hot))
                if i == 0:
                    link(V.scalar_tensor_tensor(X[6], hot, -2.0, prob, ALU.mult, ALU.add))
                    prob = X[6]
            link(TT(Y[0], Y[3], Y[4], ALU.add))
            link(V.tensor_scalar(Y[0], Y[0], TOPW_EPS, None, ALU.add))
            link(V.reciprocal(Y[1], Y[0]))
            TT(Y[5], Y[3], Y[1], ALU.mult)
            link(TT(Y[6], Y[4], Y[1], ALU.mult))
            TT(X[0], X[3], b8(Y[5]), ALU.mult)
            TT(X[1], X[4], b8(Y[6]), ALU.mult)
            link(TT(X[7], X[3], X[4], ALU.add))
            link(TT(wgt[:, :, :], X[0], X[1], ALU.add))
            V.tensor_scalar(X[5], X[7], -1.0, None, ALU.add).then_inc(r_dve, 1)
            dve.wait_ge(r_dve, 1)
            TT(val[:, :, :], wgt[:, :, :], X[5], ALU.add).then_inc(r_dve, 1)
            V.memset(thr[:, :], 0)
            V.memset(bit[:, :], 1 << (TOP_BIT - 1))
            link(V.memset(cand[:, :], 1 << TOP_BIT))
            dve.wait_ge(r_pe, 1)
            link(V.tensor_copy(valT[:, :], bank[0][:, 0:2 * P]))
            with dve.Fori(0, TOP_BIT + 1) as i:
                V.tensor_scalar(hit[:, :], valT[:, :], cand[:, :].bitcast(F32), 0.0, ALU.is_ge, ALU.add,
                                accum_out=cnt[:, :]).then_inc(cnt_d, 1)
                dve.wait_ge(tot_d, i + 1)
                V.tensor_scalar(flag[:, :], bank[1][:, 0:1], float(CAP), None, ALU.is_ge).then_inc(flag_d, 1)
                wait_apart(dve, flag_d, i + 1, apart)
                V.copy_predicated(thr[:, :], flag[:, :], cand[:, :]).then_inc(thr_d, 1)
                dve.wait_ge(thr_d, i + 1)
                TT(cand[:, :], thr[:, :], bit[:, :], ALU.bitwise_or).then_inc(cand_d, 1)
                dve.wait_ge(cand_d, i + 1)
                V.tensor_scalar(bit[:, :], bit[:, :], 1, None, ALU.logical_shift_right).then_inc(bit_d, 1)
                dve.wait_ge(bit_d, i + 1)
            V.tensor_scalar(thr_sel[:, :], sel_e[:, :], thr[:, :].bitcast(F32), None, ALU.mult).then_inc(r_dve, 1)
            dve.wait_ge(r_pe, 2)
            link(V.tensor_copy(thr_b[:, :], bank[2][:, 0:E]))
            tb = thr_b[:, :].unsqueeze(1).to_broadcast([P, NT, E])
            TT(mask2[:, 0, :, :].rearrange("p e n -> p n e"), val[:, :, :], tb, ALU.is_gt)
            TT(mask2[:, 1, :, :].rearrange("p e n -> p n e"), val[:, :, :], tb, ALU.is_equal).then_inc(r_dve, 1)
            dve.wait_ge(r_pe, 3)
            tot = bank[4][:, :]
            m2 = lambda a: a.rearrange("p k e n -> p (k e n)")
            link(V.tensor_tensor_scan(m2(run[:, :, :, :]), reset[:, :, :].rearrange("p g n -> p (g n)"), tot, 0.0,
                                      ALU.mult, ALU.add))
            V.tensor_scalar(need[:, :], run[:, 0, :, NT - 1], -1.0, float(CAP), ALU.mult, ALU.add)
            link(TT(m2(pre[:, :, :, :]), m2(run[:, :, :, :]), tot, ALU.subtract))
            link(TT(m2(pre[:, :, :, :]), m2(pre[:, :, :, :]), bank[3][:, :], ALU.add))
            need_b = need[:, :].unsqueeze(2).to_broadcast([P, E, NT])
            TT(tmp_s[:, :, :], pre[:, 1, :, :], need_b, ALU.is_lt)
            link(TT(slot[:, :, :], pre[:, 1, :, :], need_b, ALU.min))
            link(TT(tmp_s[:, :, :], tmp_s[:, :, :], mask2[:, 1, :, :], ALU.mult))
            TT(keep[:, :, :], tmp_s[:, :, :], mask2[:, 0, :, :], ALU.add)
            link(TT(slot[:, :, :], slot[:, :, :], pre[:, 0, :, :], ALU.add))
            link(V.scalar_tensor_tensor(keep[:, :, :], slot[:, :, :], float(CAP), keep[:, :, :], ALU.is_lt, ALU.mult))
            link(V.scalar_tensor_tensor(slot[:, :, :], slot[:, :, :], 1.0, keep[:, :, :], ALU.add, ALU.mult))
            V.tensor_scalar(slot[:, :, :], slot[:, :, :], -1.0, None, ALU.add).then_inc(slots_d, 1)
            dve.wait_ge(slots_d, 1)
            dve.wait_ge(r_pool, 7)

            def describe_tiles(e):
                sl = slot[:, e, :]
                TT(tile_ge[:, :, :], sl.unsqueeze(2).to_broadcast([P, NT, CT + 1]),
                   tile_thr[:, :].unsqueeze(1).to_broadcast([P, NT, CT + 1]), ALU.is_ge).then_inc(ge_d, 1)
                dve.wait_ge(ge_d, e + 1)
                RED(tile_no[:, :], tile_ge[:, :, 1:], AX, ALU.add).then_inc(tn_d, 1)
                TT(in_tile[:, :, :], tile_ge[:, :, 0:CT], tile_ge[:, :, 1:], ALU.subtract).then_inc(in_d, 1)
                dve.wait_ge(tn_d, e + 1)
                V.scalar_tensor_tensor(row_in[:, :], tile_no[:, :], -float(P), sl, ALU.mult, ALU.add).then_inc(ri_d, 1)

            def describe_facts(e):
                wait(dve, look_d, e)
                dve.wait_ge(in_d, e + 1)
                TT(facts[:, :, :, :], vals[:, e, :, :].unsqueeze(3).to_broadcast([P, NT, NV, CT]),
                   in_tile[:, :, :].unsqueeze(2).to_broadcast([P, NT, NV, CT]), ALU.mult)

            def describe_rows(e):
                dve.wait_ge(ri_d, e + 1)
                TT(onehot[:, :, :], iota_b[:, :, :], row_in[:, :].unsqueeze(1).to_broadcast([P, P, NT]), ALU.is_equal)\
                    .then_inc(facts_d, 1)

            def describe(e):
                describe_tiles(e)
                describe_facts(e)
                describe_rows(e)

            fin_n = 7

            def finish(e, par, slots=True):
                n = [0]

                def lk(ins):
                    n[0] += 1
                    ins.then_inc(fin_l, 1)
                    dve.wait_ge(fin_l, e * fin_n + n[0])

                dve.wait_ge(look_d, e + 1)
                V.tensor_copy(got[:, :, :], bank[7][:, 0:NV * CT].rearrange("p (v a) -> p v a", v=NV))\
                    .then_inc(got_d, 1)
                dve.wait_ge(got_d, e + 1)
                lk(V.scalar_tensor_tensor(tok[:, :], got[:, 1, :], float(P), got[:, 0, :], ALU.mult, ALU.add))
                V.tensor_scalar(far[:, :], got[:, 1, :], 0.5, float(FAR), ALU.is_lt, ALU.mult)
                lk(V.tensor_scalar(tok[:, :], tok[:, :], -float(P), 0.0, ALU.add, ALU.max))
                if slots:
                    wait(dve, sc_d, (e - 1) * CT * 16 + 16)
                V.tensor_copy(g_idx[par][:, :], tok[:, :])
                lk(TT(s_idx[par][:, :], tok[:, :], far[:, :], ALU.add))
                lk(TT(w_slot[:, 0, :], got[:, 2, :], got[:, 3, :], ALU.add))
                lk(TT(w_slot[:, 1, :], w_slot[:, 0, :], got[:, 4, :], ALU.add))
                lk(V.tensor_scalar(w_slot[:, 2, :], got[:, 1, :], float(TB) + 0.5, None, ALU.is_ge))
                lk(TT(w_b[par][:, 1, :], w_slot[:, 2, :], w_slot[:, 1, :], ALU.mult))
                assert n[0] == fin_n
                TT(w_b[par][:, 0, :], w_slot[:, 1, :], w_b[par][:, 1, :], ALU.subtract).then_inc(idx_d, 1)

            dve.sem_inc(ym_d, 1)
            describe(0)
            finish(0, 0, slots=False)
            describe(1)

            def x_low(e, par, g):
                n = min(2, CT - 2 * g) * P
                wait(dve, xh_d, e * 3 + g + 1)
                sl = slice(2 * g * P, 2 * g * P + n)
                V.tensor_tensor(xT_l[par][:, :, sl], bank[7][:, 0:2 * n].rearrange("p (c n) -> p c n", c=KC),
                                xT_h[par][:, :, sl].bitcast(F32), ALU.subtract).then_inc(xl_d, 1)

            for g in range(3):
                x_low(0, 0, g)

            def expert(e, par, last):
                for f in range(FC):
                    for h in range(2):
                        i = e * 2 * FC + 2 * f + h
                        wait(dve, silu_d, i + 1)
                        if f:
                            wait(dve, hh_d, i - 1)
                        V.tensor_tensor(hid[h][:, :], act_g[h][:, :], bank[2 * h + 1][:, 0:HCAP], ALU.mult)\
                            .then_inc(hid_d, 1)
                        wait(dve, hh_d, i + 1)
                        V.tensor_tensor(hid_l[f % 2][:, h * HCAP:(h + 1) * HCAP], hid[h][:, :],
                                        hid_h[f % 2][:, h * HCAP:(h + 1) * HCAP].bitcast(F32), ALU.subtract)\
                            .then_inc(hl_d, 1)
                    if f < CT:
                        wait(dve, gw0_d, e * CT + f + 1)
                        V.scalar_tensor_tensor(gw[:, f, :], gates[1][:, 1, :], w_b[par][:, 1, f:f + 1], gw0[:, :],
                                               ALU.mult, ALU.add).then_inc(gw_d, 1)
                    if f == 1 and last < 1:
                        finish(e + 1, 1 - par)
                    if last == 0:
                        if f == 2:
                            describe_tiles(e + 2)
                        if f == 3:
                            describe_facts(e + 2)
                        if f == 4:
                            describe_rows(e + 2)
                    if last < 1 and XF <= f < XF + 3:
                        x_low(e + 1, 1 - par, f - XF)
                wait(dve, sc_d, e * CT * 16 + 16)
                for a in range(CT):
                    if a == CT - 1:
                        wait(dve, dn_d, (e + 1) * FC)
                    elif a % 2 == 0:
                        wait(dve, y_tile, e * (CT // 2) + a // 2 + 1)
                    V.tensor_tensor(yo[:, a, :], bank[4 + a // 2][:, a % 2 * D:(a % 2 + 1) * D], gw[:, a, :], ALU.mult)\
                        .then_inc(ym_d, 1)
                    wait(dve, ym_d, e * CT + a + 2)
                    wait(dve, xo_d, (e + 1) * CT * 16)
                    V.tensor_tensor(yo[:, a, :], yo[:, a, :], xo[:, a, :], ALU.add).then_inc(yo_d, 1)

            with dve.Fori(0, (E - 2) // 2) as k:
                expert(k * 2, 0, 0)
                expert(k * 2 + 1, 1, 0)
            expert(E - 2, 0, 0.5)
            expert(E - 1, 1, 1)

        @block.tensor
        def _(pe):
            MM = nc.tensor.matmul
            TR = nc.tensor.transpose
            pe.wait_ge(act_pre, 1)
            for k in range(KC):
                last = TR(bank[0][:, k * B:(k + 1) * B], c_act[:, k * P:(k + 1) * P], ident[0:B, 0:B])
            last.then_inc(pe_pre, 1)
            pe.wait_ge(dve_pre, 1)
            pe.wait_ge(ld_mod, 16)
            for i in range(2):
                for m in range(KC):
                    for k in range(KC):
                        at = i * D + m * P
                        last = MM(bank[1][:, (i * KC + m) * B:(i * KC + m + 1) * B], wmod_sb[:, k, at:at + P],
                                  cT[:, k, :], start=k == 0, stop=k == KC - 1)
            last.then_inc(pe_pre, 1)
            for b in range(B):
                for i in range(2):
                    for k in range(KC):
                        at = 2 * D + i * 512
                        last = MM(row_ps[b][i][:, :], c_bc[:, k, b, :], wmod_sb[:, k, at:at + 512],
                                  start=k == 0, stop=k == KC - 1)
                last.then_inc(pe_pre, 1)
            pe.wait_ge(ld_w, 48)
            for k in range(KC):
                last = TR(bank[0][:, 2 * P + k * E:2 * P + (k + 1) * E], router_sb[:, k * P:(k + 1) * P],
                          ident[0:E, 0:E])
            last.then_inc(pe_pre, 1)

            def step(s):
                on = stages(s)
                if on["proj"]:
                    o = -LAG - 1
                    wait(pe, att_d, s.t(o + 1))
                    wait(pe, x2_d, s.t(o))
                    for k in range(KC):
                        last = TR(oT_ps[:, k * P:(k + 1) * P], att[:, k * P:(k + 1) * P], ident[:, :])
                    last.then_inc(tr_o, 1)
                if on["logit"]:
                    o = -LAG - 3
                    wait(pe, h2T_d, s.t(o + 1))
                    wait(pe, att_d, min(s.t(o + 3), NT) if isinstance(s.k, int) else s.t(o + 3))
                    for k in range(KC):
                        last = MM(lg_ps, h2T[:, k * P:(k + 1) * P], routerT[:, k, :], start=k == 0, stop=k == KC - 1)
                    last.then_inc(lg_d, 1)
                if on["qkv"]:
                    if s.rep == 0:
                        pe.wait_ge(dve_pre, 4)
                    wait(pe, hT_a, s.t(1))
                    wait(pe, hT_d, s.t(1))
                    wait(pe, rope_m, s.t(0))
                    wait(pe, v_done, s.t(0))
                    if s.rep > LAG + 2:
                        wait(pe, h2T_d, s.t(-LAG - 2))
                    for k in range(KC):
                        MM(qk_ps, hT[:, k, :], wqkv_sb[:, k, 0:2 * D], start=k == 0, stop=k == KC - 1)
                    for k in range(KC):
                        last = MM(v_ps, hT[:, k, :], wqkv_sb[:, k, 2 * D:], start=k == 0, stop=k == KC - 1)
                    last.then_inc(qkv_done, 1)
                if on["proj"]:
                    o = -LAG - 1
                    b = (s.rep + o) // TB
                    wait(pe, oT_d, s.t(o + 1))
                    if s.rep == LAG + 1:
                        pe.wait_ge(dve_pre, 6)
                    for k in range(KC):
                        last = MM(y_ps, attT[:, k * P:(k + 1) * P], wout_g[b][:, k, :], start=k == 0, stop=k == KC - 1)
                    last.then_inc(y_d, 1)
                if on["att"]:
                    o = -LAG
                    b = (s.rep + o) // TB
                    if s.rep == LAG:
                        pe.wait_ge(dve_pre, 6)
                    if s.rep in (TB + 1, NT + 1):
                        pe.wait_ge(kvb_d, b + 1)
                    wait(pe, ld_q[s.par(o)], (s.half(o) + 1) * 16)
                    wait(pe, att_d, s.t(o))
                    if on["logit"]:
                        wait(pe, lgc, s.t(o - 2))
                    for k in range(KC):
                        last = MM(o_ps[:, k, :], q_in[s.par(o)][:, k * P:(k + 1) * P], kvb[b][:, k, :],
                                  start=True, stop=True)
                    last.then_inc(o_d, 1)
                if on["feat"]:
                    wait(pe, feat_d, s.t(0))
                    wait(pe, qT_d, s.t(-1))
                    for k in range(KC):
                        last = TR(qT_ps[:, k * P:(k + 1) * P], feat[:, k * P:(k + 1) * P], ident[:, :])
                    last.then_inc(tr_q, 1)
                    wait(pe, v_done, s.t(0))
                    if s.rep == 1:
                        pe.wait_ge(dve_pre, 5)
                    if (s.rep - 1) % TB == 0:
                        if s.rep == 1:
                            pe.wait_ge(plink_s, 4)
                        else:
                            pe.wait_ge(kvb_d, 1)
                        MM(bank[3][:, :], zeros[0:1, 0:P], zeros[0:1, :], start=True, stop=False, skip_group_check=True)
                    for k in range(KC):
                        last = MM(kv_ps[:, k, :], feat[:, D + k * P:D + (k + 1) * P], vx[s.par(-1)][:, k, :],
                                  start=False, stop=False, skip_group_check=True)
                    last.then_inc(kv_d, 1)
                if on["second"]:
                    o = -LAG - 2
                    wait(pe, h2_d, s.t(o + 1))
                    wait(pe, h2T_d, s.t(o))
                    if on["qkv"]:
                        wait(pe, v_done, s.t(1))
                    for k in range(KC):
                        last = TR(h2T_ps[:, k * P:(k + 1) * P], h2[s.par(o)][:, k * P:(k + 1) * P], ident[:, :])
                    last.then_inc(tr_h2, 1)
                if on["norm"]:
                    wait(pe, norm1, s.t(2))
                    wait(pe, hT_a, s.t(1))
                    wait(pe, hT_d, s.t(1))
                    for k in range(KC):
                        last = TR(hT_ps[k], hn[:, k * P:(k + 1) * P], ident[:, :])
                    last.then_inc(tr_h, 1)

            steps(pe, step, ATT)

            pe.wait_ge(r_dve, 2)
            flat = val[:, :, :].rearrange("p n e -> p (n e)")
            for k in range(2):
                last = TR(bank[0][:, k * P:(k + 1) * P], flat[:, k * P:(k + 1) * P], ident[:, :])
            last.then_inc(r_pe, 1)
            with pe.Fori(0, TOP_BIT + 1) as i:
                pe.wait_ge(cnt_d, i + 1)
                MM(bank[1][:, 0:1], same_e[:, :], cnt[:, :], start=True, stop=True).then_inc(tot_d, 1)
            pe.wait_ge(r_dve, 3)
            MM(bank[2][:, 0:E], ones_f[:, :], thr_sel[:, :], start=True, stop=True).then_inc(r_pe, 1)
            pe.wait_ge(r_dve, 4)
            masks = mask2[:, :, :, :].rearrange("p k e n -> p (k e n)")
            MM(bank[3][:, :], before[:, :], masks, start=True, stop=True)
            MM(bank[4][:, :], ones_b[:, :], masks, start=True, stop=True).then_inc(r_pe, 1)

            def look(e):
                wait(pe, facts_d, e + 1)
                for n in range(NT):
                    last = MM(bank[7][:, 0:NV * CT], onehot[:, :, n], facts[:, n, :, :].rearrange("p v a -> p (v a)"),
                              start=n == 0, stop=n == NT - 1)
                last.then_inc(look_d, 1)

            def transpose_x(e, g):
                tiles = range(2 * g, min(2 * g + 2, CT))
                wait(pe, ga_d, (e + 1) * CT * 16)
                wait(pe, xl_d, e * 3 + g)
                wait(pe, got_d, e + 1)
                for k in range(KC):
                    for j, a in enumerate(tiles):
                        at = (k * len(tiles) + j) * P
                        last = TR(bank[7][:, at:at + P], xg[:, a, k * P:(k + 1) * P], ident[:, :])
                last.then_inc(trx_d, 1)

            PASSES = ((0, 0), (0, 1), (1, 0))

            look(0)
            for g in range(3):
                transpose_x(0, g)
            wait(pe, xl_d, 3)
            look(1)

            def expert(e, par, last_e):
                W, XT = (w_h, w_l), (xT_h[par], xT_l[par])

                def gate_up(f):
                    wait(pe, sp_l, e * FC + f + 1)
                    if f == 0:
                        wait(pe, xl_d, e * 3 + 3)
                    for h in range(2):
                        if f:
                            wait(pe, hid_d, e * 2 * FC + 2 * f + h - 1)
                        cols = slice(h * HCAP, (h + 1) * HCAP)
                        for m in range(2):
                            n = 0
                            for k in range(KC):
                                for i, j in PASSES:
                                    at = (2 * m + k) * P
                                    last = MM(bank[2 * h + m][:, 0:HCAP], W[i][:, f, at:at + P], XT[j][:, k, cols],
                                              start=n == 0, stop=n == 3 * KC - 1)
                                    n += 1
                        last.then_inc(gu_d, 1)

                def down(f):
                    wait(pe, hh_d, e * 2 * FC + 2 * f + 2)
                    wait(pe, hl_d, e * 2 * FC + 2 * f + 2)
                    if f == 0:
                        wait(pe, ym_d, e * CT + 1)
                    for a in range(CT):
                        for n, (i, j) in enumerate(PASSES):
                            last = MM(bank[4 + a // 2][:, a % 2 * D:(a % 2 + 1) * D],
                                      (hid_h, hid_l)[j][f % 2][:, a * P:(a + 1) * P], W[i][:, f, 4 * P:],
                                      start=f == 0 and n == 0 and a % 2 == 0, stop=f == FC - 1 and n == 2,
                                      skip_group_check=True)
                        if f == FC - 1 and a % 2 == 1:
                            last.then_inc(y_tile, 1)
                    last.then_inc(dn_d, 1)

                gate_up(0)
                for f in range(1, FC):
                    gate_up(f)
                    if last_e < 1 and XF <= f < XF + 3:
                        transpose_x(e + 1, f - XF)
                    down(f - 1)
                if last_e == 0:
                    wait(pe, xl_d, e * 3 + 6)
                    look(e + 2)
                down(FC - 1)

            with pe.Fori(0, (E - 2) // 2) as k:
                expert(k * 2, 0, 0)
                expert(k * 2 + 1, 1, 0)
            expert(E - 2, 0, 0.5)
            expert(E - 1, 1, 1)


def kernel(L0_attn_x, L0_attn_W_qkv, L0_attn_W_out, L0_ffn_router_w, L0_ffn_wg, L0_ffn_wu, L0_ffn_wd, L0_c, L0_wmod):
    import numpy as np
    from concourse import bacc
    from concourse.bass_utils import run_bass_kernel_spmd

    nc = bacc.Bacc("TRN2", target_bir_lowering=False, num_devices=1)
    inv = (1.0 / np.float32(500000.0) ** (np.arange(0, HD, 2, dtype=np.float32) / np.float32(HD))).astype(np.float32)
    ang = np.arange(T, dtype=np.float32)[:, None] * inv[None, :]
    rope = np.concatenate([np.cos(ang), np.sin(ang), -np.sin(ang)], axis=1).astype(np.float32)
    row = np.arange(P)
    consts = np.concatenate([
        row[:, None] == row[None, :],
        row[:, None] // HD == row[None, :] // HD,
        row[:, None] // HD == np.arange(HC)[None, :],
        row[:, None] == np.arange(E)[None, :],
        row[:, None] % E == row[None, :] % E,
    ], axis=1).astype(np.float32)
    arrays = {
        "x": L0_attn_x, "w_qkv": L0_attn_W_qkv, "w_out": L0_attn_W_out, "router": L0_ffn_router_w, "wg": L0_ffn_wg,
        "wu": L0_ffn_wu, "wd": L0_ffn_wd, "c": L0_c, "wmod": L0_wmod, "rope": rope, "consts": consts,
    }
    arrays = {n: np.ascontiguousarray(a) for n, a in arrays.items()}
    aps = {n: nc.dram_tensor(n, a.shape, mybir.dt.from_np(a.dtype), kind="ExternalInput").ap()
           for n, a in arrays.items()}
    out = nc.dram_tensor("out", (B, T, D), F32, kind="ExternalOutput").ap()
    build_program(nc, out=out, **aps)
    result = run_bass_kernel_spmd(nc, [arrays], core_ids=[0])
    return result.results[0]["out"]
```

```python
from contextlib import ExitStack

import concourse.bass as bass
from concourse import mybir

P = 128
F32, F32R = mybir.dt.float32, mybir.dt.float32r
BF16, I32 = mybir.dt.bfloat16, mybir.dt.int32
ALU = mybir.AluOpType
ACT = mybir.ActivationFunctionType
AX = mybir.AxisListType.X

B, T, D = 2, 2048, 256
H, HD = 16, 16
HALF = HD // 2
N = B * T
NT = N // P
TB = NT // B
KC = D // P
HC = H // KC
E, TOPK, F = 8, 2, 1024
CAP = int(1.25 * N / E)
CT = CAP // P
XG = -(-CT // 2)
FC = F // P
HCAP = CAP // 2
WU = 5 * P + P
LAG = TB + 2
LN_EPS, DEN_EPS, TOPW_EPS, GATE_MIN = 1e-5, 1e-6, 1e-6, 0.25
TOP_BIT = 29
SEARCH = 6
NV = 5
XF = 4
FAR = 1 << 20


class Step:

    def __init__(self, k, j, rep):
        self.k, self.j, self.rep = k, j, rep

    def t(self, off):
        return self.k * 2 + (self.j + off)

    def par(self, off):
        return (self.j + off) % 2

    def half(self, off):
        return self.k + (self.j + off) // 2


def wait(eng, sem, value):
    if isinstance(value, int) and value <= 0:
        return
    assert isinstance(value, int) or bass.sinput_min_value(value) > 0
    eng.wait_ge(sem, value)


def wait_apart(eng, sem, value, apart):
    wait(eng, sem, value)
    eng.sem_inc(apart, 1)


def steps(eng, emit, segments):
    for lo, hi, looped in segments:
        if looped:
            with eng.Fori(lo // 2, hi // 2) as k:
                emit(Step(k, 0, lo))
                emit(Step(k, 1, lo + 1))
        else:
            for s in range(lo, hi):
                emit(Step(s // 2, s % 2, s))


ATT = [(-3, 4, False), (4, TB - 2, True), (TB - 2, TB + 8, False), (TB + 8, NT - 4, True),
       (NT - 4, NT + 6, False), (NT + 6, NT + TB, True), (NT + TB, NT + TB + 7, False)]


def stages(s):
    r = s.rep
    u = r - LAG
    on = lambda t: 0 <= t < NT
    return dict(xload=on(r + 4), stats=on(r + 3), norm=on(r + 2), trh=on(r + 1), qkv=on(r), feat=on(r - 1), kv=on(r - 2),
                qload=on(u + 1), xrload=on(u), att=on(u), proj=on(u - 1), scale2=on(u - 2), second=on(u - 3),
                trh2=on(u - 4), logit=on(u - 5))


def build_program(nc, x, w_qkv, w_out, router, wg, wu, wd, c, wmod, rope, consts, out):
    xt = x.rearrange("b (n p) d -> (b n) p d", p=P)
    out_rows = out.rearrange("b t d -> (b t) d")
    out_t = out_rows.rearrange("(n p) d -> n p d", p=P)
    h2_rows = nc.dram_tensor("h2_rows", (N, D), F32, kind="Internal").ap()
    h2_t = h2_rows.rearrange("(n p) d -> n p d", p=P)
    q_store = nc.dram_tensor("q_store", (NT, P, D), F32, kind="Internal").ap()
    mod_store = nc.dram_tensor("mod_store", (B, 4, D), F32, kind="Internal").ap()

    with ExitStack() as ctx:
        def sb(name, shape, dt=F32):
            return ctx.enter_context(nc.sbuf_tensor(name, shape, dt))

        def sem(name):
            return ctx.enter_context(nc.semaphore(name))

        bank = [ctx.enter_context(nc.psum_tensor(f"bank{i}", [P, 512], F32)) for i in range(8)]

        const_sb = sb("const_sb", [P, 3 * P + HC + E])
        ident = const_sb[:, 0:P]
        blk = const_sb[:, P:2 * P + HC]
        sel_e = const_sb[:, 2 * P + HC:2 * P + HC + E]
        same_f = const_sb[:, 2 * P + HC + E:]
        same_e = sb("same_e", [P, P], BF16)
        before = sb("before", [P, P], BF16)
        ones_b = sb("ones_b", [P, P], BF16)
        ones_f = sb("ones_f", [P, P])
        zeros = sb("zeros", [1, 512], BF16)
        rope_sb = sb("rope_sb", [P, TB, 3 * HALF])
        router_sb = sb("router_sb", [E, D])
        routerT = sb("routerT", [P, KC, E])
        c_sb = sb("c_sb", [B, D])
        c_act = sb("c_act", [B, D])
        cT = sb("cT", [P, KC, B])
        mod_col = sb("mod_col", [P, 2, KC, B])
        mod_row = sb("mod_row", [B, 4, D])
        gate_mag = sb("gate_mag", [B, 2, D])
        gate_sgn = sb("gate_sgn", [B, 2, D])
        mod_all = sb("mod_all", [P, B, 4, D])
        pad = sb("pad", [1, HALF])
        half_neg = sb("half_neg", [P, 1])
        iota_s = sb("iota_s", [P, P], BF16)

        logits = sb("logits", [P, NT, E])

        small = [sb(f"small{i}", [P, NT]) for i in range(8)]
        rev = sb("rev", [P, E])
        wgt = sb("wgt", [P, NT, E])
        val = sb("val", [P, NT, E])
        valT = sb("valT", [P, 2 * P])
        thr, cand, base = sb("thr", [P, 1], I32), sb("cand", [P, 1], I32), sb("base", [P, 1], I32)
        won = sb("won", [P, 1], I32)
        bits = sb("bits", [P, TOP_BIT + 2, 1], I32)
        cnt = sb("cnt", [P, 1], BF16)
        hit = sb("hit", [P, 2 * P], BF16)
        thr_sel, thr_b = sb("thr_sel", [P, E]), sb("thr_b", [P, E])
        mask2 = sb("mask2", [P, 2, E, NT], BF16)
        reset = sb("reset", [P, 2 * E, NT])
        run = sb("run", [P, 2, E, NT])
        pre = sb("pre", [P, 2, E, NT])
        need = sb("need", [P, E])
        slot, keep = sb("slot", [P, E, NT]), sb("keep", [P, E, NT])
        tmp_s = sb("tmp_s", [P, E, NT])
        vals = sb("vals", [P, E, NT, NV], BF16)
        w_hi, w_mid = sb("w_hi", [P, NT, E], BF16), sb("w_mid", [P, NT, E], BF16)
        w_r1, w_r2 = sb("w_r1", [P, NT, E]), sb("w_r2", [P, NT, E])

        iota_b = sb("iota_b", [P, P, NT], BF16)
        tile_ge = sb("tile_ge", [P, NT, CT + 1])
        tile_thr = sb("tile_thr", [P, CT + 1])
        in_tile = sb("in_tile", [P, NT, CT])
        tile_no = sb("tile_no", [P, NT])
        row_in = sb("row_in", [P, NT], BF16)
        onehot = sb("onehot", [P, P, NT], BF16)
        facts = sb("facts", [P, NT, NV, CT], BF16)
        got = sb("got", [P, NV, CT])
        tok = sb("tok", [P, CT])
        far = sb("far", [P, CT])
        g_idx = [sb(f"g_idx{i}", [P, CT], I32) for i in range(2)]
        s_idx = [sb(f"s_idx{i}", [P, CT], I32) for i in range(2)]
        w_slot = sb("w_slot", [P, 3, CT])
        w_b = [sb(f"w_b{i}", [P, B, CT]) for i in range(2)]

        w_raw = sb("w_raw", [P, FC, WU])
        w_h, w_l = sb("w_h", [P, FC, WU], F32R), sb("w_l", [P, FC, WU], F32R)
        own = ExitStack()

        def sa(name, shape, dt=F32):
            return own.enter_context(nc.sbuf_tensor(name, shape, dt))

        wmod_sb = sa("wmod_sb", [P, KC, 6 * D])
        wqkv_sb = sa("wqkv_sb", [P, KC, 3 * D])
        wout_sb = sa("wout_sb", [P, KC, D])
        wout_g = [sa(f"wout_g{b}", [P, KC, D]) for b in range(B)]
        x_in = [sa(f"x_in{i}", [P, D]) for i in range(2)]
        st1, mv1 = sa("st1", [P, 6]), sa("mv1", [P, 2])
        nm1, ve1, rs1, sh1 = (sa(n, [P, 1]) for n in ("nm1", "ve1", "rs1", "sh1"))
        hn = sa("hn", [P, D])
        hT = [sa(f"hT{i}", [P, KC, P]) for i in range(2)]
        rot_a, rot_b = sa("rot_a", [P, 2 * D]), sa("rot_b", [P, 2 * D])
        rot = [sa(f"rot{i}", [P, 2 * D]) for i in range(2)]
        neg, ex, feat = sa("neg", [P, 2 * D]), sa("ex", [P, 2 * D]), sa("feat", [P, 2 * D])
        vx = [sa(f"vx{i}", [P, KC, P + 1]) for i in range(2)]
        qT = [sa(f"qT{i}", [P, D]) for i in range(2)]
        kvb = [sa(f"kvb{b}", [P, KC, P + HC]) for b in range(B)]

        q_in = [sa(f"q_in{i}", [P, D]) for i in range(2)]
        den_m, den_r = sa("den_m", [P, KC, HC]), sa("den_r", [P, KC, HC])
        att, attT = sa("att", [P, D]), sa("attT", [P, D])
        x_re = [sa(f"x_re{i}", [P, D]) for i in range(2)]
        x2 = [sa(f"x2_{i}", [P, D]) for i in range(2)]
        st2, mv2 = sa("st2", [P, 6]), sa("mv2", [P, 2])
        nm2, ve2, rs2, sh2 = (sa(n, [P, 1]) for n in ("nm2", "ve2", "rs2", "sh2"))
        xn2, xm2 = sa("xn2", [P, D]), sa("xm2", [P, D])
        h2 = [sa(f"h2_{i}", [P, D]) for i in range(2)]
        h2T = sa("h2T", [P, D])
        own.close()

        big = [sb(f"big{i}", [P, NT, E]) for i in range(8)]
        xg = sb("xg", [P, CT, D])
        xT_h = [sb(f"xT_h{i}", [P, KC, CAP], F32R) for i in range(2)]
        xT_l = [sb(f"xT_l{i}", [P, KC, CAP], F32R) for i in range(2)]
        act_g = [sb(f"act_g{i}", [P, HCAP]) for i in range(2)]
        hid = [sb(f"hid{i}", [P, HCAP]) for i in range(2)]
        hid_h = [sb(f"hid_h{i}", [P, CAP], F32R) for i in range(2)]
        hid_l = [sb(f"hid_l{i}", [P, CAP], F32R) for i in range(2)]
        gw0 = sb("gw0", [P, D])
        gw = sb("gw", [P, CT, D])
        xo, yo = sb("xo", [P, CT, D]), sb("yo", [P, CT, D])

        qk_ps = bank[0][:, :]
        v_ps = bank[1][:, 0:D]
        h2T_ps = bank[6][:, 0:D]
        o_ps = bank[2][:, 0:KC * (P + HC)].rearrange("p (c n) -> p c n", c=KC)
        lg_ps = bank[6][:, D:D + E]
        kv_ps = bank[3][:, 0:KC * (P + 1)].rearrange("p (c n) -> p c n", c=KC)
        hT_ps = bank[4][:, 0:D].rearrange("p (c n) -> p c n", c=KC)
        qT_ps = bank[5][:, 0:D]
        oT_ps = bank[7][:, 0:D]
        y_ps = bank[7][:, D:2 * D]
        row_ps = (bank[2][0:B, :], bank[7][0:B, :])

        ld_c, ld_mod, ld_const, ld_w = sem("ld_c"), sem("ld_mod"), sem("ld_const"), sem("ld_w")
        ld_rest, st_mod, ld_all = sem("ld_rest"), sem("st_mod"), sem("ld_all")
        ld_x, ld_q, ld_xr = ([sem(f"{n}{i}") for i in range(2)] for n in ("ld_x", "ld_q", "ld_xr"))
        st_q, st_x2, st_h2 = ([sem(f"{n}{i}") for i in range(2)] for n in ("st_q", "st_x2", "st_h2"))
        pe_pre, act_pre, dve_pre, pool_pre = sem("pe_pre"), sem("act_pre"), sem("dve_pre"), sem("pool_pre")
        link_s, plink_s = sem("link_s"), sem("plink_s")
        bn1, ag1, stat1, pow1, scale1, norm1 = (sem(n) for n in ("bn1", "ag1", "stat1", "pow1", "scale1", "norm1"))
        tr_h, hT_d, qk_done, qkv_done, neg_d = (sem(n) for n in ("tr_h", "hT_d", "qk_done", "qkv_done", "neg_d"))
        rope_m, rope_d, v_done, exp_d, feat_d = (sem(n) for n in ("rope_m", "rope_d", "v_done", "exp_d", "feat_d"))
        tr_q, qT_d, kv_d, kvb_d, kvb_link = (sem(n) for n in ("tr_q", "qT_d", "kv_d", "kvb_d", "kvb_link"))
        o_d, dmax, drec, att_d = sem("o_d"), sem("dmax"), sem("drec"), sem("att_d")
        tr_o, oT_d, y_d, x2_d = sem("tr_o"), sem("oT_d"), sem("y_d"), sem("x2_d")
        bn2, ag2, stat2, pow2, scale2 = (sem(n) for n in ("bn2", "ag2", "stat2", "pow2", "scale2"))
        norm2, pm2, h2_d = sem("norm2"), sem("pm2"), sem("h2_d")
        tr_h2, h2T_d, lg_d, lgc = sem("tr_h2"), sem("h2T_d"), sem("lg_d"), sem("lgc")
        iota_d = sem("iota_d")
        r_dve, r_act, r_pe, r_pool = sem("r_dve"), sem("r_act"), sem("r_pe"), sem("r_pool")
        cnt_d, tot_d, thr_d, base_d, won_d, cand_d = (sem(n) for n in ("cnt_d", "tot_d", "thr_d", "base_d", "won_d", "cand_d"))
        slots_d = sem("slots_d")
        ge_d, in_d, tn_d, ri_d = sem("ge_d"), sem("in_d"), sem("tn_d"), sem("ri_d")
        facts_d, look_d, got_d, fin_l, idx_d = (sem(n) for n in ("facts_d", "look_d", "got_d", "fin_l", "idx_d"))
        raw_a, raw_b, sp_h, sp_l = sem("raw_a"), sem("raw_b"), sem("sp_h"), sem("sp_l")
        ga_d = [sem(f"ga_d{g}") for g in range(XG)]
        trx_d, xh_d, xl_d = sem("trx_d"), sem("xh_d"), sem("xl_d")
        gu_d, silu_d, hid_d, hh_d, hl_d, dn_d = (sem(n) for n in ("gu_d", "silu_d", "hid_d", "hh_d", "hl_d", "dn_d"))
        y_tile, wb_l, wb_d = sem("y_tile"), sem("wb_l"), sem("wb_d")
        gw0_d, gw_d, xo_d, ym_d, yo_d, sc_d = (sem(n) for n in ("gw0_d", "gw_d", "xo_d", "ym_d", "yo_d", "sc_d"))

        apart = sem("apart")

        block = ctx.enter_context(nc.Block())

        @block.sync
        def _(sp):
            sp.dma_start(c_sb[:, :], c).then_inc(ld_c, 16)
            sp.dma_start(const_sb[:, :], consts).then_inc(ld_c, 16)
            sp.dma_start(x_in[0][:, :], xt[0]).then_inc(ld_x[0], 16)
            sp.dma_start(x_in[1][:, :], xt[1]).then_inc(ld_x[1], 16)
            wm = wmod.rearrange("(c p) n -> p c n", p=P)
            sp.dma_start(wmod_sb[:, :, 0:2 * D], wm[:, :, 0:2 * D]).then_inc(ld_mod, 16)
            sp.dma_start(wqkv_sb[:, :, :], w_qkv.rearrange("(c p) n -> p c n", p=P)).then_inc(ld_w, 16)
            sp.dma_start(rope_sb[:, :, :], rope.rearrange("(n p) d -> p n d", p=P)).then_inc(ld_const, 16)
            sp.dma_start(wmod_sb[:, :, 2 * D:], wm[:, :, 2 * D:]).then_inc(ld_rest, 16)
            sp.dma_start(router_sb[:, :], router).then_inc(ld_rest, 16)
            sp.dma_start(wout_sb[:, :, :], w_out.rearrange("(c p) n -> p c n", p=P)).then_inc(ld_rest, 16)

            def load_weights(e, lo, done):
                hi = lo + FC // 2
                for k in range(KC):
                    for w, at in ((wg, 0), (wu, 2 * P)):
                        src = w[e, k * P:(k + 1) * P, :].rearrange("p (f n) -> p f n", n=P)
                        sp.dma_start(w_raw[:, lo:hi, at + k * P:at + (k + 1) * P], src[:, lo:hi, :]).then_inc(done, 16)
                sp.dma_start(w_raw[:, lo:hi, 4 * P:], wd[e].rearrange("(f p) n -> p f n", p=P)[:, lo:hi, :])\
                    .then_inc(done, 16)

            def step(s):
                on = stages(s)
                if on["qload"]:
                    o = 1 - LAG
                    wait(sp, o_d, s.t(o - 1))
                    wait(sp, st_q[s.par(o)], (s.half(o) + 1) * 16)
                    sp.dma_start(q_in[s.par(o)][:, :], q_store[s.t(o)]).then_inc(ld_q[s.par(o)], 16)
                if on["xrload"]:
                    o = -LAG
                    wait(sp, x2_d, s.t(o - 1))
                    sp.dma_start(x_re[s.par(o)][:, :], xt[s.t(o)]).then_inc(ld_xr[s.par(o)], 16)
                if on["second"]:
                    o = -LAG - 3
                    wait(sp, h2_d, s.t(o + 1))
                    sp.dma_start(h2_t[s.t(o)], h2[s.par(o)][:, :]).then_inc(st_h2[s.par(o)], 16)
                if on["xload"] and s.rep >= -2:
                    wait(sp, norm1, s.t(3))
                    sp.dma_start(x_in[s.par(4)][:, :], xt[s.t(4)]).then_inc(ld_x[s.par(4)], 16)
                if on["kv"]:
                    wait(sp, qT_d, s.t(-1))
                    sp.dma_start(q_store[s.t(-2)], qT[s.par(-2)][:, :]).then_inc(st_q[s.par(-2)], 16)
                if on["proj"]:
                    o = -LAG - 1
                    wait(sp, x2_d, s.t(o + 1))
                    sp.dma_start(out_t[s.t(o)], x2[s.par(o)][:, :]).then_inc(st_x2[s.par(o)], 16)
                if s.rep == 2:
                    sp.wait_ge(dve_pre, 5)
                    sp.dma_start(mod_store, mod_row[:, :, :]).then_inc(st_mod, 16)
                if s.rep == 3:
                    sp.wait_ge(st_mod, 16)
                    sp.dma_start(mod_all[:, :, :, :].rearrange("p b r d -> p (b r d)"),
                                 mod_store.rearrange("b r d -> (b r d)").partition_broadcast(P)).then_inc(ld_all, 16)
                if s.rep == TB + 2:
                    load_weights(0, 0, raw_a)
                if s.rep == TB + 3:
                    load_weights(0, FC // 2, raw_b)

            steps(sp, step, ATT)

            sp.wait_ge(sp_h, 4)
            sp.wait_ge(sp_l, 4)
            load_weights(1, 0, raw_a)

            def expert(e, last):
                if last >= 1:
                    return
                wait(sp, sp_h, e * FC + FC)
                wait(sp, sp_l, e * FC + FC)
                load_weights(e + 1, FC // 2, raw_b)
                if last == 0:
                    wait(sp, sp_h, e * FC + FC + FC // 2)
                    wait(sp, sp_l, e * FC + FC + FC // 2)
                    load_weights(e + 2, 0, raw_a)

            with sp.Fori(0, (E - 2) // 2) as k:
                expert(k * 2, 0)
                expert(k * 2 + 1, 0)
            expert(E - 2, 0.5)

        @block.gpsimd
        def _(pool):
            pool.dma_start(pad[:, :], rope[0:1, 0:HALF]).then_inc(sc_d, 16)
            nc.gpsimd.memset(half_neg[:, :], -0.5).then_inc(plink_s, 1)
            nc.gpsimd.memset(ones_b[:, :], 1.0).then_inc(plink_s, 1)
            nc.gpsimd.memset(ones_f[:, :], 1.0).then_inc(plink_s, 1)
            nc.gpsimd.memset(zeros[:, :], 0.0).then_inc(plink_s, 1)
            for i in range(2):
                nc.gpsimd.memset(vx[i][:, :, P:P + 1], 1.0).then_inc(plink_s, 1)
            nc.gpsimd.memset(reset[:, :, :], 1.0).then_inc(plink_s, 1)
            pool.wait_ge(plink_s, 7)
            nc.gpsimd.memset(reset[:, :, 0:1], 0.0).then_inc(plink_s, 1)
            nc.gpsimd.affine_select(out=before[:, :], in_=ones_b[:, :], compare_op=ALU.is_gt, fill=0.0, base=0,
                                    pattern=[[1, P]], channel_multiplier=-1).then_inc(plink_s, 1)
            nc.gpsimd.iota(iota_s[:, :], pattern=[[1, P]], base=0, channel_multiplier=0,
                           allow_small_or_imprecise_dtypes=True).then_inc(plink_s, 1)
            nc.gpsimd.iota(rev[:, :], pattern=[[-1, E]], base=E, channel_multiplier=0,
                           allow_small_or_imprecise_dtypes=True).then_inc(plink_s, 1)
            nc.gpsimd.iota(tile_thr[:, :], pattern=[[P, CT + 1]], base=0, channel_multiplier=0,
                           allow_small_or_imprecise_dtypes=True).then_inc(plink_s, 1)
            nc.gpsimd.iota(vals[:, :, :, 0], pattern=[[0, E], [0, NT]], base=0, channel_multiplier=1,
                           allow_small_or_imprecise_dtypes=True).then_inc(plink_s, 1)
            nc.gpsimd.iota(vals[:, :, :, 1], pattern=[[0, E], [1, NT]], base=1, channel_multiplier=0,
                           allow_small_or_imprecise_dtypes=True).then_inc(plink_s, 1)

            def step(s):
                on = stages(s)
                if on["norm"]:
                    wait(pool, stat1, s.t(3))
                    wait(pool, norm1, s.t(2))
                    nc.gpsimd.tensor_tensor(rs1[:, :], ve1[:, :], half_neg[:, :], ALU.pow).then_inc(pow1, 1)
                    pool.wait_ge(pow1, s.t(3))
                    nc.gpsimd.tensor_tensor(sh1[:, :], nm1[:, :], rs1[:, :], ALU.mult).then_inc(scale1, 1)
                if on["scale2"]:
                    o = -LAG - 2
                    wait(pool, stat2, s.t(o + 1))
                    wait(pool, norm2, s.t(o))
                    nc.gpsimd.tensor_tensor(rs2[:, :], ve2[:, :], half_neg[:, :], ALU.pow).then_inc(pow2, 1)
                    pool.wait_ge(pow2, s.t(o + 1))
                    nc.gpsimd.tensor_tensor(sh2[:, :], nm2[:, :], rs2[:, :], ALU.mult).then_inc(scale2, 1)
                if on["second"]:
                    o = -LAG - 3
                    b = (s.rep + o) // TB
                    if s.rep + o == 0:
                        pool.wait_ge(ld_all, 16)
                    wait(pool, norm2, s.t(o + 1))
                    wait(pool, h2_d, s.t(o))
                    nc.gpsimd.tensor_tensor(xm2[:, :], xn2[:, :], mod_all[:, b, 2, :], ALU.mult).then_inc(pm2, 1)
                    pool.wait_ge(pm2, s.t(o + 1))
                    wait(pool, st_h2[s.par(o)], s.half(o) * 16)
                    wait(pool, tr_h2, s.t(o - 1))
                    nc.gpsimd.tensor_tensor(h2[s.par(o)][:, :], xm2[:, :], mod_all[:, b, 1, :], ALU.add)\
                        .then_inc(h2_d, 1)
                if on["qkv"]:
                    wait(pool, rope_m, s.t(1))
                    wait(pool, feat_d, s.t(-1))
                    nc.gpsimd.tensor_tensor(rot[s.par(0)][:, :], rot_a[:, :], rot_b[:, :], ALU.add).then_inc(rope_d, 1)

            steps(pool, step, ATT)

            wT = lambda a: a.rearrange("p n e -> p e n")
            pool.wait_ge(r_dve, 1)
            nc.gpsimd.tensor_copy(w_hi[:, :, :], wgt[:, :, :]).then_inc(r_pool, 1)
            pool.wait_ge(r_pool, 1)
            nc.gpsimd.tensor_tensor(w_r1[:, :, :], wgt[:, :, :], w_hi[:, :, :], ALU.subtract).then_inc(r_pool, 1)
            pool.wait_ge(r_pool, 2)
            nc.gpsimd.tensor_copy(w_mid[:, :, :], w_r1[:, :, :]).then_inc(r_pool, 1)
            pool.wait_ge(r_pool, 3)
            nc.gpsimd.tensor_tensor(w_r2[:, :, :], w_r1[:, :, :], w_mid[:, :, :], ALU.subtract).then_inc(r_pool, 1)
            pool.wait_ge(r_pool, 4)
            nc.gpsimd.tensor_copy(vals[:, :, :, 2], wT(w_hi[:, :, :])).then_inc(r_pool, 1)
            nc.gpsimd.tensor_copy(vals[:, :, :, 3], wT(w_mid[:, :, :])).then_inc(r_pool, 1)
            nc.gpsimd.tensor_copy(vals[:, :, :, 4], wT(w_r2[:, :, :])).then_inc(r_pool, 1)

            def split_low(e, f, count):
                raw = raw_a if f < FC // 2 else raw_b
                wait(pool, raw, (e + 1) * 5 * 16)
                wait(pool, sp_h, count + 1)
                nc.gpsimd.tensor_tensor(w_l[:, f, :], w_raw[:, f, :], w_h[:, f, :].bitcast(F32), ALU.subtract)\
                    .then_inc(sp_l, 1)

            for f in range(FC - 2):
                split_low(0, f, f)

            def gather(rows, dst, idx, done):
                for a in range(CT):
                    nc.gpsimd.indirect_dma_start(
                        out=dst[:, a, :], out_offset=None, in_=rows,
                        in_offset=bass.IndirectOffsetOnAxis(ap=idx[:, a:a + 1], axis=0))\
                        .then_inc(done[a // 2] if isinstance(done, list) else done, 16)

            for i in range(2):
                pool.wait_ge(st_h2[i], NT // 2 * 16)
                pool.wait_ge(st_x2[i], NT // 2 * 16)
            pool.wait_ge(idx_d, 1)
            gather(h2_rows, xg, g_idx[0], ga_d)

            def expert(e, par, last):
                for f in (0, 1):
                    split_low(e, FC - 2 + f, e * FC + FC - 2 + f)
                if last < 1:
                    wait_apart(pool, idx_d, e + 2, apart)
                    wait_apart(pool, trx_d, e * XG + XG, apart)
                    gather(h2_rows, xg, g_idx[1 - par], ga_d)
                wait_apart(pool, sc_d, e * CT * 16 + 16, apart)
                gather(out_rows, xo, g_idx[par], xo_d)
                if last < 1:
                    for f in range(FC - 2):
                        split_low(e + 1, f, e * FC + FC + f)
                for a in range(CT):
                    wait_apart(pool, yo_d, e * CT + a + 1, apart)
                    nc.gpsimd.indirect_dma_start(
                        out=out_rows, out_offset=bass.IndirectOffsetOnAxis(ap=s_idx[par][:, a:a + 1], axis=0),
                        in_=yo[:, a, :], in_offset=None, bounds_check=N - 1, oob_is_err=False).then_inc(sc_d, 16)

            with pool.Fori(0, (E - 2) // 2) as k:
                expert(k * 2, 0, 0)
                expert(k * 2 + 1, 1, 0)
            expert(E - 2, 0, 0.5)
            expert(E - 1, 1, 1)
            pool.wait_ge(sc_d, E * CT * 16 + 16)

        @block.scalar
        def _(act):
            act.wait_ge(ld_c, 32)
            nc.scalar.activation(c_act[:, :], c_sb[:, :], ACT.Silu).then_inc(act_pre, 1)
            act.wait_ge(plink_s, 10)
            nc.scalar.copy(iota_b[:, :, :], iota_s[:, :].unsqueeze(2).to_broadcast([P, P, NT])).then_inc(iota_d, 1)

            def step(s):
                on = stages(s)
                if on["trh"]:
                    b = (s.rep + 1) // TB
                    if s.rep == -1:
                        act.wait_ge(dve_pre, 3)
                    wait(act, tr_h, s.t(2))
                    wait(act, qkv_done, s.t(0))
                    for k in range(KC):
                        ins = nc.scalar.activation(hT[s.par(1)][:, k, :], hT_ps[:, k, :], ACT.Identity,
                                                   bias=mod_col[:, 0, k, b:b + 1], scale=mod_col[:, 1, k, b:b + 1])
                    ins.then_inc(hT_d, 1)
                if on["norm"]:
                    wait(act, scale1, s.t(3))
                    wait(act, tr_h, s.t(2))
                    nc.scalar.activation(hn[:, :], x_in[s.par(2)][:, :], ACT.Identity, bias=sh1[:, :],
                                         scale=rs1[:, :]).then_inc(norm1, 1)
                if on["feat"]:
                    wait(act, rope_d, s.t(0))
                    wait(act, feat_d, s.t(-1))
                    nc.scalar.activation(neg[:, :], rot[s.par(-1)][:, :], ACT.Relu, scale=-1.0).then_inc(neg_d, 1)
                if on["feat"]:
                    wait(act, neg_d, s.t(0))
                    nc.scalar.activation(ex[:, :], neg[:, :], ACT.Exp, scale=-1.0).then_inc(exp_d, 1)
                if on["proj"]:
                    o = -LAG - 1
                    wait(act, tr_o, s.t(o + 1))
                    wait(act, y_d, s.t(o))
                    nc.scalar.copy(attT[:, :], oT_ps).then_inc(oT_d, 1)
                if on["qkv"]:
                    wait(act, qkv_done, s.t(1))
                    wait(act, kv_d, s.t(-1))
                    if s.rep < 2:
                        act.wait_ge(plink_s, 7)
                    nc.scalar.copy(vx[s.par(0)][:, :, 0:P], v_ps.rearrange("p (c n) -> p c n", c=KC)).then_inc(v_done, 1)
                if on["kv"]:
                    wait(act, tr_q, s.t(-1))
                    wait(act, st_q[s.par(-2)], s.half(-2) * 16)
                    nc.scalar.copy(qT[s.par(-2)][:, :], qT_ps).then_inc(qT_d, 1)
                if on["logit"]:
                    o = -LAG - 5
                    wait(act, lg_d, s.t(o + 1))
                    nc.scalar.copy(logits[:, s.t(o), :], lg_ps).then_inc(lgc, 1)
                if on["scale2"]:
                    o = -LAG - 2
                    wait(act, scale2, s.t(o + 1))
                    wait(act, pm2, s.t(o))
                    nc.scalar.activation(xn2[:, :], x2[s.par(o)][:, :], ACT.Identity, bias=sh2[:, :], scale=rs2[:, :])\
                        .then_inc(norm2, 1)
                if on["trh2"]:
                    o = -LAG - 4
                    wait(act, tr_h2, s.t(o + 1))
                    wait(act, lg_d, s.t(o))
                    nc.scalar.copy(h2T[:, :], h2T_ps).then_inc(h2T_d, 1)

            steps(act, step, ATT)

            act.wait_ge(r_act, 1)
            nc.scalar.activation(big[1][:, :, :], big[0][:, :, :], ACT.Exp).then_inc(act_pre, 1)

            def split_high(e, f, count, implied=False):
                raw = raw_a if f < FC // 2 else raw_b
                wait(act, raw, (e + 1) * 5 * 16)
                if not implied:
                    wait(act, dn_d, count - FC + 1)
                nc.scalar.copy(w_h[:, f, :], w_raw[:, f, :]).then_inc(sp_h, 1)

            for f in range(FC - 2):
                split_high(0, f, f)

            def x_high(e, par, g, bk=7):
                n = min(2, CT - 2 * g) * P
                wait(act, trx_d, e * XG + g + 1)
                nc.scalar.copy(xT_h[par][:, :, 2 * g * P:2 * g * P + n],
                               bank[bk][:, 0:2 * n].rearrange("p (c n) -> p c n", c=KC)).then_inc(xh_d, 1)

            for g in range(XG):
                x_high(0, 0, g, bk=g)

            def expert(e, par, last):
                def gate_weight(a):
                    wait(act, wb_d, e + 1)
                    if a:
                        wait(act, gw_d, e * CT + a)
                    nc.scalar.activation(gw0[:, :], mod_all[:, 0, 3, :], ACT.Copy, scale=w_b[par][:, 0, a:a + 1])\
                        .then_inc(gw0_d, 1)

                for f in range(FC):
                    for h in range(2):
                        i = e * 2 * FC + 2 * f + h
                        wait(act, gu_d, i + 1)
                        if f:
                            wait(act, hid_d, i - 1)
                        nc.scalar.activation(act_g[h][:, :], bank[2 * h][:, 0:HCAP], ACT.Silu).then_inc(silu_d, 1)
                        wait(act, hid_d, i + 1)
                        if f >= 2:
                            wait(act, dn_d, e * FC + f - 1)
                        nc.scalar.copy(hid_h[f % 2][:, h * HCAP:(h + 1) * HCAP], hid[h][:, :]).then_inc(hh_d, 1)
                    if last < 1 and XF <= f < XF + XG:
                        x_high(e + 1, 1 - par, f - XF)
                    if f < 2:
                        split_high(e, FC - 2 + f, e * FC + FC - 2 + f, implied=True)
                    elif last < 1:
                        split_high(e + 1, f - 2, e * FC + FC + f - 2)
                    if f < CT:
                        gate_weight(f)

            with act.Fori(0, (E - 2) // 2) as k:
                expert(k * 2, 0, 0)
                expert(k * 2 + 1, 1, 0)
            expert(E - 2, 0, 0.5)
            expert(E - 1, 1, 1)

        @block.vector
        def _(dve):
            chain = [0]

            def link(ins):
                chain[0] += 1
                ins.then_inc(link_s, 1)
                dve.wait_ge(link_s, chain[0])

            V = nc.vector
            dve.wait_ge(pe_pre, 1)
            V.tensor_copy(cT[:, :, :], bank[0][:, 0:KC * B].rearrange("p (c b) -> p c b", c=KC)).then_inc(dve_pre, 1)
            dve.wait_ge(pe_pre, 2)
            V.tensor_copy(mod_col[:, 0, :, :], bank[1][:, 0:KC * B].rearrange("p (c b) -> p c b", c=KC))\
                .then_inc(dve_pre, 1)
            V.tensor_scalar(mod_col[:, 1, :, :], bank[1][:, KC * B:2 * KC * B].rearrange("p (c b) -> p c b", c=KC),
                            1.0, None, ALU.add).then_inc(dve_pre, 1)

            def mod_rows():
                dve.wait_ge(pe_pre, 3)
                V.tensor_copy(routerT[:, :, :], bank[6][:, 0:KC * E].rearrange("p (c e) -> p c e", c=KC))
                V.tensor_copy(mod_row[:, 1, :], row_ps[0][:, D:])
                V.tensor_scalar(mod_row[:, 2, :], row_ps[1][:, 0:D], 1.0, None, ALU.add)
                for i, g in enumerate((row_ps[0][:, 0:D], row_ps[1][:, D:])):
                    V.tensor_scalar(gate_sgn[:, i, :], g, 0.0, 2.0, ALU.is_ge, ALU.mult)
                    link(V.tensor_scalar(gate_mag[:, i, :], g, -1.0, None, ALU.mult))
                    link(V.tensor_tensor(gate_mag[:, i, :], g, gate_mag[:, i, :], ALU.max))
                link(V.tensor_scalar(gate_mag[:, :, :], gate_mag[:, :, :], GATE_MIN, None, ALU.max))
                V.scalar_tensor_tensor(mod_row[:, 0:4:3, :], gate_sgn[:, :, :], -1.0, gate_mag[:, :, :],
                                       ALU.add, ALU.mult).then_inc(dve_pre, 1)
                V.tensor_copy(same_e[:, :], same_f)

            def gate_wout(b):
                dve.wait_ge(ld_all, 16)
                V.tensor_tensor(wout_g[b][:, :, :], wout_sb[:, :, :],
                                mod_all[:, b, 0, :].unsqueeze(1).to_broadcast([P, KC, D]), ALU.mult).then_inc(dve_pre, 1)

            def stats(src, st, mv, nm, ve, bn, ag, done, count):
                V.bn_stats(st[:, :], src).then_inc(bn, 1)
                wait_apart(dve, bn, count, apart)
                V.bn_aggr(mv[:, :], st[:, :]).then_inc(ag, 1)
                dve.wait_ge(ag, count)
                V.tensor_scalar(nm[:, :], mv[:, 0:1], -1.0, None, ALU.mult)
                V.tensor_scalar(ve[:, :], mv[:, 1:2], LN_EPS, None, ALU.add).then_inc(done, 1)

            def step(s):
                on = stages(s)
                if s.rep == -1:
                    dve.wait_ge(ld_w, 16)
                    V.tensor_scalar(wqkv_sb[:, :, 0:D], wqkv_sb[:, :, 0:D], float(HD) ** -0.5, None, ALU.mult)\
                        .then_inc(dve_pre, 1)
                if s.rep == 2:
                    mod_rows()
                if s.rep in (TB - 2, TB - 1):
                    gate_wout(s.rep - TB + 2)
                if on["qkv"]:
                    if s.rep == 0:
                        dve.wait_ge(ld_const, 16)
                    cs = rope_sb[:, s.t(-(s.rep // TB) * TB), :]
                    wait(dve, qk_done, s.t(1))
                    wait(dve, rope_d, s.t(0))
                    g = 2 * D // HALF
                    V.tensor_tensor(rot_a[:, :].rearrange("p (g d) -> p g d", d=HALF),
                                    qk_ps.rearrange("p (g d) -> p g d", d=HALF),
                                    cs[:, 0:HALF].unsqueeze(1).to_broadcast([P, g, HALF]), ALU.mult)
                    qv = qk_ps.rearrange("p (g a d) -> p g a d", a=2, d=HALF)
                    rv = rot_b[:, :].rearrange("p (g a d) -> p g a d", a=2, d=HALF)
                    V.tensor_tensor(rv[:, :, 0, :], qv[:, :, 1, :],
                                    cs[:, 2 * HALF:].unsqueeze(1).to_broadcast([P, g // 2, HALF]), ALU.mult)
                    V.tensor_tensor(rv[:, :, 1, :], qv[:, :, 0, :],
                                    cs[:, HALF:2 * HALF].unsqueeze(1).to_broadcast([P, g // 2, HALF]), ALU.mult)\
                        .then_inc(rope_m, 1)
                if on["feat"]:
                    wait(dve, exp_d, s.t(0))
                    wait(dve, tr_q, s.t(-1))
                    wait(dve, kv_d, s.t(-1))
                    V.scalar_tensor_tensor(feat[:, :], rot[s.par(-1)][:, :], 0.0, ex[:, :], ALU.max, ALU.add).then_inc(feat_d, 1)
                if on["att"]:
                    o = -LAG
                    wait(dve, o_d, s.t(o + 1))
                    V.tensor_scalar(den_m[:, :, :], o_ps[:, :, P:], DEN_EPS, None, ALU.max).then_inc(dmax, 1)
                    dve.wait_ge(dmax, s.t(o + 1))
                    V.reciprocal(den_r[:, :, :], den_m[:, :, :]).then_inc(drec, 1)
                    dve.wait_ge(drec, s.t(o + 1))
                    wait(dve, tr_o, s.t(o))
                    V.tensor_tensor(att[:, :].rearrange("p (c h d) -> p c h d", c=KC, d=HD),
                                    o_ps[:, :, 0:P].rearrange("p c (h d) -> p c h d", d=HD),
                                    den_r[:, :, :].unsqueeze(3).to_broadcast([P, KC, HC, HD]), ALU.mult)\
                        .then_inc(att_d, 1)
                if on["stats"]:
                    wait(dve, ld_x[s.par(3)], (s.half(3) + 1) * 16)
                    wait(dve, scale1, s.t(3))
                    stats(x_in[s.par(3)][:, :], st1, mv1, nm1, ve1, bn1, ag1, stat1, s.t(4))
                if on["proj"]:
                    o = -LAG - 1
                    wait(dve, y_d, s.t(o + 1))
                    wait(dve, ld_xr[s.par(o)], (s.half(o) + 1) * 16)
                    wait(dve, st_x2[s.par(o)], s.half(o) * 16)
                    wait(dve, norm2, s.t(o - 1))
                    V.tensor_tensor(x2[s.par(o)][:, :], y_ps, x_re[s.par(o)][:, :], ALU.add).then_inc(x2_d, 1)
                    dve.wait_ge(x2_d, s.t(o + 1))
                    wait(dve, scale2, s.t(o))
                    stats(x2[s.par(o)][:, :], st2, mv2, nm2, ve2, bn2, ag2, stat2, s.t(o + 1))
                if s.rep in (TB + 1, NT + 1):
                    b = s.rep // TB - 1
                    dve.wait_ge(kv_d, s.rep - 1)
                    V.tensor_tensor(kvb[b][:, :, 0:P], kv_ps[:, :, 0:P],
                                    blk[:, 0:P].unsqueeze(1).to_broadcast([P, KC, P]), ALU.mult)
                    V.tensor_tensor(kvb[b][:, :, P:], kv_ps[:, :, P:P + 1].to_broadcast([P, KC, HC]),
                                    blk[:, P:].unsqueeze(1).to_broadcast([P, KC, HC]), ALU.mult).then_inc(kvb_d, 1)

            steps(dve, step, ATT)

            b8 = lambda a: a.unsqueeze(2).to_broadcast([P, NT, E])
            rev_b = rev[:, :].unsqueeze(1).to_broadcast([P, NT, E])
            X = [t[:, :, :] for t in big]
            Y = [t[:, :] for t in small]
            TT, RED = V.tensor_tensor, V.tensor_reduce
            for i in range(TOP_BIT + 2):
                V.memset(bits[:, i, :], 1 << (TOP_BIT - i) if i <= TOP_BIT else 0)
            dve.wait_ge(lgc, NT)
            dve.wait_ge(plink_s, 13)
            dve.wait_ge(iota_d, 1)
            link(RED(Y[0], logits[:, :, :], AX, ALU.max))
            TT(X[0], logits[:, :, :], b8(Y[0]), ALU.subtract).then_inc(r_act, 1)
            dve.wait_ge(act_pre, 2)
            link(RED(Y[1], X[1], AX, ALU.add))
            link(V.reciprocal(Y[2], Y[1]))
            link(TT(X[2], X[1], b8(Y[2]), ALU.mult))
            tops = []
            prob = X[2]
            for i in range(TOPK):
                m, first, hot, q = Y[3 + i], Y[5 + i], X[3 + i], X[5]
                link(RED(m, prob, AX, ALU.max))
                link(TT(q, prob, b8(m), ALU.is_equal))
                link(TT(q, q, rev_b, ALU.mult))
                link(RED(first, q, AX, ALU.max))
                link(TT(hot, q, b8(first), ALU.is_equal))
                tops.append((m, hot))
                if i == 0:
                    link(V.scalar_tensor_tensor(X[6], hot, -2.0, prob, ALU.mult, ALU.add))
                    prob = X[6]
            link(TT(Y[0], Y[3], Y[4], ALU.add))
            link(V.tensor_scalar(Y[0], Y[0], TOPW_EPS, None, ALU.add))
            link(V.reciprocal(Y[1], Y[0]))
            TT(Y[5], Y[3], Y[1], ALU.mult)
            link(TT(Y[6], Y[4], Y[1], ALU.mult))
            TT(X[0], X[3], b8(Y[5]), ALU.mult)
            TT(X[1], X[4], b8(Y[6]), ALU.mult)
            link(TT(X[7], X[3], X[4], ALU.add))
            link(TT(wgt[:, :, :], X[0], X[1], ALU.add))
            V.tensor_scalar(X[5], X[7], -1.0, None, ALU.add).then_inc(r_dve, 1)
            dve.wait_ge(r_dve, 1)
            TT(val[:, :, :], wgt[:, :, :], X[5], ALU.add).then_inc(r_dve, 1)
            V.memset(thr[:, :], 0)
            V.memset(won[:, :], 0)
            link(V.memset(cand[:, :], 1 << TOP_BIT))
            dve.wait_ge(r_pe, 1)
            link(V.tensor_copy(valT[:, :], bank[0][:, 0:2 * P]))
            with dve.Fori(0, (TOP_BIT + 1) // SEARCH) as i:
                for j in range(SEARCH):
                    n = i * SEARCH + j
                    V.tensor_scalar(hit[:, :], valT[:, :], cand[:, :].bitcast(F32), 0.0, ALU.is_ge, ALU.add,
                                    accum_out=cnt[:, :]).then_inc(cnt_d, 1)
                    TT(thr[:, :], thr[:, :], won[:, :], ALU.bitwise_or).then_inc(thr_d, 1)
                    dve.wait_ge(thr_d, n + 1)
                    TT(base[:, :], thr[:, :], bits[:, n + 1, :], ALU.bitwise_or).then_inc(base_d, 1)
                    dve.wait_ge(tot_d, n + 1)
                    V.scalar_tensor_tensor(won[:, :], bank[1][:, 0:1], float(CAP), bits[:, n, :],
                                           ALU.is_ge, ALU.mult).then_inc(won_d, 1)
                    dve.wait_ge(base_d, n + 1)
                    dve.wait_ge(won_d, n + 1)
                    TT(cand[:, :], base[:, :], won[:, :], ALU.bitwise_or).then_inc(cand_d, 1)
                    dve.wait_ge(cand_d, n + 1)
            link(TT(thr[:, :], thr[:, :], won[:, :], ALU.bitwise_or))
            V.tensor_scalar(thr_sel[:, :], sel_e[:, :], thr[:, :].bitcast(F32), None, ALU.mult).then_inc(r_dve, 1)
            dve.wait_ge(r_pe, 2)
            link(V.tensor_copy(thr_b[:, :], bank[2][:, 0:E]))
            tb = thr_b[:, :].unsqueeze(1).to_broadcast([P, NT, E])
            TT(mask2[:, 0, :, :].rearrange("p e n -> p n e"), val[:, :, :], tb, ALU.is_gt)
            TT(mask2[:, 1, :, :].rearrange("p e n -> p n e"), val[:, :, :], tb, ALU.is_equal).then_inc(r_dve, 1)
            dve.wait_ge(r_pe, 3)
            tot = bank[4][:, :]
            m2 = lambda a: a.rearrange("p k e n -> p (k e n)")
            link(V.tensor_tensor_scan(m2(run[:, :, :, :]), reset[:, :, :].rearrange("p g n -> p (g n)"), tot, 0.0,
                                      ALU.mult, ALU.add))
            V.tensor_scalar(need[:, :], run[:, 0, :, NT - 1], -1.0, float(CAP), ALU.mult, ALU.add)
            link(TT(m2(pre[:, :, :, :]), m2(run[:, :, :, :]), tot, ALU.subtract))
            link(TT(m2(pre[:, :, :, :]), m2(pre[:, :, :, :]), bank[3][:, :], ALU.add))
            need_b = need[:, :].unsqueeze(2).to_broadcast([P, E, NT])
            TT(tmp_s[:, :, :], pre[:, 1, :, :], need_b, ALU.is_lt)
            link(TT(slot[:, :, :], pre[:, 1, :, :], need_b, ALU.min))
            link(TT(tmp_s[:, :, :], tmp_s[:, :, :], mask2[:, 1, :, :], ALU.mult))
            TT(keep[:, :, :], tmp_s[:, :, :], mask2[:, 0, :, :], ALU.add)
            link(TT(slot[:, :, :], slot[:, :, :], pre[:, 0, :, :], ALU.add))
            link(V.scalar_tensor_tensor(keep[:, :, :], slot[:, :, :], float(CAP), keep[:, :, :], ALU.is_lt, ALU.mult))
            link(V.scalar_tensor_tensor(slot[:, :, :], slot[:, :, :], 1.0, keep[:, :, :], ALU.add, ALU.mult))
            V.tensor_scalar(slot[:, :, :], slot[:, :, :], -1.0, None, ALU.add).then_inc(slots_d, 1)
            dve.wait_ge(slots_d, 1)
            dve.wait_ge(r_pool, 7)

            def describe_tiles(e):
                sl = slot[:, e, :]
                TT(tile_ge[:, :, :], sl.unsqueeze(2).to_broadcast([P, NT, CT + 1]),
                   tile_thr[:, :].unsqueeze(1).to_broadcast([P, NT, CT + 1]), ALU.is_ge).then_inc(ge_d, 1)
                dve.wait_ge(ge_d, e + 1)
                RED(tile_no[:, :], tile_ge[:, :, 1:], AX, ALU.add).then_inc(tn_d, 1)
                TT(in_tile[:, :, :], tile_ge[:, :, 0:CT], tile_ge[:, :, 1:], ALU.subtract).then_inc(in_d, 1)
                dve.wait_ge(tn_d, e + 1)
                V.scalar_tensor_tensor(row_in[:, :], tile_no[:, :], -float(P), sl, ALU.mult, ALU.add).then_inc(ri_d, 1)

            def describe_facts(e, part):
                sl = slice(part * NT // 2, (part + 1) * NT // 2)
                if part == 0:
                    wait(dve, look_d, e)
                    dve.wait_ge(in_d, e + 1)
                TT(facts[:, sl, :, :], vals[:, e, sl, :].unsqueeze(3).to_broadcast([P, NT // 2, NV, CT]),
                   in_tile[:, sl, :].unsqueeze(2).to_broadcast([P, NT // 2, NV, CT]), ALU.mult)

            def describe_rows(e, part):
                if part == 0:
                    dve.wait_ge(ri_d, e + 1)
                sl = slice(part * P // 4, (part + 1) * P // 4)
                TT(onehot[:, sl, :], iota_b[:, sl, :], row_in[:, :].unsqueeze(1).to_broadcast([P, P // 4, NT]),
                   ALU.is_equal).then_inc(facts_d, 1)

            def describe(e):
                describe_tiles(e)
                for part in range(2):
                    describe_facts(e, part)
                for part in range(4):
                    describe_rows(e, part)

            def chained(sem, base):
                n = [0]

                def lk(ins):
                    n[0] += 1
                    ins.then_inc(sem, 1)
                    dve.wait_ge(sem, base + n[0])
                return lk

            def find_tokens(e, par):
                lk = chained(fin_l, e * 3)
                dve.wait_ge(look_d, e + 1)
                V.tensor_copy(got[:, :, :], bank[7][:, 0:NV * CT].rearrange("p (v a) -> p v a", v=NV))\
                    .then_inc(got_d, 1)
                dve.wait_ge(got_d, e + 1)
                lk(V.scalar_tensor_tensor(tok[:, :], got[:, 1, :], float(P), got[:, 0, :], ALU.mult, ALU.add))
                V.tensor_scalar(far[:, :], got[:, 1, :], 0.5, float(FAR), ALU.is_lt, ALU.mult)
                lk(V.tensor_scalar(tok[:, :], tok[:, :], -float(P), 0.0, ALU.add, ALU.max))
                if not isinstance(e, int) or e > 1:
                    wait(dve, sc_d, (e - 1) * CT * 16 + 16)
                lk(V.tensor_copy(g_idx[par][:, :], tok[:, :]))
                V.tensor_tensor(s_idx[par][:, :], tok[:, :], far[:, :], ALU.add).then_inc(idx_d, 1)

            def find_weights(e, par):
                lk = chained(wb_l, e * 3)
                lk(TT(w_slot[:, 0, :], got[:, 2, :], got[:, 3, :], ALU.add))
                V.tensor_scalar(w_slot[:, 2, :], got[:, 1, :], float(TB) + 0.5, None, ALU.is_ge)
                lk(TT(w_slot[:, 1, :], w_slot[:, 0, :], got[:, 4, :], ALU.add))
                lk(TT(w_b[par][:, 1, :], w_slot[:, 2, :], w_slot[:, 1, :], ALU.mult))
                TT(w_b[par][:, 0, :], w_slot[:, 1, :], w_b[par][:, 1, :], ALU.subtract).then_inc(wb_d, 1)

            dve.sem_inc(ym_d, 1)
            describe(0)
            find_tokens(0, 0)
            find_weights(0, 0)
            describe(1)

            def x_low(e, par, g, bk=7):
                n = min(2, CT - 2 * g) * P
                wait(dve, xh_d, e * XG + g + 1)
                sl = slice(2 * g * P, 2 * g * P + n)
                V.tensor_tensor(xT_l[par][:, :, sl], bank[bk][:, 0:2 * n].rearrange("p (c n) -> p c n", c=KC),
                                xT_h[par][:, :, sl].bitcast(F32), ALU.subtract).then_inc(xl_d, 1)

            for g in range(XG):
                x_low(0, 0, g, bk=g)

            def weigh(e):
                wait(dve, sc_d, e * CT * 16 + 16)
                for a in range(CT):
                    if a == CT - 1:
                        wait(dve, dn_d, (e + 1) * FC)
                    elif a % 2 == 0:
                        wait(dve, y_tile, e * (CT // 2) + a // 2 + 1)
                    V.tensor_tensor(yo[:, a, :], bank[4 + a // 2][:, a % 2 * D:(a % 2 + 1) * D], gw[:, a, :], ALU.mult)\
                        .then_inc(ym_d, 1)

            def combine(e, lo, hi):
                wait(dve, xo_d, (e + 1) * CT * 16)
                for a in range(lo, hi):
                    wait(dve, ym_d, e * CT + a + 2)
                    V.tensor_tensor(yo[:, a, :], yo[:, a, :], xo[:, a, :], ALU.add).then_inc(yo_d, 1)

            def expert(e, par, first=False, last=False, ahead=True):
                if not first:
                    weigh(e - 1)
                for f in range(FC):
                    for h in range(2):
                        i = e * 2 * FC + 2 * f + h
                        wait(dve, silu_d, i + 1)
                        if f:
                            wait(dve, hh_d, i - 1)
                        V.tensor_tensor(hid[h][:, :], act_g[h][:, :], bank[2 * h + 1][:, 0:HCAP], ALU.mult)\
                            .then_inc(hid_d, 1)
                        wait(dve, hh_d, i + 1)
                        V.tensor_tensor(hid_l[f % 2][:, h * HCAP:(h + 1) * HCAP], hid[h][:, :],
                                        hid_h[f % 2][:, h * HCAP:(h + 1) * HCAP].bitcast(F32), ALU.subtract)\
                            .then_inc(hl_d, 1)
                        if f == 0 and not first:
                            combine(e - 1, h * 2, (2, CT)[h])
                    if not last and XF <= f < XF + XG:
                        x_low(e + 1, 1 - par, f - XF)
                    if f < CT:
                        wait(dve, gw0_d, e * CT + f + 1)
                        V.scalar_tensor_tensor(gw[:, f, :], mod_all[:, 1, 3, :], w_b[par][:, 1, f:f + 1], gw0[:, :],
                                               ALU.mult, ALU.add).then_inc(gw_d, 1)
                    if f == 1 and not last:
                        find_tokens(e + 1, 1 - par)
                    if f == 3 and not last:
                        find_weights(e + 1, 1 - par)
                    if ahead:
                        if f == 2:
                            describe_tiles(e + 2)
                        if f in (2, 3):
                            describe_facts(e + 2, f - 2)
                        if 4 <= f < 7:
                            describe_rows(e + 2, f - 4)
                        if f == 6:
                            describe_rows(e + 2, 3)
            expert(0, 0, first=True)
            with dve.Fori(0, (E - 4) // 2) as k:
                expert(k * 2 + 1, 1)
                expert(k * 2 + 2, 0)
            for e in range(E - 3, E):
                expert(e, e % 2, last=e == E - 1, ahead=e + 2 < E)
            weigh(E - 1)
            combine(E - 1, 0, CT)

        @block.tensor
        def _(pe):
            MM = nc.tensor.matmul
            TR = nc.tensor.transpose
            pe.wait_ge(act_pre, 1)
            for k in range(KC):
                last = TR(bank[0][:, k * B:(k + 1) * B], c_act[:, k * P:(k + 1) * P], ident[0:B, 0:B])
            last.then_inc(pe_pre, 1)
            pe.wait_ge(dve_pre, 1)
            pe.wait_ge(ld_mod, 16)
            for i in range(2):
                for m in range(KC):
                    for k in range(KC):
                        at = i * D + m * P
                        last = MM(bank[1][:, (i * KC + m) * B:(i * KC + m + 1) * B], wmod_sb[:, k, at:at + P],
                                  cT[:, k, :], start=k == 0, stop=k == KC - 1)
            last.then_inc(pe_pre, 1)

            def mod_rows():
                pe.wait_ge(ld_rest, 48)
                for i in range(2):
                    for k in range(KC):
                        at = 2 * D + i * 2 * D
                        MM(row_ps[i], cT[:, k, :], wmod_sb[:, k, at:at + 2 * D], start=k == 0, stop=k == KC - 1)
                for k in range(KC):
                    last = TR(bank[6][:, k * E:(k + 1) * E], router_sb[:, k * P:(k + 1) * P], ident[0:E, 0:E])
                last.then_inc(pe_pre, 1)

            def step(s):
                on = stages(s)
                if on["trh"]:
                    wait(pe, norm1, s.t(2))
                    wait(pe, hT_d, s.t(1))
                    for k in range(KC):
                        last = TR(hT_ps[:, k, :], hn[:, k * P:(k + 1) * P], ident[:, :])
                    last.then_inc(tr_h, 1)
                if on["qkv"]:
                    if s.rep == 0:
                        pe.wait_ge(dve_pre, 4)
                    wait(pe, hT_d, s.t(1))
                    wait(pe, rope_m, s.t(0))
                    for k in range(KC):
                        last = MM(qk_ps, hT[s.par(0)][:, k, :], wqkv_sb[:, k, 0:2 * D], start=k == 0, stop=k == KC - 1)
                    last.then_inc(qk_done, 1)
                    wait(pe, v_done, s.t(0))
                    for k in range(KC):
                        last = MM(v_ps, hT[s.par(0)][:, k, :], wqkv_sb[:, k, 2 * D:], start=k == 0, stop=k == KC - 1)
                    last.then_inc(qkv_done, 1)
                if on["kv"]:
                    wait(pe, feat_d, s.t(-1))
                    wait(pe, qT_d, s.t(-2))
                    for k in range(KC):
                        last = TR(qT_ps[:, k * P:(k + 1) * P], feat[:, k * P:(k + 1) * P], ident[:, :])
                    last.then_inc(tr_q, 1)
                    wait(pe, v_done, s.t(-1))
                    if (s.rep - 2) % TB == 0:
                        if s.rep == 2:
                            pe.wait_ge(plink_s, 4)
                        else:
                            pe.wait_ge(kvb_d, 1)
                        MM(bank[3][:, :], zeros[0:1, 0:P], zeros[0:1, :], start=True, stop=False, skip_group_check=True)
                    for k in range(KC):
                        last = MM(kv_ps[:, k, :], feat[:, D + k * P:D + (k + 1) * P], vx[s.par(-2)][:, k, :],
                                  start=False, stop=False, skip_group_check=True)
                    last.then_inc(kv_d, 1)
                if s.rep == 1:
                    mod_rows()
                if on["proj"]:
                    o = -LAG - 1
                    wait(pe, att_d, s.t(o + 1))
                    wait(pe, x2_d, s.t(o))
                    for k in range(KC):
                        last = TR(oT_ps[:, k * P:(k + 1) * P], att[:, k * P:(k + 1) * P], ident[:, :])
                    last.then_inc(tr_o, 1)
                if on["att"]:
                    o = -LAG
                    b = (s.rep + o) // TB
                    if s.rep == LAG:
                        pe.wait_ge(dve_pre, 5)
                    if s.rep in (LAG, NT + 2):
                        pe.wait_ge(kvb_d, b + 1)
                    wait(pe, ld_q[s.par(o)], (s.half(o) + 1) * 16)
                    wait(pe, att_d, s.t(o))
                    for k in range(KC):
                        last = MM(o_ps[:, k, :], q_in[s.par(o)][:, k * P:(k + 1) * P], kvb[b][:, k, :],
                                  start=True, stop=True)
                    last.then_inc(o_d, 1)
                if on["logit"]:
                    o = -LAG - 5
                    wait(pe, h2T_d, s.t(o + 1))
                    for k in range(KC):
                        last = MM(lg_ps, h2T[:, k * P:(k + 1) * P], routerT[:, k, :], start=k == 0, stop=k == KC - 1)
                    last.then_inc(lg_d, 1)
                if on["proj"]:
                    o = -LAG - 1
                    b = (s.rep + o) // TB
                    wait(pe, oT_d, s.t(o + 1))
                    if s.rep == LAG + 1:
                        pe.wait_ge(dve_pre, 7)
                    for k in range(KC):
                        last = MM(y_ps, attT[:, k * P:(k + 1) * P], wout_g[b][:, k, :], start=k == 0, stop=k == KC - 1)
                    last.then_inc(y_d, 1)
                if on["trh2"]:
                    o = -LAG - 4
                    if s.rep + o == 0:
                        pe.wait_ge(dve_pre, 5)
                    wait(pe, h2_d, s.t(o + 1))
                    wait(pe, h2T_d, s.t(o))
                    if on["logit"]:
                        wait(pe, lgc, s.t(o))
                    for k in range(KC):
                        last = TR(h2T_ps[:, k * P:(k + 1) * P], h2[s.par(o)][:, k * P:(k + 1) * P], ident[:, :])
                    last.then_inc(tr_h2, 1)

            steps(pe, step, ATT)

            pe.wait_ge(r_dve, 2)
            flat = val[:, :, :].rearrange("p n e -> p (n e)")
            for k in range(2):
                last = TR(bank[0][:, k * P:(k + 1) * P], flat[:, k * P:(k + 1) * P], ident[:, :])
            last.then_inc(r_pe, 1)
            with pe.Fori(0, (TOP_BIT + 1) // SEARCH) as i:
                for j in range(SEARCH):
                    pe.wait_ge(cnt_d, i * SEARCH + j + 1)
                    MM(bank[1][:, 0:1], same_e[:, :], cnt[:, :], start=True, stop=True).then_inc(tot_d, 1)
            pe.wait_ge(r_dve, 3)
            MM(bank[2][:, 0:E], ones_f[:, :], thr_sel[:, :], start=True, stop=True).then_inc(r_pe, 1)
            pe.wait_ge(r_dve, 4)
            masks = mask2[:, :, :, :].rearrange("p k e n -> p (k e n)")
            MM(bank[3][:, :], before[:, :], masks, start=True, stop=True)
            MM(bank[4][:, :], ones_b[:, :], masks, start=True, stop=True).then_inc(r_pe, 1)

            def look(e):
                wait(pe, facts_d, e * 4 + 4)
                for n in range(NT):
                    last = MM(bank[7][:, 0:NV * CT], onehot[:, :, n], facts[:, n, :, :].rearrange("p v a -> p (v a)"),
                              start=n == 0, stop=n == NT - 1)
                last.then_inc(look_d, 1)

            def transpose_x(e, g, first=False):
                tiles = range(2 * g, min(2 * g + 2, CT))
                wait(pe, ga_d[g], (e + 1) * len(tiles) * 16)
                if not first:
                    wait(pe, xl_d, e * XG + g)
                    wait(pe, got_d, e + 1)
                for k in range(KC):
                    for j, a in enumerate(tiles):
                        at = (k * len(tiles) + j) * P
                        last = TR(bank[g if first else 7][:, at:at + P], xg[:, a, k * P:(k + 1) * P], ident[:, :])
                last.then_inc(trx_d, 1)

            PASSES = ((0, 0), (0, 1), (1, 0))

            look(0)
            wait(pe, got_d, 1)
            look(1)
            for g in range(XG):
                transpose_x(0, g, first=True)

            def expert(e, par, last_e):
                W, XT = (w_h, w_l), (xT_h[par], xT_l[par])

                def gate_up(f):
                    wait(pe, sp_l, e * FC + f + 1)
                    if f == 0:
                        wait(pe, xl_d, e * XG + XG)
                    for h in range(2):
                        if f:
                            wait(pe, hid_d, e * 2 * FC + 2 * f + h - 1)
                        cols = slice(h * HCAP, (h + 1) * HCAP)
                        for m in range(2):
                            n = 0
                            for k in range(KC):
                                for i, j in PASSES:
                                    at = (2 * m + k) * P
                                    last = MM(bank[2 * h + m][:, 0:HCAP], W[i][:, f, at:at + P], XT[j][:, k, cols],
                                              start=n == 0, stop=n == 3 * KC - 1)
                                    n += 1
                        last.then_inc(gu_d, 1)

                def down(f):
                    wait(pe, hh_d, e * 2 * FC + 2 * f + 2)
                    wait(pe, hl_d, e * 2 * FC + 2 * f + 2)
                    if f == 0:
                        wait(pe, ym_d, e * CT + 1)
                    for a in range(CT):
                        for n, (i, j) in enumerate(PASSES):
                            last = MM(bank[4 + a // 2][:, a % 2 * D:(a % 2 + 1) * D],
                                      (hid_h, hid_l)[j][f % 2][:, a * P:(a + 1) * P], W[i][:, f, 4 * P:],
                                      start=f == 0 and n == 0 and a % 2 == 0, stop=f == FC - 1 and n == 2,
                                      skip_group_check=True)
                        if f == FC - 1 and a % 2 == 1:
                            last.then_inc(y_tile, 1)
                    last.then_inc(dn_d, 1)

                gate_up(0)
                for f in range(1, FC):
                    gate_up(f)
                    if last_e < 1 and XF <= f < XF + XG:
                        transpose_x(e + 1, f - XF)
                    down(f - 1)
                if last_e == 0:
                    wait(pe, xl_d, e * XG + 2 * XG)
                    look(e + 2)
                down(FC - 1)

            with pe.Fori(0, (E - 2) // 2) as k:
                expert(k * 2, 0, 0)
                expert(k * 2 + 1, 1, 0)
            expert(E - 2, 0, 0.5)
            expert(E - 1, 1, 1)


def kernel(L0_attn_x, L0_attn_W_qkv, L0_attn_W_out, L0_ffn_router_w, L0_ffn_wg, L0_ffn_wu, L0_ffn_wd, L0_c, L0_wmod):
    import numpy as np
    from concourse import bacc
    from concourse.bass_utils import run_bass_kernel_spmd

    nc = bacc.Bacc("TRN2", target_bir_lowering=False, num_devices=1)
    inv = (1.0 / np.float32(500000.0) ** (np.arange(0, HD, 2, dtype=np.float32) / np.float32(HD))).astype(np.float32)
    ang = np.arange(T, dtype=np.float32)[:, None] * inv[None, :]
    rope = np.concatenate([np.cos(ang), np.sin(ang), -np.sin(ang)], axis=1).astype(np.float32)
    row = np.arange(P)
    consts = np.concatenate([
        row[:, None] == row[None, :],
        row[:, None] // HD == row[None, :] // HD,
        row[:, None] // HD == np.arange(HC)[None, :],
        row[:, None] == np.arange(E)[None, :],
        row[:, None] % E == row[None, :] % E,
    ], axis=1).astype(np.float32)
    arrays = {
        "x": L0_attn_x, "w_qkv": L0_attn_W_qkv, "w_out": L0_attn_W_out, "router": L0_ffn_router_w, "wg": L0_ffn_wg,
        "wu": L0_ffn_wu, "wd": L0_ffn_wd, "c": L0_c, "wmod": L0_wmod, "rope": rope, "consts": consts,
    }
    arrays = {n: np.ascontiguousarray(a) for n, a in arrays.items()}
    aps = {n: nc.dram_tensor(n, a.shape, mybir.dt.from_np(a.dtype), kind="ExternalInput").ap()
           for n, a in arrays.items()}
    out = nc.dram_tensor("out", (B, T, D), F32, kind="ExternalOutput").ap()
    build_program(nc, out=out, **aps)
    result = run_bass_kernel_spmd(nc, [arrays], core_ids=[0])
    return result.results[0]["out"]
```

```python
from contextlib import ExitStack

import concourse.bass as bass
from concourse import mybir

P = 128
F32, F32R = mybir.dt.float32, mybir.dt.float32r
BF16, I32 = mybir.dt.bfloat16, mybir.dt.int32
ALU = mybir.AluOpType
ACT = mybir.ActivationFunctionType
AX = mybir.AxisListType.X

B, T, D = 2, 2048, 256
H, HD = 16, 16
HALF = HD // 2
N = B * T
NT = N // P
TB = NT // B
KC = D // P
HC = H // KC
E, TOPK, F = 8, 2, 1024
CAP = int(1.25 * N / E)
CT = CAP // P
XG = -(-CT // 2)
FC = F // P
HCAP = CAP // 2
WEIGHT_LOADS = 2 * KC + 1
WU = 5 * P + P
LAG = TB + 2
LN_EPS, DEN_EPS, TOPW_EPS, GATE_MIN = 1e-5, 1e-6, 1e-6, 0.25
TOP_BIT = 29
PLACES = ((0, 2), (2, E))
EARLY = NT - 6
DIGITS = (TOP_BIT + 1) // 2
SEARCH = 5
NV = 5
XF = 4
FAR = 1 << 20


class Step:

    def __init__(self, k, j, rep):
        self.k, self.j, self.rep = k, j, rep

    def t(self, off):
        return self.k * 2 + (self.j + off)

    def par(self, off):
        return (self.j + off) % 2

    def half(self, off):
        return self.k + (self.j + off) // 2


def wait(eng, sem, value):
    if isinstance(value, int) and value <= 0:
        return
    assert isinstance(value, int) or bass.sinput_min_value(value) > 0
    eng.wait_ge(sem, value)


def wait_apart(eng, sem, value, apart):
    wait(eng, sem, value)
    eng.sem_inc(apart, 1)


def steps(eng, emit, segments):
    for lo, hi, looped in segments:
        if looped:
            with eng.Fori(lo // 2, hi // 2) as k:
                emit(Step(k, 0, lo))
                emit(Step(k, 1, lo + 1))
        else:
            for s in range(lo, hi):
                emit(Step(s // 2, s % 2, s))


ATT = [(-3, 4, False), (4, TB - 2, True), (TB - 2, TB + 8, False), (TB + 8, NT - 4, True),
       (NT - 4, NT + 6, False), (NT + 6, NT + TB, True), (NT + TB, NT + TB + 7, False)]


def spared(s):
    return 2 <= s.rep < TB


def alone(s):
    return s.rep >= NT + 6


def stages(s):
    r = s.rep
    u = r - LAG
    on = lambda t: 0 <= t < NT
    return dict(xload=on(r + 4), stats=on(r + 3), norm=on(r + 2), trh=on(r + 1), qkv=on(r), feat=on(r - 1),
                kv=on(r - 2), qstore=on(r - 3),
                qload=on(u + 1), xrload=on(u), att=on(u), proj=on(u - 1), scale2=on(u - 2), second=on(u - 3),
                trh2=on(u - 4), logit=on(u - 5))


def build_program(nc, x, w_qkv, w_out, router, wg, wu, wd, c, wmod, rope, consts, out):
    xt = x.rearrange("b (n p) d -> (b n) p d", p=P)
    out_rows = out.rearrange("b t d -> (b t) d")
    out_t = out_rows.rearrange("(n p) d -> n p d", p=P)
    h2_rows = nc.dram_tensor("h2_rows", (N, D), F32, kind="Internal").ap()
    h2_t = h2_rows.rearrange("(n p) d -> n p d", p=P)
    q_store = nc.dram_tensor("q_store", (NT, P, D), F32, kind="Internal").ap()
    mod_store = nc.dram_tensor("mod_store", (B, 4, D), F32, kind="Internal").ap()

    with ExitStack() as ctx:
        def sb(name, shape, dt=F32):
            return ctx.enter_context(nc.sbuf_tensor(name, shape, dt))

        def sem(name):
            return ctx.enter_context(nc.semaphore(name))

        bank = [ctx.enter_context(nc.psum_tensor(f"bank{i}", [P, 512], F32)) for i in range(8)]

        const_sb = sb("const_sb", [P, 3 * P + HC + E])
        ident = const_sb[:, 0:P]
        blk = const_sb[:, P:2 * P + HC]
        sel_e = const_sb[:, 2 * P + HC:2 * P + HC + E]
        same_f = const_sb[:, 2 * P + HC + E:]
        same_e = sb("same_e", [P, P], BF16)
        before = sb("before", [P, P], BF16)
        ones_b = sb("ones_b", [P, P], BF16)
        ones_f = sb("ones_f", [P, P])
        zeros = sb("zeros", [1, 512], BF16)
        rope_sb = sb("rope_sb", [P, TB, 3 * HALF])
        router_sb = sb("router_sb", [E, D])
        routerT = sb("routerT", [P, KC, E])
        c_sb = sb("c_sb", [B, D])
        c_act = sb("c_act", [B, D])
        cT = sb("cT", [P, KC, B])
        mod_col = sb("mod_col", [P, 2, KC, B])
        mod_row = sb("mod_row", [B, 4, D])
        gate_mag = sb("gate_mag", [B, 2, D])
        gate_sgn = sb("gate_sgn", [B, 2, D])
        mod_all = sb("mod_all", [P, B, 4, D])
        pad = sb("pad", [1, HALF])
        half_neg = sb("half_neg", [P, 1])
        iota_s = sb("iota_s", [P, P], BF16)

        logits = sb("logits", [P, NT, E])

        small = [sb(f"small{i}", [P, NT]) for i in range(8)]
        rev = sb("rev", [P, E])
        wgt = sb("wgt", [P, NT, E])
        val = sb("val", [P, NT, E])
        cand, base = sb("cand", [P, 3], I32), sb("base", [P, 3], I32)
        won, beats = sb("won", [P, 1], I32), sb("beats", [P, 3])
        digits = sb("digits", [P, DIGITS, 3], I32)
        swaps = sb("swaps", [P, DIGITS, 3], I32)
        cnt = sb("cnt", [P, 3], BF16)
        thr_sel, thr_b = sb("thr_sel", [P, E]), sb("thr_b", [P, E])
        mask2 = sb("mask2", [P, 2, E, NT], BF16)
        need = sb("need", [P, E])
        slot, keep = sb("slot", [P, E, NT]), sb("keep", [P, E, NT])
        vals = sb("vals", [P, E, NT, NV], BF16)
        w_hi, w_mid = sb("w_hi", [P, NT, E], BF16), sb("w_mid", [P, NT, E], BF16)

        iota_b = sb("iota_b", [P, P, NT], BF16)
        tile_ge = sb("tile_ge", [P, NT, CT + 1])
        tile_thr = sb("tile_thr", [P, CT + 1])
        in_tile = sb("in_tile", [P, NT, CT])
        tile_no = sb("tile_no", [P, NT])
        row_in = sb("row_in", [P, NT], BF16)
        onehot = sb("onehot", [P, P, NT], BF16)
        facts = sb("facts", [P, NT, NV, CT], BF16)
        got = sb("got", [P, NV, CT])
        tok = sb("tok", [P, CT])
        far = sb("far", [P, CT])
        g_idx = [sb(f"g_idx{i}", [P, CT], I32) for i in range(2)]
        s_idx = [sb(f"s_idx{i}", [P, CT], I32) for i in range(2)]
        w_slot = sb("w_slot", [P, 3, CT])
        w_b = [sb(f"w_b{i}", [P, B, CT]) for i in range(2)]

        w_raw = sb("w_raw", [P, FC, WU])
        w_h, w_l = sb("w_h", [P, FC, WU], F32R), sb("w_l", [P, FC, WU], F32R)
        own = ExitStack()

        def sa(name, shape, dt=F32):
            return own.enter_context(nc.sbuf_tensor(name, shape, dt))

        wmod_sb = sa("wmod_sb", [P, KC, 6 * D])
        wqkv_sb = sa("wqkv_sb", [P, KC, 3 * D])
        wqkv_h, wqkv_l = sa("wqkv_h", [P, KC, 3 * D], F32R), sa("wqkv_l", [P, KC, 3 * D], F32R)
        wout_sb = sa("wout_sb", [P, KC, D])
        wout_g = [sa(f"wout_g{b}", [P, KC, D]) for b in range(B)]
        x_in = [sa(f"x_in{i}", [P, D]) for i in range(2)]
        st1, mv1 = sa("st1", [P, 6]), sa("mv1", [P, 2])
        nm1, ve1 = ([sa(f"{n}_{i}", [P, 1]) for i in range(2)] for n in ("nm1", "ve1"))
        rs1, sh1 = sa("rs1", [P, 1]), sa("sh1", [P, 1])
        hn = sa("hn", [P, D])
        hT = sa("hT", [P, KC, P])
        hT_h, hT_l = ([sa(f"{n}{i}", [P, KC, P], F32R) for i in range(2)] for n in ("hT_h", "hT_l"))
        rot_a, rot_b = sa("rot_a", [P, 2 * D]), sa("rot_b", [P, 2 * D])
        rot = [sa(f"rot{i}", [P, 2 * D]) for i in range(2)]
        neg, ex, feat = sa("neg", [P, 2 * D]), sa("ex", [P, 2 * D]), sa("feat", [P, 2 * D])
        vx = [sa(f"vx{i}", [P, KC, P + 1]) for i in range(2)]
        qT = [sa(f"qT{i}", [P, D]) for i in range(2)]
        kvb = [sa(f"kvb{b}", [P, KC, P + HC]) for b in range(B)]

        q_in = [sa(f"q_in{i}", [P, D]) for i in range(2)]
        den_m, den_r = sa("den_m", [P, KC, HC]), sa("den_r", [P, KC, HC])
        att, attT = sa("att", [P, D]), sa("attT", [P, D])
        x_re = [sa(f"x_re{i}", [P, D]) for i in range(2)]
        x2 = [sa(f"x2_{i}", [P, D]) for i in range(2)]
        st2, mv2 = sa("st2", [P, 6]), sa("mv2", [P, 2])
        nm2, ve2 = ([sa(f"{n}_{i}", [P, 1]) for i in range(2)] for n in ("nm2", "ve2"))
        rs2, sh2 = sa("rs2", [P, 1]), sa("sh2", [P, 1])
        xn2, xm2 = [sa(f"xn2_{i}", [P, D]) for i in range(2)], sa("xm2", [P, D])
        h2 = [sa(f"h2_{i}", [P, D]) for i in range(2)]
        h2T = sa("h2T", [P, D])
        own.close()

        big = [sb(f"big{i}", [P, NT, E]) for i in range(8)]
        valT = sb("valT", [P, 2 * P])
        hit = sb("hit", [P, 3, 2 * P], BF16)
        reset = sb("reset", [P, 2 * E, NT])
        run = sb("run", [P, 2, E, NT])
        pre = sb("pre", [P, 2, E, NT])
        tmp_s = sb("tmp_s", [P, E, NT])
        w_r1, w_r2 = sb("w_r1", [P, NT, E]), sb("w_r2", [P, NT, E])
        xg = sb("xg", [P, CT, D])
        xT_h = [sb(f"xT_h{i}", [P, KC, CAP], F32R) for i in range(2)]
        xT_l = [sb(f"xT_l{i}", [P, KC, CAP], F32R) for i in range(2)]
        act_g = [sb(f"act_g{i}", [P, HCAP]) for i in range(2)]
        hid = [sb(f"hid{i}", [P, HCAP]) for i in range(2)]
        hid_h = [sb(f"hid_h{i}", [P, CAP], F32R) for i in range(2)]
        hid_l = [sb(f"hid_l{i}", [P, CAP], F32R) for i in range(2)]
        gw0 = sb("gw0", [P, D])
        gw = sb("gw", [P, CT, D])
        xo, yo = sb("xo", [P, CT, D]), sb("yo", [P, CT, D])

        qk_ps = bank[0][:, :]
        v_ps = bank[1][:, 0:D]
        h2T_ps = bank[6][:, 0:D]
        o_ps = bank[2][:, 0:KC * (P + HC)].rearrange("p (c n) -> p c n", c=KC)
        lg_ps = [bank[6][:, D:D + E], bank[4][:, 0:E]]
        kv_ps = bank[3][:, 0:KC * (P + 1)].rearrange("p (c n) -> p c n", c=KC)
        hT_ps = bank[4][:, 0:D].rearrange("p (c n) -> p c n", c=KC)
        qT_ps = bank[5][:, 0:D]
        oT_ps = [bank[7][:, 0:D], bank[5][:, 0:D]]
        y_ps = bank[7][:, D:2 * D]
        row_ps = (bank[2][0:B, :], bank[7][0:B, :])

        ld_c, ld_mod, ld_const, ld_w = sem("ld_c"), sem("ld_mod"), sem("ld_const"), sem("ld_w")
        ld_rest, st_mod, ld_ga, ld_all = sem("ld_rest"), sem("st_mod"), sem("ld_ga"), sem("ld_all")
        ld_x, ld_q, ld_xr = ([sem(f"{n}{i}") for i in range(2)] for n in ("ld_x", "ld_q", "ld_xr"))
        st_q, st_x2, st_h2 = ([sem(f"{n}{i}") for i in range(2)] for n in ("st_q", "st_x2", "st_h2"))
        pe_pre, act_pre, dve_pre = sem("pe_pre"), sem("act_pre"), sem("dve_pre")
        link_s, plink_s = sem("link_s"), sem("plink_s")
        bn1, ag1, stat1, pow1, scale1, norm1 = (sem(n) for n in ("bn1", "ag1", "stat1", "pow1", "scale1", "norm1"))
        tr_h, hT_d, qk_done, qkv_done, neg_d = (sem(n) for n in ("tr_h", "hT_d", "qk_done", "qkv_done", "neg_d"))
        hTh_d, hTl_d = sem("hTh_d"), sem("hTl_d")
        rope_m, rope_d, v_done, exp_d, feat_d = (sem(n) for n in ("rope_m", "rope_d", "v_done", "exp_d", "feat_d"))
        tr_q, qT_d, kv_d, kvb_d, kvb_link = (sem(n) for n in ("tr_q", "qT_d", "kv_d", "kvb_d", "kvb_link"))
        o_d, dmax, drec, att_d = sem("o_d"), sem("dmax"), sem("drec"), sem("att_d")
        tr_o, oT_d, y_d, x2_d = sem("tr_o"), sem("oT_d"), sem("y_d"), sem("x2_d")
        bn2, ag2, stat2, pow2, scale2 = (sem(n) for n in ("bn2", "ag2", "stat2", "pow2", "scale2"))
        norm2, pm2, h2_d = sem("norm2"), sem("pm2"), sem("h2_d")
        tr_h2, h2T_d, lg_d, lgc = sem("tr_h2"), sem("h2T_d"), sem("lg_d"), sem("lgc")
        iota_d = sem("iota_d")
        r_dve, r_act, r_pe, r_pool = sem("r_dve"), sem("r_act"), sem("r_pe"), sem("r_pool")
        cnt_d, tot_d, wonf_d, won_d, cand_d = (sem(n) for n in ("cnt_d", "tot_d", "wonf_d", "won_d", "cand_d"))
        pre_d = sem("pre_d")
        ge_d, in_d, tn_d, ri_d = sem("ge_d"), sem("in_d"), sem("tn_d"), sem("ri_d")
        facts_d, look_d, got_d, fin_l, idx_d = (sem(n) for n in ("facts_d", "look_d", "got_d", "fin_l", "idx_d"))
        raw_a, raw_b, sp_h, sp_l = sem("raw_a"), sem("raw_b"), sem("sp_h"), sem("sp_l")
        ga_d = [sem(f"ga_d{g}") for g in range(XG)]
        trx_d, xh_d, xl_d = sem("trx_d"), sem("xh_d"), sem("xl_d")
        gu_d, silu_d, hid_d, hh_d, hl_d, dn_d = (sem(n) for n in ("gu_d", "silu_d", "hid_d", "hh_d", "hl_d", "dn_d"))
        y_tile, wb_l, wb_d = sem("y_tile"), sem("wb_l"), sem("wb_d")
        gw0_d, gw_d, xo_d, ym_d, yo_d, sc_d = (sem(n) for n in ("gw0_d", "gw_d", "xo_d", "ym_d", "yo_d", "sc_d"))

        apart = sem("apart")

        block = ctx.enter_context(nc.Block())

        @block.sync
        def _(sp):
            sp.dma_start(c_sb[:, :], c).then_inc(ld_c, 16)
            sp.dma_start(const_sb[:, :], consts).then_inc(ld_c, 16)
            sp.dma_start(x_in[0][:, :], xt[0]).then_inc(ld_x[0], 16)
            sp.dma_start(x_in[1][:, :], xt[1]).then_inc(ld_x[1], 16)
            wm = wmod.rearrange("(c p) n -> p c n", p=P)
            sp.dma_start(wmod_sb[:, :, 0:2 * D], wm[:, :, 0:2 * D]).then_inc(ld_mod, 16)
            sp.dma_start(wqkv_sb[:, :, :], w_qkv.rearrange("(c p) n -> p c n", p=P)).then_inc(ld_w, 16)
            sp.dma_start(rope_sb[:, :, :], rope.rearrange("(n p) d -> p n d", p=P)).then_inc(ld_const, 16)

            def load_weights(e, lo, done, parts=range(WEIGHT_LOADS)):
                hi = lo + FC // 2
                for part in parts:
                    if part < 2 * KC:
                        w, at, k = (wg, wu)[part // KC], (0, 2 * P)[part // KC], part % KC
                        src = w[e, k * P:(k + 1) * P, :].rearrange("p (f n) -> p f n", n=P)[:, lo:hi, :]
                        dst = w_raw[:, lo:hi, at + k * P:at + (k + 1) * P]
                    else:
                        src = wd[e].rearrange("(f p) n -> p f n", p=P)[:, lo:hi, :]
                        dst = w_raw[:, lo:hi, 4 * P:]
                    sp.dma_start(dst, src).then_inc(done, 16)

            def step(s):
                on = stages(s)
                if on["qload"]:
                    o = 1 - LAG
                    wait(sp, o_d, s.t(o - 1))
                    wait(sp, st_q[s.par(o)], (s.half(o) + 1) * 16)
                    sp.dma_start(q_in[s.par(o)][:, :], q_store[s.t(o)]).then_inc(ld_q[s.par(o)], 16)
                if on["xrload"]:
                    o = -LAG
                    wait(sp, x2_d, s.t(o - 1))
                    sp.dma_start(x_re[s.par(o)][:, :], xt[s.t(o)]).then_inc(ld_xr[s.par(o)], 16)
                if on["trh2"]:
                    o = -LAG - 4
                    wait(sp, h2_d, s.t(o + 1))
                    sp.dma_start(h2_t[s.t(o)], h2[s.par(o)][:, :]).then_inc(st_h2[s.par(o)], 16)
                if on["scale2"]:
                    o = -LAG - 2
                    wait(sp, x2_d, s.t(o + 1))
                    sp.dma_start(out_t[s.t(o)], x2[s.par(o)][:, :]).then_inc(st_x2[s.par(o)], 16)
                if on["qstore"]:
                    wait(sp, qT_d, s.t(-2))
                    sp.dma_start(q_store[s.t(-3)], qT[s.par(-3)][:, :]).then_inc(st_q[s.par(-3)], 16)
                if on["xload"] and s.rep >= -2:
                    wait(sp, norm1, s.t(3))
                    sp.dma_start(x_in[s.par(4)][:, :], xt[s.t(4)]).then_inc(ld_x[s.par(4)], 16)
                if s.rep in (-1, 0):
                    at = (s.rep + 1) * 2 * D + 2 * D
                    sp.dma_start(wmod_sb[:, :, at:at + 2 * D], wm[:, :, at:at + 2 * D]).then_inc(ld_rest, 16)
                if s.rep == 1:
                    sp.dma_start(router_sb[:, :], router).then_inc(ld_rest, 16)
                    sp.dma_start(wout_sb[:, :, :], w_out.rearrange("(c p) n -> p c n", p=P)).then_inc(ld_rest, 16)
                if s.rep == TB:
                    sp.wait_ge(dve_pre, 6)
                    sp.dma_start(mod_store, mod_row[:, :, :]).then_inc(st_mod, 16)
                if 0 <= s.rep - (TB + 1) < 4:
                    row = s.rep - (TB + 1)
                    if row == 0:
                        sp.wait_ge(st_mod, 16)
                    for b in range(B):
                        sp.dma_start(mod_all[:, b, row, :], mod_store[b, row, :].partition_broadcast(P))\
                            .then_inc(ld_all if row else ld_ga, 16)
                if 0 <= s.rep - (LAG + 1) < WEIGHT_LOADS:
                    part = s.rep - (LAG + 1)
                    load_weights(0, 0, raw_a, parts=(part,))
                    load_weights(0, FC // 2, raw_b, parts=(part,))

            steps(sp, step, ATT)

            sp.wait_ge(sp_h, 4)
            sp.wait_ge(sp_l, 4)
            load_weights(1, 0, raw_a)

            def expert(e, last):
                if last >= 1:
                    return
                wait(sp, sp_h, e * FC + FC)
                wait(sp, sp_l, e * FC + FC)
                load_weights(e + 1, FC // 2, raw_b)
                if last == 0:
                    wait(sp, sp_h, e * FC + FC + FC // 2)
                    wait(sp, sp_l, e * FC + FC + FC // 2)
                    load_weights(e + 2, 0, raw_a)

            with sp.Fori(0, (E - 2) // 2) as k:
                expert(k * 2, 0)
                expert(k * 2 + 1, 0)
            expert(E - 2, 0.5)

        @block.gpsimd
        def _(pool):
            pool.dma_start(pad[:, :], rope[0:1, 0:HALF]).then_inc(sc_d, 16)
            nc.gpsimd.memset(half_neg[:, :], -0.5).then_inc(plink_s, 1)
            nc.gpsimd.memset(ones_b[:, :], 1.0).then_inc(plink_s, 1)
            nc.gpsimd.memset(ones_f[:, :], 1.0).then_inc(plink_s, 1)
            nc.gpsimd.memset(zeros[:, :], 0.0).then_inc(plink_s, 1)
            for i in range(2):
                nc.gpsimd.memset(vx[i][:, :, P:P + 1], 1.0).then_inc(plink_s, 1)
            pool.wait_ge(plink_s, 6)
            nc.gpsimd.affine_select(out=before[:, :], in_=ones_b[:, :], compare_op=ALU.is_gt, fill=0.0, base=0,
                                    pattern=[[1, P]], channel_multiplier=-1).then_inc(plink_s, 1)
            nc.gpsimd.iota(iota_s[:, :], pattern=[[1, P]], base=0, channel_multiplier=0,
                           allow_small_or_imprecise_dtypes=True).then_inc(plink_s, 1)
            nc.gpsimd.iota(rev[:, :], pattern=[[-1, E]], base=E, channel_multiplier=0,
                           allow_small_or_imprecise_dtypes=True).then_inc(plink_s, 1)
            nc.gpsimd.iota(tile_thr[:, :], pattern=[[P, CT + 1]], base=0, channel_multiplier=0,
                           allow_small_or_imprecise_dtypes=True).then_inc(plink_s, 1)
            nc.gpsimd.iota(vals[:, :, :, 0], pattern=[[0, E], [0, NT]], base=0, channel_multiplier=1,
                           allow_small_or_imprecise_dtypes=True).then_inc(plink_s, 1)
            nc.gpsimd.iota(vals[:, :, :, 1], pattern=[[0, E], [1, NT]], base=1, channel_multiplier=0,
                           allow_small_or_imprecise_dtypes=True).then_inc(plink_s, 1)
            for n in range(DIGITS):
                unit = 1 << (TOP_BIT - 1 - 2 * n)
                for d in range(3):
                    nc.gpsimd.memset(digits[:, n, d:d + 1], (d + 1) * unit)
                    ins = nc.gpsimd.memset(swaps[:, n, d:d + 1], (d + 1) * unit | ((d + 1) * unit >> 2))
            ins.then_inc(plink_s, 1)

            def step(s):
                on = stages(s)
                if on["norm"]:
                    wait(pool, stat1, s.t(3))
                    wait(pool, norm1, s.t(2))
                    nc.gpsimd.tensor_tensor(rs1[:, :], ve1[s.par(2)][:, :], half_neg[:, :], ALU.pow).then_inc(pow1, 1)
                    if on["att"]:
                        pool.wait_ge(pow1, s.t(3))
                        nc.gpsimd.tensor_tensor(sh1[:, :], nm1[s.par(2)][:, :], rs1[:, :], ALU.mult).then_inc(scale1, 1)
                    else:
                        wait(pool, tr_h, s.t(2))
                        wait_apart(pool, pow1, s.t(3), apart)
                        nc.gpsimd.tensor_scalar(hn[:, :], x_in[s.par(2)][:, :], nm1[s.par(2)][:, :], rs1[:, :],
                                                ALU.add, ALU.mult).then_inc(norm1, 1)
                        pool.sem_inc(scale1, 1)
                if on["trh"] and spared(s):
                    wait(pool, hTh_d, s.t(2))
                    nc.gpsimd.tensor_tensor(hT_l[s.par(1)][:, :, :], hT[:, :, :], hT_h[s.par(1)][:, :, :].bitcast(F32),
                                            ALU.subtract).then_inc(hTl_d, 1)
                if on["scale2"]:
                    o = -LAG - 2
                    wait(pool, stat2, s.t(o + 1))
                    wait(pool, norm2, s.t(o))
                    nc.gpsimd.tensor_tensor(rs2[:, :], ve2[s.par(o)][:, :], half_neg[:, :], ALU.pow).then_inc(pow2, 1)
                    pool.wait_ge(pow2, s.t(o + 1))
                    nc.gpsimd.tensor_tensor(sh2[:, :], nm2[s.par(o)][:, :], rs2[:, :], ALU.mult).then_inc(scale2, 1)
                if on["second"]:
                    o = -LAG - 3
                    b = (s.rep + o) // TB
                    if s.rep + o == 0:
                        pool.wait_ge(ld_all, 3 * B * 16)
                    wait(pool, norm2, s.t(o + 1))
                    wait(pool, h2_d, s.t(o))
                    nc.gpsimd.tensor_tensor(xm2[:, :], xn2[s.par(o)][:, :], mod_all[:, b, 2, :], ALU.mult).then_inc(pm2, 1)
                    pool.wait_ge(pm2, s.t(o + 1))
                    wait(pool, st_h2[s.par(o)], s.half(o) * 16)
                    wait(pool, tr_h2, s.t(o - 1))
                    nc.gpsimd.tensor_tensor(h2[s.par(o)][:, :], xm2[:, :], mod_all[:, b, 1, :], ALU.add)\
                        .then_inc(h2_d, 1)
                if on["qkv"]:
                    wait(pool, rope_m, s.t(1))
                    wait(pool, feat_d, s.t(-1))
                    nc.gpsimd.tensor_tensor(rot[s.par(0)][:, :], rot_a[:, :], rot_b[:, :], ALU.add).then_inc(rope_d, 1)

            steps(pool, step, ATT)

            pool.wait_ge(lgc, NT)
            nc.gpsimd.memset(reset[:, :, :], 1.0).then_inc(plink_s, 1)
            pool.wait_ge(plink_s, 14)
            nc.gpsimd.memset(reset[:, :, 0:1], 0.0).then_inc(plink_s, 1)
            wT = lambda a: a.rearrange("p n e -> p e n")
            pool.wait_ge(r_dve, 3)
            nc.gpsimd.tensor_copy(w_hi[:, :, :], wgt[:, :, :]).then_inc(r_pool, 1)
            pool.wait_ge(r_pool, 1)
            nc.gpsimd.tensor_tensor(w_r1[:, :, :], wgt[:, :, :], w_hi[:, :, :], ALU.subtract).then_inc(r_pool, 1)
            pool.wait_ge(r_pool, 2)
            nc.gpsimd.tensor_copy(w_mid[:, :, :], w_r1[:, :, :]).then_inc(r_pool, 1)
            pool.wait_ge(r_pool, 3)
            nc.gpsimd.tensor_tensor(w_r2[:, :, :], w_r1[:, :, :], w_mid[:, :, :], ALU.subtract).then_inc(r_pool, 1)
            pool.wait_ge(r_pool, 4)
            nc.gpsimd.tensor_copy(vals[:, :, :, 2], wT(w_hi[:, :, :])).then_inc(r_pool, 1)
            nc.gpsimd.tensor_copy(vals[:, :, :, 3], wT(w_mid[:, :, :])).then_inc(r_pool, 1)
            nc.gpsimd.tensor_copy(vals[:, :, :, 4], wT(w_r2[:, :, :])).then_inc(r_pool, 1)

            def split_low(e, f, count):
                raw = raw_a if f < FC // 2 else raw_b
                wait(pool, raw, (e + 1) * WEIGHT_LOADS * 16)
                wait(pool, sp_h, count + 1)
                nc.gpsimd.tensor_tensor(w_l[:, f, :], w_raw[:, f, :], w_h[:, f, :].bitcast(F32), ALU.subtract)\
                    .then_inc(sp_l, 1)

            for f in range(FC - 2):
                split_low(0, f, f)

            def gather(rows, dst, idx, done):
                for a in range(CT):
                    nc.gpsimd.indirect_dma_start(
                        out=dst[:, a, :], out_offset=None, in_=rows,
                        in_offset=bass.IndirectOffsetOnAxis(ap=idx[:, a:a + 1], axis=0))\
                        .then_inc(done[a // 2] if isinstance(done, list) else done, 16)

            for i in range(2):
                pool.wait_ge(st_h2[i], NT // 2 * 16)
                pool.wait_ge(st_x2[i], NT // 2 * 16)
            pool.wait_ge(idx_d, 1)
            gather(h2_rows, xg, g_idx[0], ga_d)

            def expert(e, par, last):
                for f in (0, 1):
                    split_low(e, FC - 2 + f, e * FC + FC - 2 + f)
                if last < 1:
                    wait_apart(pool, idx_d, e + 2, apart)
                    wait_apart(pool, trx_d, e * XG + XG, apart)
                    gather(h2_rows, xg, g_idx[1 - par], ga_d)
                wait_apart(pool, sc_d, e * CT * 16 + 16, apart)
                gather(out_rows, xo, g_idx[par], xo_d)
                if last < 1:
                    for f in range(FC - 2):
                        split_low(e + 1, f, e * FC + FC + f)
                for a in range(CT):
                    wait_apart(pool, yo_d, e * CT + a + 1, apart)
                    nc.gpsimd.indirect_dma_start(
                        out=out_rows, out_offset=bass.IndirectOffsetOnAxis(ap=s_idx[par][:, a:a + 1], axis=0),
                        in_=yo[:, a, :], in_offset=None, bounds_check=N - 1, oob_is_err=False).then_inc(sc_d, 16)

            with pool.Fori(0, (E - 2) // 2) as k:
                expert(k * 2, 0, 0)
                expert(k * 2 + 1, 1, 0)
            expert(E - 2, 0, 0.5)
            expert(E - 1, 1, 1)
            pool.wait_ge(sc_d, E * CT * 16 + 16)

        @block.scalar
        def _(act):
            act.wait_ge(ld_c, 32)
            nc.scalar.activation(c_act[:, :], c_sb[:, :], ACT.Silu).then_inc(act_pre, 1)
            act.wait_ge(plink_s, 8)
            nc.scalar.copy(iota_b[:, :, :], iota_s[:, :].unsqueeze(2).to_broadcast([P, P, NT])).then_inc(iota_d, 1)

            def exp_logits(lo, hi):
                act.wait_ge(r_act, 2 if hi == NT else 1)
                nc.scalar.activation(big[1][:, lo:hi, :], big[0][:, lo:hi, :], ACT.Exp).then_inc(act_pre, 1)

            def copy_v(s):
                wait(act, qkv_done, s.t(1))
                wait(act, kv_d, s.t(-1))
                if s.rep < 2:
                    act.wait_ge(plink_s, 6)
                nc.scalar.copy(vx[s.par(0)][:, :, 0:P], v_ps.rearrange("p (c n) -> p c n", c=KC)).then_inc(v_done, 1)

            def step(s):
                on = stages(s)
                if s.rep == -1:
                    act.wait_ge(dve_pre, 4)
                    nc.scalar.copy(wqkv_h[:, :, 0:2 * D], wqkv_sb[:, :, 0:2 * D]).then_inc(act_pre, 1)
                    nc.scalar.copy(wqkv_h[:, :, 2 * D:], wqkv_sb[:, :, 2 * D:]).then_inc(act_pre, 1)
                if on["trh"]:
                    b = (s.rep + 1) // TB
                    if s.rep == -1:
                        act.wait_ge(dve_pre, 3)
                    wait(act, tr_h, s.t(2))
                    wait(act, hTl_d, s.t(1))
                    for k in range(KC):
                        ins = nc.scalar.activation(hT[:, k, :], hT_ps[:, k, :], ACT.Identity,
                                                   bias=mod_col[:, 0, k, b:b + 1], scale=mod_col[:, 1, k, b:b + 1])
                    ins.then_inc(hT_d, 1)
                if on["norm"] and on["att"]:
                    wait(act, scale1, s.t(3))
                    wait(act, tr_h, s.t(2))
                    nc.scalar.activation(hn[:, :], x_in[s.par(2)][:, :], ACT.Identity, bias=sh1[:, :],
                                         scale=rs1[:, :]).then_inc(norm1, 1)
                if on["trh"]:
                    wait(act, hT_d, s.t(2))
                    wait(act, qkv_done, s.t(0))
                    nc.scalar.copy(hT_h[s.par(1)][:, :, :], hT[:, :, :]).then_inc(hTh_d, 1)
                if on["feat"]:
                    wait(act, rope_d, s.t(0))
                    wait(act, feat_d, s.t(-1))
                    nc.scalar.activation(neg[:, :], rot[s.par(-1)][:, :], ACT.Relu, scale=-1.0).then_inc(neg_d, 1)
                if on["qkv"] and not on["att"]:
                    copy_v(s)
                if on["feat"]:
                    wait(act, neg_d, s.t(0))
                    nc.scalar.activation(ex[:, :], neg[:, :], ACT.Exp, scale=-1.0).then_inc(exp_d, 1)
                if on["proj"]:
                    o = -LAG - 1
                    wait(act, tr_o, s.t(o + 1))
                    wait(act, y_d, s.t(o))
                    nc.scalar.copy(attT[:, :], oT_ps[alone(s)]).then_inc(oT_d, 1)
                if on["qkv"] and on["att"]:
                    copy_v(s)
                if on["kv"]:
                    wait(act, tr_q, s.t(-1))
                    wait(act, st_q[s.par(-2)], s.half(-2) * 16)
                    nc.scalar.copy(qT[s.par(-2)][:, :], qT_ps).then_inc(qT_d, 1)
                if on["logit"]:
                    o = -LAG - 5
                    wait(act, lg_d, s.t(o + 1))
                    nc.scalar.copy(logits[:, s.t(o), :], lg_ps[alone(s)]).then_inc(lgc, 1)
                if on["scale2"]:
                    o = -LAG - 2
                    wait(act, scale2, s.t(o + 1))
                    wait(act, pm2, s.t(o - 1))
                    nc.scalar.activation(xn2[s.par(o)][:, :], x2[s.par(o)][:, :], ACT.Identity,
                                         bias=sh2[:, :], scale=rs2[:, :])\
                        .then_inc(norm2, 1)
                if on["trh2"]:
                    o = -LAG - 4
                    wait(act, tr_h2, s.t(o + 1))
                    wait(act, lg_d, s.t(o))
                    nc.scalar.copy(h2T[:, :], h2T_ps).then_inc(h2T_d, 1)
                if s.rep == NT + LAG + 1:
                    exp_logits(0, EARLY)

            steps(act, step, ATT)

            exp_logits(EARLY, NT)

            def split_high(e, f, count, implied=False):
                raw = raw_a if f < FC // 2 else raw_b
                wait(act, raw, (e + 1) * WEIGHT_LOADS * 16)
                if not implied:
                    wait(act, dn_d, count - FC + 1)
                nc.scalar.copy(w_h[:, f, :], w_raw[:, f, :]).then_inc(sp_h, 1)

            for f in range(FC - 2):
                split_high(0, f, f)

            def x_high(e, par, g, bk=7):
                n = min(2, CT - 2 * g) * P
                wait(act, trx_d, e * XG + g + 1)
                nc.scalar.copy(xT_h[par][:, :, 2 * g * P:2 * g * P + n],
                               bank[bk][:, 0:2 * n].rearrange("p (c n) -> p c n", c=KC)).then_inc(xh_d, 1)

            for g in range(XG):
                x_high(0, 0, g, bk=g)

            def expert(e, par, last):
                def gate_weight(a):
                    wait(act, wb_d, e + 1)
                    if a:
                        wait(act, gw_d, e * CT + a)
                    nc.scalar.activation(gw0[:, :], mod_all[:, 0, 3, :], ACT.Copy, scale=w_b[par][:, 0, a:a + 1])\
                        .then_inc(gw0_d, 1)

                for f in range(FC):
                    for h in range(2):
                        i = e * 2 * FC + 2 * f + h
                        wait(act, gu_d, i + 1)
                        if f:
                            wait(act, hid_d, i - 1)
                        nc.scalar.activation(act_g[h][:, :], bank[2 * h][:, 0:HCAP], ACT.Silu).then_inc(silu_d, 1)
                        wait(act, hid_d, i + 1)
                        if f >= 2:
                            wait(act, dn_d, e * FC + f - 1)
                        nc.scalar.copy(hid_h[f % 2][:, h * HCAP:(h + 1) * HCAP], hid[h][:, :]).then_inc(hh_d, 1)
                    if last < 1 and XF <= f < XF + XG:
                        x_high(e + 1, 1 - par, f - XF)
                    if f < 2:
                        split_high(e, FC - 2 + f, e * FC + FC - 2 + f, implied=True)
                    elif last < 1:
                        split_high(e + 1, f - 2, e * FC + FC + f - 2)
                    if f < CT:
                        gate_weight(f)

            with act.Fori(0, (E - 2) // 2) as k:
                expert(k * 2, 0, 0)
                expert(k * 2 + 1, 1, 0)
            expert(E - 2, 0, 0.5)
            expert(E - 1, 1, 1)

        @block.vector
        def _(dve):
            chain = [0]

            def link(ins):
                chain[0] += 1
                ins.then_inc(link_s, 1)
                dve.wait_ge(link_s, chain[0])

            V = nc.vector
            dve.wait_ge(pe_pre, 1)
            V.tensor_copy(cT[:, :, :], bank[0][:, 0:KC * B].rearrange("p (c b) -> p c b", c=KC)).then_inc(dve_pre, 1)
            dve.wait_ge(pe_pre, 2)
            V.tensor_copy(mod_col[:, 0, :, :], bank[1][:, 0:KC * B].rearrange("p (c b) -> p c b", c=KC))\
                .then_inc(dve_pre, 1)
            V.tensor_scalar(mod_col[:, 1, :, :], bank[1][:, KC * B:2 * KC * B].rearrange("p (c b) -> p c b", c=KC),
                            1.0, None, ALU.add).then_inc(dve_pre, 1)

            def mod_rows(part):
                g_ps = (row_ps[0][:, 0:D], row_ps[1][:, D:])
                if part == 0:
                    dve.wait_ge(pe_pre, 3)
                    V.tensor_copy(routerT[:, :, :], bank[6][:, 0:KC * E].rearrange("p (c e) -> p c e", c=KC))
                    V.tensor_copy(mod_row[:, 1, :], row_ps[0][:, D:])
                    V.tensor_scalar(mod_row[:, 2, :], row_ps[1][:, 0:D], 1.0, None, ALU.add)
                    V.tensor_copy(same_e[:, :], same_f)
                    return
                if part == 1:
                    for i in range(2):
                        V.tensor_scalar(gate_sgn[:, i, :], g_ps[i], 0.0, 2.0, ALU.is_ge, ALU.mult)
                        ins = V.tensor_scalar(gate_mag[:, i, :], g_ps[i], -1.0, None, ALU.mult)
                    link(ins)
                    return
                for i in range(2):
                    ins = V.tensor_tensor(gate_mag[:, i, :], g_ps[i], gate_mag[:, i, :], ALU.max)
                link(ins)
                link(V.tensor_scalar(gate_mag[:, :, :], gate_mag[:, :, :], GATE_MIN, None, ALU.max))
                V.scalar_tensor_tensor(mod_row[:, 0:4:3, :], gate_sgn[:, :, :], -1.0, gate_mag[:, :, :],
                                       ALU.add, ALU.mult).then_inc(dve_pre, 1)

            def gate_wout(b):
                dve.wait_ge(ld_ga, B * 16)
                V.tensor_tensor(wout_g[b][:, :, :], wout_sb[:, :, :],
                                mod_all[:, b, 0, :].unsqueeze(1).to_broadcast([P, KC, D]), ALU.mult).then_inc(dve_pre, 1)

            def variance(st, mv, bn, ag, count):
                wait_apart(dve, bn, count, apart)
                V.bn_aggr(mv[:, :], st[:, :]).then_inc(ag, 1)

            def finish_stats(mv, nm, ve, ag, done, count):
                dve.wait_ge(ag, count)
                V.tensor_scalar(nm[:, :], mv[:, 0:1], -1.0, None, ALU.mult)
                V.tensor_scalar(ve[:, :], mv[:, 1:2], LN_EPS, None, ALU.add).then_inc(done, 1)

            def variance2(s, o):
                variance(st2, mv2, bn2, ag2, s.t(o + 1))
                wait(dve, scale2, s.t(o - 1))
                finish_stats(mv2, nm2[s.par(o)], ve2[s.par(o)], ag2, stat2, s.t(o + 1))

            def between(s):
                return stages(s)["qkv"] and stages(s)["scale2"]

            TT, RED = V.tensor_tensor, V.tensor_reduce

            def choose(lo, hi):
                n = hi - lo
                b8 = lambda a: a.unsqueeze(2).to_broadcast([P, n, E])
                rev_b = rev[:, :].unsqueeze(1).to_broadcast([P, n, E])
                X = [t[:, lo:hi, :] for t in big]
                Y = [t[:, lo:hi] for t in small]
                part = 1 if hi == NT else 0
                dve.wait_ge(lgc, hi)
                link(RED(Y[0], logits[:, lo:hi, :], AX, ALU.max))
                TT(X[0], logits[:, lo:hi, :], b8(Y[0]), ALU.subtract).then_inc(r_act, 1)
                dve.wait_ge(act_pre, 4 + part)
                link(RED(Y[1], X[1], AX, ALU.add))
                link(V.reciprocal(Y[2], Y[1]))
                link(TT(X[2], X[1], b8(Y[2]), ALU.mult))
                prob = X[2]
                for i in range(TOPK):
                    m, first, hot, q = Y[3 + i], Y[5 + i], X[3 + i], X[5]
                    link(RED(m, prob, AX, ALU.max))
                    link(TT(q, prob, b8(m), ALU.is_equal))
                    link(TT(q, q, rev_b, ALU.mult))
                    link(RED(first, q, AX, ALU.max))
                    link(TT(hot, q, b8(first), ALU.is_equal))
                    if i == 0:
                        link(V.scalar_tensor_tensor(X[6], hot, -2.0, prob, ALU.mult, ALU.add))
                        prob = X[6]
                link(TT(Y[0], Y[3], Y[4], ALU.add))
                link(V.tensor_scalar(Y[0], Y[0], TOPW_EPS, None, ALU.add))
                link(V.reciprocal(Y[1], Y[0]))
                TT(Y[5], Y[3], Y[1], ALU.mult)
                link(TT(Y[6], Y[4], Y[1], ALU.mult))
                TT(X[0], X[3], b8(Y[5]), ALU.mult)
                TT(X[1], X[4], b8(Y[6]), ALU.mult)
                link(TT(X[7], X[3], X[4], ALU.add))
                link(TT(wgt[:, lo:hi, :], X[0], X[1], ALU.add))
                V.tensor_scalar(X[5], X[7], -1.0, None, ALU.add).then_inc(r_dve, 1)
                dve.wait_ge(r_dve, 1 + 2 * part)
                TT(val[:, lo:hi, :], wgt[:, lo:hi, :], X[5], ALU.add).then_inc(r_dve, 1)

            def step(s):
                on = stages(s)
                if s.rep == -1:
                    dve.wait_ge(ld_w, 16)
                    V.tensor_scalar(wqkv_sb[:, :, 0:D], wqkv_sb[:, :, 0:D], float(HD) ** -0.5, None, ALU.mult)\
                        .then_inc(dve_pre, 1)
                if s.rep == -1:
                    for i, sl in enumerate((slice(0, 2 * D), slice(2 * D, 3 * D))):
                        dve.wait_ge(act_pre, 2 + i)
                        ins = V.tensor_tensor(wqkv_l[:, :, sl], wqkv_sb[:, :, sl], wqkv_h[:, :, sl].bitcast(F32),
                                              ALU.subtract)
                    ins.then_inc(dve_pre, 1)
                if s.rep in (LAG, NT - 4):
                    gate_wout(int(s.rep > LAG))
                if on["stats"]:
                    wait(dve, ld_x[s.par(3)], (s.half(3) + 1) * 16)
                    V.bn_stats(st1[:, :], x_in[s.par(3)][:, :]).then_inc(bn1, 1)
                if on["scale2"] and between(s):
                    variance2(s, -LAG - 2)
                if on["qkv"]:
                    if s.rep == 0:
                        dve.wait_ge(ld_const, 16)
                    cs = rope_sb[:, s.t(-(s.rep // TB) * TB), :]
                    wait(dve, qk_done, s.t(1))
                    wait(dve, rope_d, s.t(0))
                    g = 2 * D // HALF
                    V.tensor_tensor(rot_a[:, :].rearrange("p (g d) -> p g d", d=HALF),
                                    qk_ps.rearrange("p (g d) -> p g d", d=HALF),
                                    cs[:, 0:HALF].unsqueeze(1).to_broadcast([P, g, HALF]), ALU.mult)
                    qv = qk_ps.rearrange("p (g a d) -> p g a d", a=2, d=HALF)
                    rv = rot_b[:, :].rearrange("p (g a d) -> p g a d", a=2, d=HALF)
                    V.tensor_tensor(rv[:, :, 0, :], qv[:, :, 1, :],
                                    cs[:, 2 * HALF:].unsqueeze(1).to_broadcast([P, g // 2, HALF]), ALU.mult)
                    V.tensor_tensor(rv[:, :, 1, :], qv[:, :, 0, :],
                                    cs[:, HALF:2 * HALF].unsqueeze(1).to_broadcast([P, g // 2, HALF]), ALU.mult)\
                        .then_inc(rope_m, 1)
                if on["stats"]:
                    variance(st1, mv1, bn1, ag1, s.t(4))
                if on["trh"] and not spared(s):
                    wait(dve, hTh_d, s.t(2))
                    V.tensor_tensor(hT_l[s.par(1)][:, :, :], hT[:, :, :], hT_h[s.par(1)][:, :, :].bitcast(F32),
                                    ALU.subtract).then_inc(hTl_d, 1)
                if on["stats"]:
                    wait(dve, scale1, s.t(2))
                    finish_stats(mv1, nm1[s.par(3)], ve1[s.par(3)], ag1, stat1, s.t(4))
                if on["feat"]:
                    wait(dve, exp_d, s.t(0))
                    wait(dve, tr_q, s.t(-1))
                    wait(dve, kv_d, s.t(-1))
                    V.scalar_tensor_tensor(feat[:, :], rot[s.par(-1)][:, :], 0.0, ex[:, :],
                                           ALU.max, ALU.add).then_inc(feat_d, 1)
                if on["att"]:
                    o = -LAG
                    wait(dve, o_d, s.t(o + 1))
                    V.tensor_scalar(den_m[:, :, :], o_ps[:, :, P:], DEN_EPS, None, ALU.max).then_inc(dmax, 1)
                    dve.wait_ge(dmax, s.t(o + 1))
                    V.reciprocal(den_r[:, :, :], den_m[:, :, :]).then_inc(drec, 1)
                    dve.wait_ge(drec, s.t(o + 1))
                    wait(dve, tr_o, s.t(o))
                    V.tensor_tensor(att[:, :].rearrange("p (c h d) -> p c h d", c=KC, d=HD),
                                    o_ps[:, :, 0:P].rearrange("p c (h d) -> p c h d", d=HD),
                                    den_r[:, :, :].unsqueeze(3).to_broadcast([P, KC, HC, HD]), ALU.mult)\
                        .then_inc(att_d, 1)
                if on["proj"]:
                    o = -LAG - 1
                    wait(dve, y_d, s.t(o + 1))
                    wait(dve, ld_xr[s.par(o)], (s.half(o) + 1) * 16)
                    wait(dve, st_x2[s.par(o)], s.half(o) * 16)
                    wait(dve, norm2, s.t(o - 1))
                    V.tensor_tensor(x2[s.par(o)][:, :], y_ps, x_re[s.par(o)][:, :], ALU.add).then_inc(x2_d, 1)
                    dve.wait_ge(x2_d, s.t(o + 1))
                    V.bn_stats(st2[:, :], x2[s.par(o)][:, :]).then_inc(bn2, 1)
                    if not between(Step(s.k, s.j, s.rep + 1)):
                        variance2(s, o)
                if s.rep == NT + LAG:
                    dve.wait_ge(plink_s, 13)
                    dve.wait_ge(iota_d, 1)
                    choose(0, EARLY)
                if s.rep == 3:
                    mod_rows(0)
                if s.rep in (TB - 2, TB - 1):
                    mod_rows(s.rep - TB + 3)
                if s.rep in (TB + 1, NT + 1):
                    b = s.rep // TB - 1
                    dve.wait_ge(kv_d, s.rep - 1)
                    V.tensor_tensor(kvb[b][:, :, 0:P], kv_ps[:, :, 0:P],
                                    blk[:, 0:P].unsqueeze(1).to_broadcast([P, KC, P]), ALU.mult)
                    V.tensor_tensor(kvb[b][:, :, P:], kv_ps[:, :, P:P + 1].to_broadcast([P, KC, HC]),
                                    blk[:, P:].unsqueeze(1).to_broadcast([P, KC, HC]), ALU.mult).then_inc(kvb_d, 1)

            steps(dve, step, ATT)

            choose(EARLY, NT)
            for d in range(3):
                ins = V.memset(cand[:, d:d + 1], (d + 1) << (TOP_BIT - 1))
            link(ins)
            dve.wait_ge(r_pe, 1)
            link(V.tensor_copy(valT[:, :], bank[0][:, 0:2 * P]))
            with dve.Fori(0, DIGITS // SEARCH) as i:
                for j in range(SEARCH):
                    n = i * SEARCH + j
                    for d in range(3):
                        ins = V.tensor_scalar(hit[:, d, :], valT[:, :], cand[:, d:d + 1].bitcast(F32), 0.0, ALU.is_ge,
                                              ALU.add, accum_out=cnt[:, d:d + 1])
                    ins.then_inc(cnt_d, 1)
                    TT(base[:, :], cand[:, :], swaps[:, n, :], ALU.bitwise_xor)
                    dve.wait_ge(tot_d, n + 1)
                    V.scalar_tensor_tensor(beats[:, :], bank[1][:, 0:3], float(CAP), digits[:, n, :],
                                           ALU.is_ge, ALU.mult).then_inc(wonf_d, 1)
                    dve.wait_ge(wonf_d, n + 1)
                    RED(won[:, :], beats[:, :], AX, ALU.max).then_inc(won_d, 1)
                    dve.wait_ge(won_d, n + 1)
                    TT(cand[:, :], base[:, :], won[:, :].to_broadcast([P, 3]), ALU.bitwise_or).then_inc(cand_d, 1)
                    dve.wait_ge(cand_d, n + 1)
            V.tensor_scalar(thr_sel[:, :], sel_e[:, :], cand[:, 0:1].bitcast(F32), None, ALU.mult).then_inc(r_dve, 1)
            dve.wait_ge(r_pe, 2)
            link(V.tensor_copy(thr_b[:, :], bank[2][:, 0:E]))
            dve.wait_ge(plink_s, 15)

            def place_masks(part):
                lo, hi = PLACES[part]
                tb = thr_b[:, lo:hi].unsqueeze(1).to_broadcast([P, NT, hi - lo])
                for k, op in enumerate((ALU.is_gt, ALU.is_equal)):
                    ins = TT(mask2[:, k, lo:hi, :].rearrange("p e n -> p n e"), val[:, :, lo:hi], tb, op)
                ins.then_inc(r_dve, 1)

            def place_counts(part):
                lo, hi = PLACES[part]
                n = hi - lo
                dve.wait_ge(r_pe, 3 + part)
                rows, tot = ([bank[bk + 2 * part][:, k * n * NT:(k + 1) * n * NT] for k in range(2)] for bk in (3, 4))
                flat = lambda a: a.rearrange("p e n -> p (e n)")
                for k in range(2):
                    ins = V.tensor_tensor_scan(flat(run[:, k, lo:hi, :]), flat(reset[:, 0:n, :]), tot[k], 0.0,
                                               ALU.mult, ALU.add)
                link(ins)
                V.tensor_scalar(need[:, lo:hi], run[:, 0, lo:hi, NT - 1], -1.0, float(CAP), ALU.mult, ALU.add)
                for k in range(2):
                    ins = TT(flat(pre[:, k, lo:hi, :]), flat(run[:, k, lo:hi, :]), tot[k], ALU.subtract)
                link(ins)
                for k in range(2):
                    ins = TT(flat(pre[:, k, lo:hi, :]), flat(pre[:, k, lo:hi, :]), rows[k], ALU.add)
                ins.then_inc(pre_d, 1)

            def place_slots(part):
                lo, hi = PLACES[part]
                dve.wait_ge(pre_d, part + 1)
                need_b = need[:, lo:hi].unsqueeze(2).to_broadcast([P, hi - lo, NT])
                at, kept, t = slot[:, lo:hi, :], keep[:, lo:hi, :], tmp_s[:, lo:hi, :]
                TT(t, pre[:, 1, lo:hi, :], need_b, ALU.is_lt)
                link(TT(at, pre[:, 1, lo:hi, :], need_b, ALU.min))
                link(TT(t, t, mask2[:, 1, lo:hi, :], ALU.mult))
                TT(kept, t, mask2[:, 0, lo:hi, :], ALU.add)
                link(TT(at, at, pre[:, 0, lo:hi, :], ALU.add))
                link(V.scalar_tensor_tensor(kept, at, float(CAP), kept, ALU.is_lt, ALU.mult))
                link(V.scalar_tensor_tensor(at, at, 1.0, kept, ALU.add, ALU.mult))
                link(V.tensor_scalar(at, at, -1.0, None, ALU.add))

            place_masks(0)
            place_counts(0)
            place_slots(0)
            dve.wait_ge(r_pool, 7)

            def describe_tiles(e):
                sl = slot[:, e, :]
                TT(tile_ge[:, :, :], sl.unsqueeze(2).to_broadcast([P, NT, CT + 1]),
                   tile_thr[:, :].unsqueeze(1).to_broadcast([P, NT, CT + 1]), ALU.is_ge).then_inc(ge_d, 1)
                dve.wait_ge(ge_d, e + 1)
                RED(tile_no[:, :], tile_ge[:, :, 1:], AX, ALU.add).then_inc(tn_d, 1)
                TT(in_tile[:, :, :], tile_ge[:, :, 0:CT], tile_ge[:, :, 1:], ALU.subtract).then_inc(in_d, 1)
                dve.wait_ge(tn_d, e + 1)
                V.scalar_tensor_tensor(row_in[:, :], tile_no[:, :], -float(P), sl, ALU.mult, ALU.add).then_inc(ri_d, 1)

            def describe_facts(e, part):
                sl = slice(part * NT // 2, (part + 1) * NT // 2)
                if part == 0:
                    wait(dve, look_d, e)
                    dve.wait_ge(in_d, e + 1)
                TT(facts[:, sl, :, :], vals[:, e, sl, :].unsqueeze(3).to_broadcast([P, NT // 2, NV, CT]),
                   in_tile[:, sl, :].unsqueeze(2).to_broadcast([P, NT // 2, NV, CT]), ALU.mult)

            def describe_rows(e, part):
                if part == 0:
                    dve.wait_ge(ri_d, e + 1)
                sl = slice(part * P // 4, (part + 1) * P // 4)
                TT(onehot[:, sl, :], iota_b[:, sl, :], row_in[:, :].unsqueeze(1).to_broadcast([P, P // 4, NT]),
                   ALU.is_equal).then_inc(facts_d, 1)

            def describe(e):
                describe_tiles(e)
                for part in range(2):
                    describe_facts(e, part)
                for part in range(4):
                    describe_rows(e, part)

            def chained(sem, base):
                n = [0]

                def lk(ins):
                    n[0] += 1
                    ins.then_inc(sem, 1)
                    dve.wait_ge(sem, base + n[0])
                return lk

            def find_tokens(e, par):
                lk = chained(fin_l, e * 3)
                dve.wait_ge(look_d, e + 1)
                V.tensor_copy(got[:, :, :], bank[7][:, 0:NV * CT].rearrange("p (v a) -> p v a", v=NV))\
                    .then_inc(got_d, 1)
                dve.wait_ge(got_d, e + 1)
                lk(V.scalar_tensor_tensor(tok[:, :], got[:, 1, :], float(P), got[:, 0, :], ALU.mult, ALU.add))
                V.tensor_scalar(far[:, :], got[:, 1, :], 0.5, float(FAR), ALU.is_lt, ALU.mult)
                lk(V.tensor_scalar(tok[:, :], tok[:, :], -float(P), 0.0, ALU.add, ALU.max))
                if not isinstance(e, int) or e > 1:
                    wait(dve, sc_d, (e - 1) * CT * 16 + 16)
                lk(V.tensor_copy(g_idx[par][:, :], tok[:, :]))
                V.tensor_tensor(s_idx[par][:, :], tok[:, :], far[:, :], ALU.add).then_inc(idx_d, 1)

            def find_weights(e, par):
                lk = chained(wb_l, e * 3)
                lk(TT(w_slot[:, 0, :], got[:, 2, :], got[:, 3, :], ALU.add))
                V.tensor_scalar(w_slot[:, 2, :], got[:, 1, :], float(TB) + 0.5, None, ALU.is_ge)
                lk(TT(w_slot[:, 1, :], w_slot[:, 0, :], got[:, 4, :], ALU.add))
                lk(TT(w_b[par][:, 1, :], w_slot[:, 2, :], w_slot[:, 1, :], ALU.mult))
                TT(w_b[par][:, 0, :], w_slot[:, 1, :], w_b[par][:, 1, :], ALU.subtract).then_inc(wb_d, 1)

            dve.sem_inc(ym_d, 1)
            describe(0)
            find_tokens(0, 0)
            place_masks(1)
            describe(1)

            def x_low(e, par, g, bk=7):
                n = min(2, CT - 2 * g) * P
                wait(dve, xh_d, e * XG + g + 1)
                sl = slice(2 * g * P, 2 * g * P + n)
                V.tensor_tensor(xT_l[par][:, :, sl], bank[bk][:, 0:2 * n].rearrange("p (c n) -> p c n", c=KC),
                                xT_h[par][:, :, sl].bitcast(F32), ALU.subtract).then_inc(xl_d, 1)

            for g in range(XG):
                x_low(0, 0, g, bk=g)
            find_weights(0, 0)
            place_counts(1)
            place_slots(1)

            def weigh(e, lo=0, hi=CT):
                wait(dve, sc_d, e * CT * 16 + 16)
                for a in range(lo, hi):
                    if a == CT - 1:
                        wait(dve, dn_d, (e + 1) * FC)
                    elif a % 2 == 0:
                        wait(dve, y_tile, e * (CT // 2) + a // 2 + 1)
                    V.tensor_tensor(yo[:, a, :], bank[4 + a // 2][:, a % 2 * D:(a % 2 + 1) * D], gw[:, a, :], ALU.mult)\
                        .then_inc(ym_d, 1)

            def combine(e, lo, hi):
                wait(dve, xo_d, (e + 1) * CT * 16)
                for a in range(lo, hi):
                    wait(dve, ym_d, e * CT + a + 2)
                    V.tensor_tensor(yo[:, a, :], yo[:, a, :], xo[:, a, :], ALU.add).then_inc(yo_d, 1)

            def expert(e, par, first=False, last=False, ahead=True):
                if not first:
                    weigh(e - 1)
                for f in range(FC):
                    for h in range(2):
                        i = e * 2 * FC + 2 * f + h
                        wait(dve, silu_d, i + 1)
                        if f:
                            wait(dve, hh_d, i - 1)
                        V.tensor_tensor(hid[h][:, :], act_g[h][:, :], bank[2 * h + 1][:, 0:HCAP], ALU.mult)\
                            .then_inc(hid_d, 1)
                        wait(dve, hh_d, i + 1)
                        V.tensor_tensor(hid_l[f % 2][:, h * HCAP:(h + 1) * HCAP], hid[h][:, :],
                                        hid_h[f % 2][:, h * HCAP:(h + 1) * HCAP].bitcast(F32), ALU.subtract)\
                            .then_inc(hl_d, 1)
                        if f == 0 and not first:
                            combine(e - 1, h * 2, (2, CT)[h])
                    if not last and XF <= f < XF + XG:
                        x_low(e + 1, 1 - par, f - XF)
                    if f < CT:
                        wait(dve, gw0_d, e * CT + f + 1)
                        V.scalar_tensor_tensor(gw[:, f, :], mod_all[:, 1, 3, :], w_b[par][:, 1, f:f + 1], gw0[:, :],
                                               ALU.mult, ALU.add).then_inc(gw_d, 1)
                    if f == 1 and not last:
                        find_tokens(e + 1, 1 - par)
                    if f == FC - 1 and not last:
                        find_weights(e + 1, 1 - par)
                    if ahead:
                        if f == 2:
                            describe_tiles(e + 2)
                        if f in (3, 4):
                            describe_facts(e + 2, f - 3)
                        for part in {3: (0,), 5: (1,), 6: (2, 3)}.get(f, ()):
                            describe_rows(e + 2, part)

            expert(0, 0, first=True)
            with dve.Fori(0, (E - 4) // 2) as k:
                expert(k * 2 + 1, 1)
                expert(k * 2 + 2, 0)
            for e in range(E - 3, E):
                expert(e, e % 2, last=e == E - 1, ahead=e + 2 < E)
            for a in range(CT):
                weigh(E - 1, a, a + 1)
                combine(E - 1, a, a + 1)

        @block.tensor
        def _(pe):
            MM = nc.tensor.matmul
            TR = nc.tensor.transpose
            PASSES = ((0, 0), (0, 1), (1, 0))
            pe.wait_ge(act_pre, 1)
            for k in range(KC):
                last = TR(bank[0][:, k * B:(k + 1) * B], c_act[:, k * P:(k + 1) * P], ident[0:B, 0:B])
            last.then_inc(pe_pre, 1)
            pe.wait_ge(dve_pre, 1)
            pe.wait_ge(ld_mod, 16)
            for i in range(2):
                for m in range(KC):
                    for k in range(KC):
                        at = i * D + m * P
                        last = MM(bank[1][:, (i * KC + m) * B:(i * KC + m + 1) * B], wmod_sb[:, k, at:at + P],
                                  cT[:, k, :], start=k == 0, stop=k == KC - 1)
            last.then_inc(pe_pre, 1)

            def product(out, x, w, cols):
                n = 0
                for k in range(KC):
                    for j, i in ((0, 0), (0, 1), (1, 0)):
                        ins = MM(out, x[j][:, k, :], w[i][:, k, cols], start=n == 0, stop=n == 3 * KC - 1)
                        n += 1
                return ins

            def mod_rows(i):
                pe.wait_ge(ld_rest, 64)
                for k in range(KC):
                    at = 2 * D + i * 2 * D
                    last = MM(row_ps[i], cT[:, k, :], wmod_sb[:, k, at:at + 2 * D], start=k == 0, stop=k == KC - 1)
                if i == 1:
                    for k in range(KC):
                        last = TR(bank[6][:, k * E:(k + 1) * E], router_sb[:, k * P:(k + 1) * P], ident[0:E, 0:E])
                    last.then_inc(pe_pre, 1)

            def step(s):
                on = stages(s)
                if on["trh"]:
                    wait(pe, norm1, s.t(2))
                    wait(pe, hT_d, s.t(1))
                    for k in range(KC):
                        last = TR(hT_ps[:, k, :], hn[:, k * P:(k + 1) * P], ident[:, :])
                    last.then_inc(tr_h, 1)
                if on["qkv"]:
                    if s.rep == 0:
                        pe.wait_ge(dve_pre, 5)
                    wait(pe, hTl_d, s.t(1))
                    wait(pe, rope_m, s.t(0))
                    product(qk_ps, (hT_h[s.par(0)], hT_l[s.par(0)]), (wqkv_h, wqkv_l), slice(0, 2 * D))\
                        .then_inc(qk_done, 1)
                    wait(pe, v_done, s.t(0))
                    product(v_ps, (hT_h[s.par(0)], hT_l[s.par(0)]), (wqkv_h, wqkv_l), slice(2 * D, 3 * D))\
                        .then_inc(qkv_done, 1)
                if on["kv"]:
                    wait(pe, feat_d, s.t(-1))
                    wait(pe, qT_d, s.t(-2))
                    for k in range(KC):
                        last = TR(qT_ps[:, k * P:(k + 1) * P], feat[:, k * P:(k + 1) * P], ident[:, :])
                    last.then_inc(tr_q, 1)
                    wait(pe, v_done, s.t(-1))
                    if (s.rep - 2) % TB == 0:
                        if s.rep == 2:
                            pe.wait_ge(plink_s, 4)
                        else:
                            pe.wait_ge(kvb_d, 1)
                        MM(bank[3][:, :], zeros[0:1, 0:P], zeros[0:1, :], start=True, stop=False, skip_group_check=True)
                    for k in range(KC):
                        last = MM(kv_ps[:, k, :], feat[:, D + k * P:D + (k + 1) * P], vx[s.par(-2)][:, k, :],
                                  start=False, stop=False, skip_group_check=True)
                    last.then_inc(kv_d, 1)
                if s.rep in (2, 3):
                    mod_rows(s.rep - 2)
                if on["proj"]:
                    o = -LAG - 1
                    wait(pe, att_d, s.t(o + 1))
                    if alone(s):
                        wait(pe, oT_d, s.t(o))
                    else:
                        wait(pe, x2_d, s.t(o))
                    for k in range(KC):
                        last = TR(oT_ps[alone(s)][:, k * P:(k + 1) * P], att[:, k * P:(k + 1) * P], ident[:, :])
                    last.then_inc(tr_o, 1)
                if on["att"]:
                    o = -LAG
                    b = (s.rep + o) // TB
                    if s.rep == LAG:
                        pe.wait_ge(dve_pre, 6)
                    if s.rep in (LAG, NT + 2):
                        pe.wait_ge(kvb_d, b + 1)
                    wait(pe, ld_q[s.par(o)], (s.half(o) + 1) * 16)
                    wait(pe, att_d, s.t(o))
                    for k in range(KC):
                        last = MM(o_ps[:, k, :], q_in[s.par(o)][:, k * P:(k + 1) * P], kvb[b][:, k, :],
                                  start=True, stop=True)
                    last.then_inc(o_d, 1)
                if on["logit"]:
                    o = -LAG - 5
                    wait(pe, h2T_d, s.t(o + 1))
                    if alone(s):
                        wait(pe, lgc, s.t(o))
                    for k in range(KC):
                        last = MM(lg_ps[alone(s)], h2T[:, k * P:(k + 1) * P], routerT[:, k, :],
                                  start=k == 0, stop=k == KC - 1)
                    last.then_inc(lg_d, 1)
                if on["proj"]:
                    o = -LAG - 1
                    b = (s.rep + o) // TB
                    wait(pe, oT_d, s.t(o + 1))
                    if (s.rep + o) % TB == 0:
                        pe.wait_ge(dve_pre, 7 + b)
                    if alone(s):
                        wait(pe, x2_d, s.t(o))
                    for k in range(KC):
                        last = MM(y_ps, attT[:, k * P:(k + 1) * P], wout_g[b][:, k, :], start=k == 0, stop=k == KC - 1)
                    last.then_inc(y_d, 1)
                if on["trh2"]:
                    o = -LAG - 4
                    if s.rep + o == 0:
                        pe.wait_ge(dve_pre, 6)
                    wait(pe, h2_d, s.t(o + 1))
                    wait(pe, h2T_d, s.t(o))
                    if on["logit"] and s.rep <= NT + 6:
                        wait(pe, lgc, s.t(o if not alone(s) else o - 1))
                    for k in range(KC):
                        last = TR(h2T_ps[:, k * P:(k + 1) * P], h2[s.par(o)][:, k * P:(k + 1) * P], ident[:, :])
                    last.then_inc(tr_h2, 1)

            steps(pe, step, ATT)

            pe.wait_ge(r_dve, 4)
            flat = val[:, :, :].rearrange("p n e -> p (n e)")
            for k in range(2):
                last = TR(bank[0][:, k * P:(k + 1) * P], flat[:, k * P:(k + 1) * P], ident[:, :])
            last.then_inc(r_pe, 1)
            with pe.Fori(0, DIGITS // SEARCH) as i:
                for j in range(SEARCH):
                    pe.wait_ge(cnt_d, i * SEARCH + j + 1)
                    MM(bank[1][:, 0:3], same_e[:, :], cnt[:, :], start=True, stop=True).then_inc(tot_d, 1)
            pe.wait_ge(r_dve, 5)
            MM(bank[2][:, 0:E], ones_f[:, :], thr_sel[:, :], start=True, stop=True).then_inc(r_pe, 1)
            pe.wait_ge(r_dve, 6)

            def count_masks(part):
                lo, hi = PLACES[part]
                for k in range(2):
                    cols = slice(k * (hi - lo) * NT, (k + 1) * (hi - lo) * NT)
                    masks = mask2[:, k, lo:hi, :].rearrange("p e n -> p (e n)")
                    MM(bank[3 + 2 * part][:, cols], before[:, :], masks, start=True, stop=True)
                    last = MM(bank[4 + 2 * part][:, cols], ones_b[:, :], masks, start=True, stop=True)
                last.then_inc(r_pe, 1)

            count_masks(0)

            def look(e):
                wait(pe, facts_d, e * 4 + 4)
                for n in range(NT):
                    last = MM(bank[7][:, 0:NV * CT], onehot[:, :, n], facts[:, n, :, :].rearrange("p v a -> p (v a)"),
                              start=n == 0, stop=n == NT - 1)
                last.then_inc(look_d, 1)

            def transpose_x(e, g, first=False):
                tiles = range(2 * g, min(2 * g + 2, CT))
                wait(pe, ga_d[g], (e + 1) * len(tiles) * 16)
                if not first:
                    wait(pe, xl_d, e * XG + g)
                    wait(pe, got_d, e + 1)
                for k in range(KC):
                    for j, a in enumerate(tiles):
                        at = (k * len(tiles) + j) * P
                        last = TR(bank[g if first else 7][:, at:at + P], xg[:, a, k * P:(k + 1) * P], ident[:, :])
                last.then_inc(trx_d, 1)

            look(0)
            pe.wait_ge(r_dve, 7)
            count_masks(1)
            for g in range(XG - 1):
                transpose_x(0, g, first=True)
            wait(pe, got_d, 1)
            look(1)
            transpose_x(0, XG - 1, first=True)

            def expert(e, par, last_e):
                W, XT = (w_h, w_l), (xT_h[par], xT_l[par])

                def gate_up(f):
                    wait(pe, sp_l, e * FC + f + 1)
                    if f == 0:
                        wait(pe, xl_d, e * XG + XG)
                    for h in range(2):
                        if f:
                            wait(pe, hid_d, e * 2 * FC + 2 * f + h - 1)
                        cols = slice(h * HCAP, (h + 1) * HCAP)
                        for m in range(2):
                            n = 0
                            for k in range(KC):
                                for i, j in PASSES:
                                    at = (2 * m + k) * P
                                    last = MM(bank[2 * h + m][:, 0:HCAP], W[i][:, f, at:at + P], XT[j][:, k, cols],
                                              start=n == 0, stop=n == 3 * KC - 1)
                                    n += 1
                        last.then_inc(gu_d, 1)

                def down(f):
                    wait(pe, hh_d, e * 2 * FC + 2 * f + 2)
                    wait(pe, hl_d, e * 2 * FC + 2 * f + 2)
                    if f == 0:
                        wait(pe, ym_d, e * CT + 1)
                    for a in range(CT):
                        for n, (i, j) in enumerate(PASSES):
                            last = MM(bank[4 + a // 2][:, a % 2 * D:(a % 2 + 1) * D],
                                      (hid_h, hid_l)[j][f % 2][:, a * P:(a + 1) * P], W[i][:, f, 4 * P:],
                                      start=f == 0 and n == 0 and a % 2 == 0, stop=f == FC - 1 and n == 2,
                                      skip_group_check=True)
                        if f == FC - 1 and a % 2 == 1:
                            last.then_inc(y_tile, 1)
                    last.then_inc(dn_d, 1)

                gate_up(0)
                for f in range(1, FC):
                    gate_up(f)
                    if last_e < 1 and XF <= f < XF + XG:
                        transpose_x(e + 1, f - XF)
                    down(f - 1)
                if last_e == 0:
                    wait(pe, xl_d, e * XG + 2 * XG)
                    look(e + 2)
                down(FC - 1)

            with pe.Fori(0, (E - 2) // 2) as k:
                expert(k * 2, 0, 0)
                expert(k * 2 + 1, 1, 0)
            expert(E - 2, 0, 0.5)
            expert(E - 1, 1, 1)


def kernel(L0_attn_x, L0_attn_W_qkv, L0_attn_W_out, L0_ffn_router_w, L0_ffn_wg, L0_ffn_wu, L0_ffn_wd, L0_c, L0_wmod):
    import numpy as np
    from concourse import bacc
    from concourse.bass_utils import run_bass_kernel_spmd

    nc = bacc.Bacc("TRN2", target_bir_lowering=False, num_devices=1)
    inv = (1.0 / np.float32(500000.0) ** (np.arange(0, HD, 2, dtype=np.float32) / np.float32(HD))).astype(np.float32)
    ang = np.arange(T, dtype=np.float32)[:, None] * inv[None, :]
    rope = np.concatenate([np.cos(ang), np.sin(ang), -np.sin(ang)], axis=1).astype(np.float32)
    row = np.arange(P)
    consts = np.concatenate([
        row[:, None] == row[None, :],
        row[:, None] // HD == row[None, :] // HD,
        row[:, None] // HD == np.arange(HC)[None, :],
        row[:, None] == np.arange(E)[None, :],
        row[:, None] % E == row[None, :] % E,
    ], axis=1).astype(np.float32)
    arrays = {
        "x": L0_attn_x, "w_qkv": L0_attn_W_qkv, "w_out": L0_attn_W_out, "router": L0_ffn_router_w, "wg": L0_ffn_wg,
        "wu": L0_ffn_wu, "wd": L0_ffn_wd, "c": L0_c, "wmod": L0_wmod, "rope": rope, "consts": consts,
    }
    arrays = {n: np.ascontiguousarray(a) for n, a in arrays.items()}
    aps = {n: nc.dram_tensor(n, a.shape, mybir.dt.from_np(a.dtype), kind="ExternalInput").ap()
           for n, a in arrays.items()}
    out = nc.dram_tensor("out", (B, T, D), F32, kind="ExternalOutput").ap()
    build_program(nc, out=out, **aps)
    result = run_bass_kernel_spmd(nc, [arrays], core_ids=[0])
    return result.results[0]["out"]
```
